# Optimizing a Trainium2 kernel written in Bass

```python
import numpy as np
import jax
import jax.numpy as jnp

def _softmax(x, axis=-1):
    return jax.nn.softmax(x, axis=axis)

def _gelu(x):
    return jax.nn.gelu(x, approximate=True)

def _silu(x):
    return jax.nn.silu(x)

def _sigmoid(x):
    return jax.nn.sigmoid(x)

def _layernorm(x, axis=-1, eps=1e-05):
    m = jnp.mean(x, axis=axis, keepdims=True)
    v = jnp.var(x, axis=axis, keepdims=True)
    return (x - m) / jnp.sqrt(v + eps)

def _scatter_add(tgt, idx, src, axis=0):
    return tgt.at[idx].add(src)

def _segment_sum(src, seg, n):
    return jax.ops.segment_sum(src, seg, n)
kernel_name = 'mk_decoder_postln_d4_seqx_r8_7c8a6e'

def setup_inputs(seed: int=0):
    np.random.seed(seed)
    _w = jnp.asarray

    def _rec_inputs():
        import jax
        import jax.numpy as jnp
        _rk = jax.random.key(seed)
        x = -0.0003929 + 0.9999 * jax.random.normal(jax.random.fold_in(_rk, 1), (32, 128, 128), jnp.float32)
        _lenS = 128 - jax.random.randint(jax.random.fold_in(_rk, 7), (32,), 0, max(1, 128 // 4) + 1, jnp.int32)
        _lenS2 = 77 - jax.random.randint(jax.random.fold_in(_rk, 8), (32,), 0, max(1, 77 // 4) + 1, jnp.int32)
        _ctx_512P = jax.random.normal(jax.random.fold_in(_rk, 11), (32, 16, 64), jnp.float32)
        _ctx_512c = jax.random.dirichlet(jax.random.fold_in(_rk, 511), 0.3 * jnp.ones((16,), jnp.float32), (32, 77))
        _ctx_512t = jnp.einsum('bsk,bkd->bsd', _ctx_512c, _ctx_512P)
        _ctx_512t = _ctx_512t * jax.lax.rsqrt(jnp.mean(jnp.square(_ctx_512t)) + 1e-12) * 0.953939
        ctx_512 = 4.13588e-05 + 0.999923 * (_ctx_512t + 0.3 * jax.random.normal(jax.random.fold_in(_rk, 611), (32, 77, 64), jnp.float32))
        return (x, ctx_512)
    x, ctx_512 = _rec_inputs()

    def _L0_attn_setup():
        import jax, jax.numpy as jnp
        import numpy as np
        NUM_HEADS = 16
        THETA = 10000.0

        def _rotate_half(x):
            x = x.reshape(x.shape[:-1] + (-1, 2))
            x1, x2 = (x[..., 0], x[..., 1])
            return jnp.stack((-x2, x1), axis=-1).reshape(x.shape[:-2] + (-1,))

        def _rope(x):
            d_k = x.shape[-1]
            seq_len = x.shape[-2]
            inv_freq = 1.0 / THETA ** (jnp.arange(0, d_k, 2, dtype=jnp.float32) / d_k)
            pos = jnp.arange(seq_len, dtype=jnp.float32)
            theta = pos[:, None] * inv_freq[None, :]
            cos = jnp.repeat(jnp.cos(theta), 2, axis=-1)
            sin = jnp.repeat(jnp.sin(theta), 2, axis=-1)
            return x * cos + _rotate_half(x) * sin
        key = jax.random.key(seed)
        kx, kq, kk, kv, ko = jax.random.split(key, 5)
        B, S, D = (2, 256, 128)
        std = 1.0 / (2.0 * (2 * D) ** 0.5)
        return {'x': jax.random.normal(kx, (B, S, D), dtype=jnp.float32), 'Wq': jax.random.normal(kq, (D, D), dtype=jnp.float32) * std, 'Wk': jax.random.normal(kk, (D, D), dtype=jnp.float32) * std, 'Wv': jax.random.normal(kv, (D, D), dtype=jnp.float32) * std, 'Wo': jax.random.normal(ko, (D, D), dtype=jnp.float32) * std}
    _L0_attn_all = _L0_attn_setup()
    _L0_attn_in = {k: v for k, v in _L0_attn_all.items() if k in ('Wq', 'Wk', 'Wv', 'Wo')}
    del _L0_attn_all

    def _L0_xattn_setup():
        import jax, jax.numpy as jnp
        import numpy as np
        B, LQ, LK = (8, 256, 256)
        QD, KD, VD = (128, 64, 64)
        key = jax.random.key(seed)
        ks = jax.random.split(key, 9)
        s = 0.02
        return {'query': jax.random.normal(ks[0], (B, LQ, QD), jnp.float32), 'key': jax.random.normal(ks[1], (B, LK, KD), jnp.float32), 'value': jax.random.normal(ks[2], (B, LK, VD), jnp.float32), 'Wq': jax.random.normal(ks[3], (QD, QD), jnp.float32) * s, 'bq': jnp.zeros((QD,), jnp.float32), 'Wk': jax.random.normal(ks[4], (KD, QD), jnp.float32) * s, 'bk': jnp.zeros((QD,), jnp.float32), 'Wv': jax.random.normal(ks[5], (VD, QD), jnp.float32) * s, 'bv': jnp.zeros((QD,), jnp.float32)}
    _L0_xattn_all = _L0_xattn_setup()
    _L0_xattn_in = {k: v for k, v in _L0_xattn_all.items() if k in ('Wq', 'bq', 'Wk', 'bk', 'Wv', 'bv')}
    del _L0_xattn_all

    def _L0_ffn_setup():
        import jax, jax.numpy as jnp
        import numpy as np
        import math
        N_EMBD = 128
        HIDDEN = 4 * N_EMBD
        N_EXPERTS = 8
        TOP_K = 2
        B, T = (4, 256)

        def new_gelu(x):
            c = math.sqrt(2.0 / math.pi)
            return 0.5 * x * (1.0 + jnp.tanh(c * (x + 0.044715 * x * x * x)))

        def _moe_forward(x, Wfc_s, bfc_s, Wproj_s, bproj_s, Wr, Wfc, bfc, Wproj, bproj):
            Bb, Tt, C = x.shape
            xf = x.reshape(Bb * Tt, C)
            N = Bb * Tt
            shared = new_gelu(xf @ Wfc_s + bfc_s) @ Wproj_s + bproj_s
            logits = xf @ Wr
            probs = jax.nn.softmax(logits, axis=-1)
            topk_p, topk_i = jax.lax.top_k(probs, TOP_K)
            topk_p = topk_p / jnp.sum(topk_p, axis=-1, keepdims=True)
            gate = jnp.zeros((N, N_EXPERTS), dtype=xf.dtype)
            gate = gate.at[jnp.arange(N)[:, None], topk_i].add(topk_p)
            routed = jnp.zeros_like(xf)
            for e in range(N_EXPERTS):
                h = new_gelu(xf @ Wfc[e] + bfc[e]) @ Wproj[e] + bproj[e]
                routed = routed + h * gate[:, e:e + 1]
            return (shared + routed).reshape(Bb, Tt, C)
        key = jax.random.key(seed)
        ks = jax.random.split(key, 10)
        s = 0.02
        return {'x': jax.random.normal(ks[0], (B, T, N_EMBD), dtype=jnp.float32), 'Wfc_s': jax.random.normal(ks[1], (N_EMBD, HIDDEN), dtype=jnp.float32) * s, 'bfc_s': jnp.zeros((HIDDEN,), dtype=jnp.float32), 'Wproj_s': jax.random.normal(ks[2], (HIDDEN, N_EMBD), dtype=jnp.float32) * s, 'bproj_s': jnp.zeros((N_EMBD,), dtype=jnp.float32), 'Wr': jax.random.normal(ks[3], (N_EMBD, N_EXPERTS), dtype=jnp.float32) * s, 'Wfc': jax.random.normal(ks[4], (N_EXPERTS, N_EMBD, HIDDEN), dtype=jnp.float32) * s, 'bfc': jnp.zeros((N_EXPERTS, HIDDEN), dtype=jnp.float32), 'Wproj': jax.random.normal(ks[5], (N_EXPERTS, HIDDEN, N_EMBD), dtype=jnp.float32) * s, 'bproj': jnp.zeros((N_EXPERTS, N_EMBD), dtype=jnp.float32)}
    _L0_ffn_all = _L0_ffn_setup()
    _L0_ffn_in = {k: v for k, v in _L0_ffn_all.items() if k in ('Wfc_s', 'bfc_s', 'Wproj_s', 'bproj_s', 'Wr', 'Wfc', 'bfc', 'Wproj', 'bproj')}
    del _L0_ffn_all

    def _L1_attn_setup():
        import jax, jax.numpy as jnp
        import numpy as np
        B, T, DIM = (2, 512, 128)
        DEPTH, HEADS = (4, 8)
        DH = DIM // HEADS
        NLOCAL, WINDOW, BUCKET = (4, 128, 64)
        MULT = 4

        def layer_norm(x, g, b, eps=1e-05):
            m = jnp.mean(x, -1, keepdims=True)
            v = jnp.mean(jnp.square(x - m), -1, keepdims=True)
            return (x - m) * jax.lax.rsqrt(v + eps) * g + b

        def causal_linear_attn(q, k, v):
            b, h, n, e = q.shape
            u = n // BUCKET
            q = jax.nn.softmax(q, axis=-1)
            k = jax.nn.elu(k) + 1.0
            bq = q.reshape(b, h, u, BUCKET, e)
            bk = k.reshape(b, h, u, BUCKET, e)
            bv = v.reshape(b, h, u, BUCKET, e)
            k_cum = jnp.cumsum(bk.sum(axis=-2), axis=-2)
            ctx = jnp.einsum('bhund,bhune->bhude', bk, bv)
            ctx = jnp.cumsum(ctx, axis=2)
            ctx = ctx / (k_cum[..., None] + 1e-06)
            ctx = jnp.pad(ctx, ((0, 0), (0, 0), (1, 0), (0, 0), (0, 0)))[:, :, :-1]
            out = jnp.einsum('bhund,bhude->bhune', bq, ctx)
            return out.reshape(b, h, n, e)

        def local_attn(q, k, v):
            b, lh, t, e = q.shape
            bh = b * lh
            nb = t // WINDOW
            bq = q.reshape(bh, nb, WINDOW, e)
            bk = k.reshape(bh, nb, WINDOW, e)
            bv = v.reshape(bh, nb, WINDOW, e)

            def look_around(x):
                padded = jnp.pad(x, ((0, 0), (1, 0), (0, 0), (0, 0)))
                return jnp.concatenate([padded[:, :-1], padded[:, 1:]], axis=2)
            bk2 = look_around(bk)
            bv2 = look_around(bv)
            tix = jnp.arange(t).reshape(1, nb, WINDOW)
            tpad = jnp.pad(tix, ((0, 0), (1, 0), (0, 0)), constant_values=-1)
            kix = jnp.concatenate([tpad[:, :-1], tpad[:, 1:]], axis=2)
            dots = jnp.einsum('bwie,bwje->bwij', bq, bk2) * e ** (-0.5)
            mask_value = -jnp.finfo(dots.dtype).max
            causal_mask = tix[:, :, :, None] < kix[:, :, None, :]
            pad_mask = (kix == -1)[:, :, None, :]
            dots = jnp.where(causal_mask | pad_mask, mask_value, dots)
            attn = jax.nn.softmax(dots, axis=-1)
            out = jnp.einsum('bwij,bwje->bwie', attn, bv2)
            return out.reshape(b, lh, t, e)

        def self_attention(x, Wq, Wk, Wv, Wo, bo):
            b, t, _ = x.shape
            mh = lambda z: z.reshape(b, t, HEADS, DH).transpose(0, 2, 1, 3)
            q, k, v = (mh(x @ Wq), mh(x @ Wk), mh(x @ Wv))
            lo = local_attn(q[:, :NLOCAL], k[:, :NLOCAL], v[:, :NLOCAL])
            go = causal_linear_attn(q[:, NLOCAL:], k[:, NLOCAL:], v[:, NLOCAL:])
            out = jnp.concatenate([lo, go], axis=1)
            out = out.transpose(0, 2, 1, 3).reshape(b, t, DIM)
            return out @ Wo + bo
        key = jax.random.key(seed)
        ks = jax.random.split(key, 8)
        s = 0.02
        rn = lambda k, shape: jax.random.normal(k, shape, dtype=jnp.float32) * s
        return {'x': jax.random.normal(ks[0], (B, T, DIM), dtype=jnp.float32), 'Wq': rn(ks[1], (DEPTH, DIM, DIM)), 'Wk': rn(ks[2], (DEPTH, DIM, DIM)), 'Wv': rn(ks[3], (DEPTH, DIM, DIM)), 'Wo': rn(ks[4], (DEPTH, DIM, DIM)), 'bo': jnp.zeros((DEPTH, DIM), jnp.float32), 'ln1_g': jnp.ones((DEPTH, DIM), jnp.float32), 'ln1_b': jnp.zeros((DEPTH, DIM), jnp.float32), 'W1': rn(ks[5], (DEPTH, DIM, DIM * MULT)), 'b1': jnp.zeros((DEPTH, DIM * MULT), jnp.float32), 'W2': rn(ks[6], (DEPTH, DIM * MULT, DIM)), 'b2': jnp.zeros((DEPTH, DIM), jnp.float32), 'ln2_g': jnp.ones((DEPTH, DIM), jnp.float32), 'ln2_b': jnp.zeros((DEPTH, DIM), jnp.float32)}
    _L1_attn_all = _L1_attn_setup()
    _L1_attn_in = {k: v for k, v in _L1_attn_all.items() if k in ('Wq', 'Wk', 'Wv', 'Wo', 'bo', 'ln1_g', 'ln1_b', 'W1', 'b1', 'W2', 'b2', 'ln2_g', 'ln2_b')}
    del _L1_attn_all

    def _L1_xattn_setup():
        import jax, jax.numpy as jnp
        import numpy as np
        DIM = 128
        LATENT_DIM = 64
        NUM_HEADS = 16
        HEAD_DIM = DIM // NUM_HEADS
        SCALE = HEAD_DIM ** (-0.5)
        key = jax.random.key(seed)
        k1, k2, k3, k4, k5 = jax.random.split(key, 5)
        B, xN, zN = (2, 256, 256)
        x = jax.random.normal(k1, (B, xN, DIM), dtype=jnp.float32)
        z = jax.random.normal(k2, (B, zN, LATENT_DIM), dtype=jnp.float32)
        Wq = jax.random.normal(k3, (DIM, DIM), dtype=jnp.float32) * DIM ** (-0.5)
        Wkv = jax.random.normal(k4, (2 * DIM, LATENT_DIM), dtype=jnp.float32) * LATENT_DIM ** (-0.5)
        Wo = jax.random.normal(k5, (DIM, DIM), dtype=jnp.float32) * DIM ** (-0.5)
        return {'x': x, 'z': z, 'Wq': Wq, 'Wkv': Wkv, 'Wo': Wo}
    _L1_xattn_all = _L1_xattn_setup()
    _L1_xattn_in = {k: v for k, v in _L1_xattn_all.items() if k in ('Wq', 'Wkv', 'Wo')}
    del _L1_xattn_all

    def _L1_ffn_setup():
        import jax, jax.numpy as jnp
        import numpy as np
        E, TOP_K, D, H = (8, 2, 128, 256)
        B, S = (2, 256)
        key = jax.random.key(seed)
        ks = jax.random.split(key, 10)
        s = 0.02
        return {'x': jax.random.normal(ks[0], (B, S, D), dtype=jnp.float32), 'gate_w': jax.random.normal(ks[1], (E, D), dtype=jnp.float32) * s, 'gate_b': jnp.zeros((E,), dtype=jnp.float32), 'w0': jax.random.normal(ks[2], (E, H, D), dtype=jnp.float32) * s, 'b0': jnp.zeros((E, H), dtype=jnp.float32), 'w1': jax.random.normal(ks[3], (E, H, D), dtype=jnp.float32) * s, 'b1': jnp.zeros((E, H), dtype=jnp.float32), 'w2': jax.random.normal(ks[4], (E, D, H), dtype=jnp.float32) * s, 'b2': jnp.zeros((E, D), dtype=jnp.float32)}
    _L1_ffn_all = _L1_ffn_setup()
    _L1_ffn_in = {k: v for k, v in _L1_ffn_all.items() if k in ('gate_w', 'gate_b', 'w0', 'b0', 'w1', 'b1', 'w2', 'b2')}
    del _L1_ffn_all

    def _L2_attn_setup():
        import jax, jax.numpy as jnp
        import numpy as np
        N_EMBD = 128
        N_HEAD = 16
        HEAD_DIM = N_EMBD // N_HEAD
        key = jax.random.key(seed)
        ks = jax.random.split(key, 9)
        B, T, C = (4, 256, N_EMBD)
        s = 1.0 / np.sqrt(C)
        return {'x': jax.random.normal(ks[0], (B, T, C), dtype=jnp.float32), 'Wq': jax.random.normal(ks[1], (C, C), dtype=jnp.float32) * s, 'bq': jnp.zeros((C,), dtype=jnp.float32), 'Wk': jax.random.normal(ks[2], (C, C), dtype=jnp.float32) * s, 'bk': jnp.zeros((C,), dtype=jnp.float32), 'Wv': jax.random.normal(ks[3], (C, C), dtype=jnp.float32) * s, 'bv': jnp.zeros((C,), dtype=jnp.float32), 'Wo': jax.random.normal(ks[4], (C, C), dtype=jnp.float32) * s, 'bo': jnp.zeros((C,), dtype=jnp.float32)}
    _L2_attn_all = _L2_attn_setup()
    _L2_attn_in = {k: v for k, v in _L2_attn_all.items() if k in ('Wq', 'bq', 'Wk', 'bk', 'Wv', 'bv', 'Wo', 'bo')}
    del _L2_attn_all

    def _L2_xattn_setup():
        import jax, jax.numpy as jnp
        import numpy as np
        H, D, C1, C2, S, M, B, W = (16, 32, 128, 64, 256, 64, 2, 4)

        def _ln(x, g, b):
            m = jnp.mean(x, -1, keepdims=True)
            v = jnp.var(x, -1, keepdims=True)
            return (x - m) * jax.lax.rsqrt(v + 1e-05) * g + b

        def _mha(x, y, wq, wk, wv, li1_w, li1_b, lnx_g, lnx_b, lny_g, lny_b, ln3_g, ln3_b, li2_w, li2_b, li3_w, li3_b, causal):
            xn = _ln(x, lnx_g, lnx_b)
            yn = _ln(y, lny_g, lny_b)
            q = jnp.einsum('bsc,hcd->bhsd', xn, wq)
            k = jnp.einsum('btc,hcd->bhtd', yn, wk)
            v = jnp.einsum('btc,hcd->bhtd', yn, wv)
            a = jax.nn.softmax(jnp.einsum('bhsd,bhtd->bhst', q, k) * D ** (-0.5), axis=-1)
            if causal:
                s, t = (a.shape[-2], a.shape[-1])
                mask = (jnp.arange(t)[None, :] > jnp.arange(s)[:, None]).astype(a.dtype)
                a = a * mask
            o = jnp.einsum('bhst,bhtd->bhsd', a, v)
            o = o.transpose(0, 2, 1, 3).reshape(x.shape[0], x.shape[1], H * D)
            x_out = x + o @ li1_w + li1_b
            h = jax.nn.gelu(_ln(x_out, ln3_g, ln3_b) @ li2_w + li2_b, approximate=False)
            return x_out + h @ li3_w + li3_b
        key = jax.random.key(seed)
        ks = iter(jax.random.split(key, 64))

        def w(shape, scale=0.02):
            return jax.random.normal(next(ks), shape, jnp.float32) * scale
        inp = {'xx': jax.random.normal(next(ks), (B, S, C1), jnp.float32), 'ee': jax.random.normal(next(ks), (B, M, C2), jnp.float32), 'ln1_g': jnp.ones(C1, jnp.float32), 'ln1_b': jnp.zeros(C1, jnp.float32), 'ln2_g': jnp.ones(C1, jnp.float32), 'ln2_b': jnp.zeros(C1, jnp.float32)}
        for pfx, cy in (('a1', C1), ('a2', C2)):
            inp[pfx + '_wq'] = w((H, C1, D))
            inp[pfx + '_wk'] = w((H, cy, D))
            inp[pfx + '_wv'] = w((H, cy, D))
            inp[pfx + '_li1_w'] = w((H * D, C1))
            inp[pfx + '_li1_b'] = jnp.zeros(C1, jnp.float32)
            inp[pfx + '_lnx_g'] = jnp.ones(C1, jnp.float32)
            inp[pfx + '_lnx_b'] = jnp.zeros(C1, jnp.float32)
            inp[pfx + '_lny_g'] = jnp.ones(cy, jnp.float32)
            inp[pfx + '_lny_b'] = jnp.zeros(cy, jnp.float32)
            inp[pfx + '_ln3_g'] = jnp.ones(C1, jnp.float32)
            inp[pfx + '_ln3_b'] = jnp.zeros(C1, jnp.float32)
            inp[pfx + '_li2_w'] = w((C1, C1 * W))
            inp[pfx + '_li2_b'] = jnp.zeros(C1 * W, jnp.float32)
            inp[pfx + '_li3_w'] = w((C1 * W, C1))
            inp[pfx + '_li3_b'] = jnp.zeros(C1, jnp.float32)
        inp['training'] = 0
        return inp
    _L2_xattn_all = _L2_xattn_setup()
    _L2_xattn_in = {k: v for k, v in _L2_xattn_all.items() if k in ('ln1_g', 'ln1_b', 'ln2_g', 'ln2_b', 'a1_wq', 'a1_wk', 'a1_wv', 'a1_li1_w', 'a1_li1_b', 'a1_lnx_g', 'a1_lnx_b', 'a1_lny_g', 'a1_lny_b', 'a1_ln3_g', 'a1_ln3_b', 'a1_li2_w', 'a1_li2_b', 'a1_li3_w', 'a1_li3_b', 'a2_wq', 'a2_wk', 'a2_wv', 'a2_li1_w', 'a2_li1_b', 'a2_lnx_g', 'a2_lnx_b', 'a2_lny_g', 'a2_lny_b', 'a2_ln3_g', 'a2_ln3_b', 'a2_li2_w', 'a2_li2_b', 'a2_li3_w', 'a2_li3_b')}
    del _L2_xattn_all

    def _L2_ffn_setup():
        import jax, jax.numpy as jnp
        import numpy as np
        EPS = 1e-05

        @jax.custom_vjp
        def ste_quantize(w):
            scale = jnp.maximum(jnp.mean(jnp.abs(w)), EPS)
            return jnp.clip(jnp.round(w / scale), -1.0, 1.0)

        def _ste_fwd(w):
            return (ste_quantize(w), None)

        def _ste_bwd(_, g):
            return (g,)
        ste_quantize.defvjp(_ste_fwd, _ste_bwd)
        key = jax.random.key(seed)
        k1, k2 = jax.random.split(key)
        x = jax.random.normal(k1, (8, 1024, 128), dtype=jnp.float32)
        weight = jax.random.normal(k2, (128, 128), dtype=jnp.float32) * 0.02
        return {'x': x, 'weight': weight}
    _L2_ffn_all = _L2_ffn_setup()
    _L2_ffn_in = {k: v for k, v in _L2_ffn_all.items() if k in ('weight',)}
    del _L2_ffn_all

    def _L3_attn_setup():
        import jax, jax.numpy as jnp
        import numpy as np
        EMBED_DIM = 128
        NUM_HEADS = 16
        HEAD_DIM = EMBED_DIM // NUM_HEADS
        SEQ_LEN = 128
        BATCH = 4
        MAX_REL_POS = 2

        def _rel_index(length_q, length_k):
            q = jnp.arange(length_q)[:, None]
            k = jnp.arange(length_k)[None, :]
            return jnp.clip(k - q, -MAX_REL_POS, MAX_REL_POS) + MAX_REL_POS
        key = jax.random.key(seed)
        ks = jax.random.split(key, 12)
        s = 1.0 / np.sqrt(EMBED_DIM)
        x = jax.random.normal(ks[0], (BATCH, SEQ_LEN, EMBED_DIM), dtype=jnp.float32)
        W_q = jax.random.normal(ks[1], (EMBED_DIM, EMBED_DIM), dtype=jnp.float32) * s
        b_q = jnp.zeros((EMBED_DIM,), dtype=jnp.float32)
        W_k = jax.random.normal(ks[2], (EMBED_DIM, EMBED_DIM), dtype=jnp.float32) * s
        b_k = jnp.zeros((EMBED_DIM,), dtype=jnp.float32)
        W_v = jax.random.normal(ks[3], (EMBED_DIM, EMBED_DIM), dtype=jnp.float32) * s
        b_v = jnp.zeros((EMBED_DIM,), dtype=jnp.float32)
        W_o = jax.random.normal(ks[4], (EMBED_DIM, EMBED_DIM), dtype=jnp.float32) * s
        b_o = jnp.zeros((EMBED_DIM,), dtype=jnp.float32)
        lim = float(np.sqrt(6.0 / (2 * MAX_REL_POS + 1 + HEAD_DIM)))
        rel_k_table = jax.random.uniform(ks[5], (2 * MAX_REL_POS + 1, HEAD_DIM), jnp.float32, -lim, lim)
        rel_v_table = jax.random.uniform(ks[6], (2 * MAX_REL_POS + 1, HEAD_DIM), jnp.float32, -lim, lim)
        return {'x': x, 'W_q': W_q, 'b_q': b_q, 'W_k': W_k, 'b_k': b_k, 'W_v': W_v, 'b_v': b_v, 'W_o': W_o, 'b_o': b_o, 'rel_k_table': rel_k_table, 'rel_v_table': rel_v_table}
    _L3_attn_all = _L3_attn_setup()
    _L3_attn_in = {k: v for k, v in _L3_attn_all.items() if k in ('W_q', 'b_q', 'W_k', 'b_k', 'W_v', 'b_v', 'W_o', 'b_o', 'rel_k_table', 'rel_v_table')}
    del _L3_attn_all

    def _L3_xattn_setup():
        import jax, jax.numpy as jnp
        import numpy as np
        B, LQ, LK = (8, 256, 256)
        QD, KD, VD = (128, 64, 64)
        key = jax.random.key(seed)
        ks = jax.random.split(key, 9)
        s = 0.02
        return {'query': jax.random.normal(ks[0], (B, LQ, QD), jnp.float32), 'key': jax.random.normal(ks[1], (B, LK, KD), jnp.float32), 'value': jax.random.normal(ks[2], (B, LK, VD), jnp.float32), 'Wq': jax.random.normal(ks[3], (QD, QD), jnp.float32) * s, 'bq': jnp.zeros((QD,), jnp.float32), 'Wk': jax.random.normal(ks[4], (KD, QD), jnp.float32) * s, 'bk': jnp.zeros((QD,), jnp.float32), 'Wv': jax.random.normal(ks[5], (VD, QD), jnp.float32) * s, 'bv': jnp.zeros((QD,), jnp.float32)}
    _L3_xattn_all = _L3_xattn_setup()
    _L3_xattn_in = {k: v for k, v in _L3_xattn_all.items() if k in ('Wq', 'bq', 'Wk', 'bk', 'Wv', 'bv')}
    del _L3_xattn_all

    def _L3_ffn_setup():
        import jax, jax.numpy as jnp
        import numpy as np
        B, S, D, H, F, E = (2, 128, 128, 16, 512, 8)
        HD = D // H
        EPS = 1e-06

        def _layernorm(x, g, b):
            m = jnp.mean(x, axis=-1, keepdims=True)
            v = jnp.var(x, axis=-1, keepdims=True)
            return (x - m) / jnp.sqrt(v + EPS) * g + b
        key = jax.random.key(seed)
        ks = jax.random.split(key, 10)
        sc = 0.02
        x = jax.random.normal(ks[0], (B, S, D), jnp.float32)
        Wq = jax.random.normal(ks[1], (D, D), jnp.float32) * sc
        Wk = jax.random.normal(ks[2], (D, D), jnp.float32) * sc
        Wv = jax.random.normal(ks[3], (D, D), jnp.float32) * sc
        Wo = jax.random.normal(ks[4], (D, D), jnp.float32) * sc
        bo = jnp.zeros((D,), jnp.float32)
        Wr = jax.random.normal(ks[5], (D, E), jnp.float32) * sc
        We1 = jax.random.normal(ks[6], (E, D, F), jnp.float32) * sc
        be1 = jnp.zeros((E, F), jnp.float32)
        We2 = jax.random.normal(ks[7], (E, F, D), jnp.float32) * sc
        be2 = jnp.zeros((E, D), jnp.float32)
        ln1_g = jnp.ones((D,), jnp.float32)
        ln1_b = jnp.zeros((D,), jnp.float32)
        ln2_g = jnp.ones((D,), jnp.float32)
        ln2_b = jnp.zeros((D,), jnp.float32)
        return {'x': x, 'Wq': Wq, 'Wk': Wk, 'Wv': Wv, 'Wo': Wo, 'bo': bo, 'Wr': Wr, 'We1': We1, 'be1': be1, 'We2': We2, 'be2': be2, 'ln1_g': ln1_g, 'ln1_b': ln1_b, 'ln2_g': ln2_g, 'ln2_b': ln2_b}
    _L3_ffn_all = _L3_ffn_setup()
    _L3_ffn_in = {k: v for k, v in _L3_ffn_all.items() if k in ('Wq', 'Wk', 'Wv', 'Wo', 'bo', 'Wr', 'We1', 'be1', 'We2', 'be2', 'ln1_g', 'ln1_b', 'ln2_g', 'ln2_b')}
    del _L3_ffn_all
    return {'x': x, 'ctx_512': ctx_512, 'L0_attn_Wq': _L0_attn_in['Wq'], 'L0_attn_Wk': _L0_attn_in['Wk'], 'L0_attn_Wv': _L0_attn_in['Wv'], 'L0_attn_Wo': _L0_attn_in['Wo'], 'L0_xattn_Wq': _L0_xattn_in['Wq'], 'L0_xattn_bq': _L0_xattn_in['bq'], 'L0_xattn_Wk': _L0_xattn_in['Wk'], 'L0_xattn_bk': _L0_xattn_in['bk'], 'L0_xattn_Wv': _L0_xattn_in['Wv'], 'L0_xattn_bv': _L0_xattn_in['bv'], 'L0_ffn_Wfc_s': _L0_ffn_in['Wfc_s'], 'L0_ffn_bfc_s': _L0_ffn_in['bfc_s'], 'L0_ffn_Wproj_s': _L0_ffn_in['Wproj_s'], 'L0_ffn_bproj_s': _L0_ffn_in['bproj_s'], 'L0_ffn_Wr': _L0_ffn_in['Wr'], 'L0_ffn_Wfc': _L0_ffn_in['Wfc'], 'L0_ffn_bfc': _L0_ffn_in['bfc'], 'L0_ffn_Wproj': _L0_ffn_in['Wproj'], 'L0_ffn_bproj': _L0_ffn_in['bproj'], 'L1_attn_Wq': _L1_attn_in['Wq'], 'L1_attn_Wk': _L1_attn_in['Wk'], 'L1_attn_Wv': _L1_attn_in['Wv'], 'L1_attn_Wo': _L1_attn_in['Wo'], 'L1_attn_bo': _L1_attn_in['bo'], 'L1_attn_ln1_g': _L1_attn_in['ln1_g'], 'L1_attn_ln1_b': _L1_attn_in['ln1_b'], 'L1_attn_W1': _L1_attn_in['W1'], 'L1_attn_b1': _L1_attn_in['b1'], 'L1_attn_W2': _L1_attn_in['W2'], 'L1_attn_b2': _L1_attn_in['b2'], 'L1_attn_ln2_g': _L1_attn_in['ln2_g'], 'L1_attn_ln2_b': _L1_attn_in['ln2_b'], 'L1_xattn_Wq': _L1_xattn_in['Wq'], 'L1_xattn_Wkv': _L1_xattn_in['Wkv'], 'L1_xattn_Wo': _L1_xattn_in['Wo'], 'L1_ffn_gate_w': _L1_ffn_in['gate_w'], 'L1_ffn_gate_b': _L1_ffn_in['gate_b'], 'L1_ffn_w0': _L1_ffn_in['w0'], 'L1_ffn_b0': _L1_ffn_in['b0'], 'L1_ffn_w1': _L1_ffn_in['w1'], 'L1_ffn_b1': _L1_ffn_in['b1'], 'L1_ffn_w2': _L1_ffn_in['w2'], 'L1_ffn_b2': _L1_ffn_in['b2'], 'L2_attn_Wq': _L2_attn_in['Wq'], 'L2_attn_bq': _L2_attn_in['bq'], 'L2_attn_Wk': _L2_attn_in['Wk'], 'L2_attn_bk': _L2_attn_in['bk'], 'L2_attn_Wv': _L2_attn_in['Wv'], 'L2_attn_bv': _L2_attn_in['bv'], 'L2_attn_Wo': _L2_attn_in['Wo'], 'L2_attn_bo': _L2_attn_in['bo'], 'L2_xattn_ln1_g': _L2_xattn_in['ln1_g'], 'L2_xattn_ln1_b': _L2_xattn_in['ln1_b'], 'L2_xattn_ln2_g': _L2_xattn_in['ln2_g'], 'L2_xattn_ln2_b': _L2_xattn_in['ln2_b'], 'L2_xattn_a1_wq': _L2_xattn_in['a1_wq'], 'L2_xattn_a1_wk': _L2_xattn_in['a1_wk'], 'L2_xattn_a1_wv': _L2_xattn_in['a1_wv'], 'L2_xattn_a1_li1_w': _L2_xattn_in['a1_li1_w'], 'L2_xattn_a1_li1_b': _L2_xattn_in['a1_li1_b'], 'L2_xattn_a1_lnx_g': _L2_xattn_in['a1_lnx_g'], 'L2_xattn_a1_lnx_b': _L2_xattn_in['a1_lnx_b'], 'L2_xattn_a1_lny_g': _L2_xattn_in['a1_lny_g'], 'L2_xattn_a1_lny_b': _L2_xattn_in['a1_lny_b'], 'L2_xattn_a1_ln3_g': _L2_xattn_in['a1_ln3_g'], 'L2_xattn_a1_ln3_b': _L2_xattn_in['a1_ln3_b'], 'L2_xattn_a1_li2_w': _L2_xattn_in['a1_li2_w'], 'L2_xattn_a1_li2_b': _L2_xattn_in['a1_li2_b'], 'L2_xattn_a1_li3_w': _L2_xattn_in['a1_li3_w'], 'L2_xattn_a1_li3_b': _L2_xattn_in['a1_li3_b'], 'L2_xattn_a2_wq': _L2_xattn_in['a2_wq'], 'L2_xattn_a2_wk': _L2_xattn_in['a2_wk'], 'L2_xattn_a2_wv': _L2_xattn_in['a2_wv'], 'L2_xattn_a2_li1_w': _L2_xattn_in['a2_li1_w'], 'L2_xattn_a2_li1_b': _L2_xattn_in['a2_li1_b'], 'L2_xattn_a2_lnx_g': _L2_xattn_in['a2_lnx_g'], 'L2_xattn_a2_lnx_b': _L2_xattn_in['a2_lnx_b'], 'L2_xattn_a2_lny_g': _L2_xattn_in['a2_lny_g'], 'L2_xattn_a2_lny_b': _L2_xattn_in['a2_lny_b'], 'L2_xattn_a2_ln3_g': _L2_xattn_in['a2_ln3_g'], 'L2_xattn_a2_ln3_b': _L2_xattn_in['a2_ln3_b'], 'L2_xattn_a2_li2_w': _L2_xattn_in['a2_li2_w'], 'L2_xattn_a2_li2_b': _L2_xattn_in['a2_li2_b'], 'L2_xattn_a2_li3_w': _L2_xattn_in['a2_li3_w'], 'L2_xattn_a2_li3_b': _L2_xattn_in['a2_li3_b'], 'L2_ffn_weight': _L2_ffn_in['weight'], 'L3_attn_W_q': _L3_attn_in['W_q'], 'L3_attn_b_q': _L3_attn_in['b_q'], 'L3_attn_W_k': _L3_attn_in['W_k'], 'L3_attn_b_k': _L3_attn_in['b_k'], 'L3_attn_W_v': _L3_attn_in['W_v'], 'L3_attn_b_v': _L3_attn_in['b_v'], 'L3_attn_W_o': _L3_attn_in['W_o'], 'L3_attn_b_o': _L3_attn_in['b_o'], 'L3_attn_rel_k_table': _L3_attn_in['rel_k_table'], 'L3_attn_rel_v_table': _L3_attn_in['rel_v_table'], 'L3_xattn_Wq': _L3_xattn_in['Wq'], 'L3_xattn_bq': _L3_xattn_in['bq'], 'L3_xattn_Wk': _L3_xattn_in['Wk'], 'L3_xattn_bk': _L3_xattn_in['bk'], 'L3_xattn_Wv': _L3_xattn_in['Wv'], 'L3_xattn_bv': _L3_xattn_in['bv'], 'L3_ffn_Wq': _L3_ffn_in['Wq'], 'L3_ffn_Wk': _L3_ffn_in['Wk'], 'L3_ffn_Wv': _L3_ffn_in['Wv'], 'L3_ffn_Wo': _L3_ffn_in['Wo'], 'L3_ffn_bo': _L3_ffn_in['bo'], 'L3_ffn_Wr': _L3_ffn_in['Wr'], 'L3_ffn_We1': _L3_ffn_in['We1'], 'L3_ffn_be1': _L3_ffn_in['be1'], 'L3_ffn_We2': _L3_ffn_in['We2'], 'L3_ffn_be2': _L3_ffn_in['be2'], 'L3_ffn_ln1_g': _L3_ffn_in['ln1_g'], 'L3_ffn_ln1_b': _L3_ffn_in['ln1_b'], 'L3_ffn_ln2_g': _L3_ffn_in['ln2_g'], 'L3_ffn_ln2_b': _L3_ffn_in['ln2_b']}

def reference(x, ctx_512, L0_attn_Wq, L0_attn_Wk, L0_attn_Wv, L0_attn_Wo, L0_xattn_Wq, L0_xattn_bq, L0_xattn_Wk, L0_xattn_bk, L0_xattn_Wv, L0_xattn_bv, L0_ffn_Wfc_s, L0_ffn_bfc_s, L0_ffn_Wproj_s, L0_ffn_bproj_s, L0_ffn_Wr, L0_ffn_Wfc, L0_ffn_bfc, L0_ffn_Wproj, L0_ffn_bproj, L1_attn_Wq, L1_attn_Wk, L1_attn_Wv, L1_attn_Wo, L1_attn_bo, L1_attn_ln1_g, L1_attn_ln1_b, L1_attn_W1, L1_attn_b1, L1_attn_W2, L1_attn_b2, L1_attn_ln2_g, L1_attn_ln2_b, L1_xattn_Wq, L1_xattn_Wkv, L1_xattn_Wo, L1_ffn_gate_w, L1_ffn_gate_b, L1_ffn_w0, L1_ffn_b0, L1_ffn_w1, L1_ffn_b1, L1_ffn_w2, L1_ffn_b2, L2_attn_Wq, L2_attn_bq, L2_attn_Wk, L2_attn_bk, L2_attn_Wv, L2_attn_bv, L2_attn_Wo, L2_attn_bo, L2_xattn_ln1_g, L2_xattn_ln1_b, L2_xattn_ln2_g, L2_xattn_ln2_b, L2_xattn_a1_wq, L2_xattn_a1_wk, L2_xattn_a1_wv, L2_xattn_a1_li1_w, L2_xattn_a1_li1_b, L2_xattn_a1_lnx_g, L2_xattn_a1_lnx_b, L2_xattn_a1_lny_g, L2_xattn_a1_lny_b, L2_xattn_a1_ln3_g, L2_xattn_a1_ln3_b, L2_xattn_a1_li2_w, L2_xattn_a1_li2_b, L2_xattn_a1_li3_w, L2_xattn_a1_li3_b, L2_xattn_a2_wq, L2_xattn_a2_wk, L2_xattn_a2_wv, L2_xattn_a2_li1_w, L2_xattn_a2_li1_b, L2_xattn_a2_lnx_g, L2_xattn_a2_lnx_b, L2_xattn_a2_lny_g, L2_xattn_a2_lny_b, L2_xattn_a2_ln3_g, L2_xattn_a2_ln3_b, L2_xattn_a2_li2_w, L2_xattn_a2_li2_b, L2_xattn_a2_li3_w, L2_xattn_a2_li3_b, L2_ffn_weight, L3_attn_W_q, L3_attn_b_q, L3_attn_W_k, L3_attn_b_k, L3_attn_W_v, L3_attn_b_v, L3_attn_W_o, L3_attn_b_o, L3_attn_rel_k_table, L3_attn_rel_v_table, L3_xattn_Wq, L3_xattn_bq, L3_xattn_Wk, L3_xattn_bk, L3_xattn_Wv, L3_xattn_bv, L3_ffn_Wq, L3_ffn_Wk, L3_ffn_Wv, L3_ffn_Wo, L3_ffn_bo, L3_ffn_Wr, L3_ffn_We1, L3_ffn_be1, L3_ffn_We2, L3_ffn_be2, L3_ffn_ln1_g, L3_ffn_ln1_b, L3_ffn_ln2_g, L3_ffn_ln2_b):
    import jax
    import jax.numpy as jnp

    def _L0_attn_ref(x, Wq, Wk, Wv, Wo):
        import jax, jax.numpy as jnp
        import numpy as np
        NUM_HEADS = 16
        THETA = 10000.0

        def _rotate_half(x):
            x = x.reshape(x.shape[:-1] + (-1, 2))
            x1, x2 = (x[..., 0], x[..., 1])
            return jnp.stack((-x2, x1), axis=-1).reshape(x.shape[:-2] + (-1,))

        def _rope(x):
            d_k = x.shape[-1]
            seq_len = x.shape[-2]
            inv_freq = 1.0 / THETA ** (jnp.arange(0, d_k, 2, dtype=jnp.float32) / d_k)
            pos = jnp.arange(seq_len, dtype=jnp.float32)
            theta = pos[:, None] * inv_freq[None, :]
            cos = jnp.repeat(jnp.cos(theta), 2, axis=-1)
            sin = jnp.repeat(jnp.sin(theta), 2, axis=-1)
            return x * cos + _rotate_half(x) * sin
        B, S, D = x.shape
        H = NUM_HEADS
        d_k = D // H

        def split_heads(t):
            return t.reshape(B, S, H, d_k).transpose(0, 2, 1, 3)
        Q = split_heads(x @ Wq)
        K = split_heads(x @ Wk)
        V = split_heads(x @ Wv)
        Q = _rope(Q)
        K = _rope(K)
        scores = jnp.einsum('bhqd,bhkd->bhqk', Q, K) / jnp.sqrt(jnp.float32(d_k))
        causal = jnp.tril(jnp.ones((S, S), dtype=bool))
        scores = jnp.where(causal[None, None], scores, -jnp.inf)
        attn = jax.nn.softmax(scores, axis=-1)
        out = jnp.einsum('bhqk,bhkd->bhqd', attn, V)
        out = out.transpose(0, 2, 1, 3).reshape(B, S, D)
        return out @ Wo

    def _L0_xattn_ref(query, key, value, Wq, bq, Wk, bk, Wv, bv):
        import jax, jax.numpy as jnp
        import numpy as np
        B, LQ, LK = (8, 256, 256)
        QD, KD, VD = (128, 64, 64)
        q = jnp.einsum('bld,de->ble', query, Wq) + bq
        k = jnp.einsum('bld,de->ble', key, Wk) + bk
        v = jnp.einsum('bld,de->ble', value, Wv) + bv
        scores = jnp.einsum('bqe,bke->bqk', q, k)
        attn = jax.nn.softmax(scores, axis=-1)
        out = jnp.einsum('bqk,bke->bqe', attn, v)
        return out

    def _L0_ffn_ref(x, Wfc_s, bfc_s, Wproj_s, bproj_s, Wr, Wfc, bfc, Wproj, bproj):
        import jax, jax.numpy as jnp
        import numpy as np
        import math
        N_EMBD = 128
        HIDDEN = 4 * N_EMBD
        N_EXPERTS = 8
        TOP_K = 2
        B, T = (4, 256)

        def new_gelu(x):
            c = math.sqrt(2.0 / math.pi)
            return 0.5 * x * (1.0 + jnp.tanh(c * (x + 0.044715 * x * x * x)))

        def _moe_forward(x, Wfc_s, bfc_s, Wproj_s, bproj_s, Wr, Wfc, bfc, Wproj, bproj):
            Bb, Tt, C = x.shape
            xf = x.reshape(Bb * Tt, C)
            N = Bb * Tt
            shared = new_gelu(xf @ Wfc_s + bfc_s) @ Wproj_s + bproj_s
            logits = xf @ Wr
            probs = jax.nn.softmax(logits, axis=-1)
            topk_p, topk_i = jax.lax.top_k(probs, TOP_K)
            topk_p = topk_p / jnp.sum(topk_p, axis=-1, keepdims=True)
            gate = jnp.zeros((N, N_EXPERTS), dtype=xf.dtype)
            gate = gate.at[jnp.arange(N)[:, None], topk_i].add(topk_p)
            routed = jnp.zeros_like(xf)
            for e in range(N_EXPERTS):
                h = new_gelu(xf @ Wfc[e] + bfc[e]) @ Wproj[e] + bproj[e]
                routed = routed + h * gate[:, e:e + 1]
            return (shared + routed).reshape(Bb, Tt, C)
        return _moe_forward(x, Wfc_s, bfc_s, Wproj_s, bproj_s, Wr, Wfc, bfc, Wproj, bproj)

    def _L1_attn_ref(x, Wq, Wk, Wv, Wo, bo, ln1_g, ln1_b, W1, b1, W2, b2, ln2_g, ln2_b):
        import jax, jax.numpy as jnp
        import numpy as np
        B, T, DIM = (2, 512, 128)
        DEPTH, HEADS = (4, 8)
        DH = DIM // HEADS
        NLOCAL, WINDOW, BUCKET = (4, 128, 64)
        MULT = 4

        def layer_norm(x, g, b, eps=1e-05):
            m = jnp.mean(x, -1, keepdims=True)
            v = jnp.mean(jnp.square(x - m), -1, keepdims=True)
            return (x - m) * jax.lax.rsqrt(v + eps) * g + b

        def causal_linear_attn(q, k, v):
            b, h, n, e = q.shape
            u = n // BUCKET
            q = jax.nn.softmax(q, axis=-1)
            k = jax.nn.elu(k) + 1.0
            bq = q.reshape(b, h, u, BUCKET, e)
            bk = k.reshape(b, h, u, BUCKET, e)
            bv = v.reshape(b, h, u, BUCKET, e)
            k_cum = jnp.cumsum(bk.sum(axis=-2), axis=-2)
            ctx = jnp.einsum('bhund,bhune->bhude', bk, bv)
            ctx = jnp.cumsum(ctx, axis=2)
            ctx = ctx / (k_cum[..., None] + 1e-06)
            ctx = jnp.pad(ctx, ((0, 0), (0, 0), (1, 0), (0, 0), (0, 0)))[:, :, :-1]
            out = jnp.einsum('bhund,bhude->bhune', bq, ctx)
            return out.reshape(b, h, n, e)

        def local_attn(q, k, v):
            b, lh, t, e = q.shape
            bh = b * lh
            nb = t // WINDOW
            bq = q.reshape(bh, nb, WINDOW, e)
            bk = k.reshape(bh, nb, WINDOW, e)
            bv = v.reshape(bh, nb, WINDOW, e)

            def look_around(x):
                padded = jnp.pad(x, ((0, 0), (1, 0), (0, 0), (0, 0)))
                return jnp.concatenate([padded[:, :-1], padded[:, 1:]], axis=2)
            bk2 = look_around(bk)
            bv2 = look_around(bv)
            tix = jnp.arange(t).reshape(1, nb, WINDOW)
            tpad = jnp.pad(tix, ((0, 0), (1, 0), (0, 0)), constant_values=-1)
            kix = jnp.concatenate([tpad[:, :-1], tpad[:, 1:]], axis=2)
            dots = jnp.einsum('bwie,bwje->bwij', bq, bk2) * e ** (-0.5)
            mask_value = -jnp.finfo(dots.dtype).max
            causal_mask = tix[:, :, :, None] < kix[:, :, None, :]
            pad_mask = (kix == -1)[:, :, None, :]
            dots = jnp.where(causal_mask | pad_mask, mask_value, dots)
            attn = jax.nn.softmax(dots, axis=-1)
            out = jnp.einsum('bwij,bwje->bwie', attn, bv2)
            return out.reshape(b, lh, t, e)

        def self_attention(x, Wq, Wk, Wv, Wo, bo):
            b, t, _ = x.shape
            mh = lambda z: z.reshape(b, t, HEADS, DH).transpose(0, 2, 1, 3)
            q, k, v = (mh(x @ Wq), mh(x @ Wk), mh(x @ Wv))
            lo = local_attn(q[:, :NLOCAL], k[:, :NLOCAL], v[:, :NLOCAL])
            go = causal_linear_attn(q[:, NLOCAL:], k[:, NLOCAL:], v[:, NLOCAL:])
            out = jnp.concatenate([lo, go], axis=1)
            out = out.transpose(0, 2, 1, 3).reshape(b, t, DIM)
            return out @ Wo + bo
        for i in range(DEPTH):
            x = x + self_attention(layer_norm(x, ln1_g[i], ln1_b[i]), Wq[i], Wk[i], Wv[i], Wo[i], bo[i])
            h = layer_norm(x, ln2_g[i], ln2_b[i])
            x = x + (jax.nn.gelu(h @ W1[i] + b1[i], approximate=False) @ W2[i] + b2[i])
        return x

    def _L1_xattn_ref(x, z, Wq, Wkv, Wo):
        import jax, jax.numpy as jnp
        import numpy as np
        DIM = 128
        LATENT_DIM = 64
        NUM_HEADS = 16
        HEAD_DIM = DIM // NUM_HEADS
        SCALE = HEAD_DIM ** (-0.5)
        B, xN, _ = x.shape
        _, zN, _ = z.shape
        Q = (x @ Wq.T).reshape(B, xN, NUM_HEADS, HEAD_DIM)
        KV = (z @ Wkv.T).reshape(B, zN, 2, NUM_HEADS, HEAD_DIM)
        K = KV[:, :, 0]
        V = KV[:, :, 1]
        attn = jnp.einsum('bqhd,bkhd->bhqk', Q, K) * SCALE
        attn = jax.nn.softmax(attn, axis=-1)
        O = jnp.einsum('bhqk,bkhd->bqhd', attn, V).reshape(B, xN, DIM)
        return O @ Wo.T

    def _L1_ffn_ref(x, gate_w, gate_b, w0, b0, w1, b1, w2, b2):
        import jax, jax.numpy as jnp
        import numpy as np
        E, TOP_K, D, H = (8, 2, 128, 256)
        B, S = (2, 256)
        Bn, Sq, Dv = x.shape
        xt = x.reshape(-1, Dv)
        logits = xt @ gate_w.T + gate_b
        top_v, top_i = jax.lax.top_k(logits, TOP_K)
        h0 = jnp.einsum('td,ehd->eth', xt, w0) + b0[:, None, :]
        h1 = jnp.einsum('td,ehd->eth', xt, w1) + b1[:, None, :]
        act = h0 * jax.nn.silu(h1)
        out_all = jnp.einsum('eth,edh->etd', act, w2) + b2[:, None, :]
        out_te = jnp.transpose(out_all, (1, 0, 2))
        sel = jnp.take_along_axis(out_te, top_i[:, :, None], axis=1)
        w = jax.nn.softmax(top_v, axis=-1)[:, :, None]
        out = (w * sel).sum(axis=1)
        return out.reshape(Bn, Sq, Dv)

    def _L2_attn_ref(x, Wq, bq, Wk, bk, Wv, bv, Wo, bo):
        import jax, jax.numpy as jnp
        import numpy as np
        N_EMBD = 128
        N_HEAD = 16
        HEAD_DIM = N_EMBD // N_HEAD
        B, T, C = x.shape
        H, D = (N_HEAD, HEAD_DIM)
        q = (x @ Wq + bq).reshape(B, T, H, D).transpose(0, 2, 1, 3)
        k = (x @ Wk + bk).reshape(B, T, H, D).transpose(0, 2, 1, 3)
        v = (x @ Wv + bv).reshape(B, T, H, D).transpose(0, 2, 1, 3)
        scores = jnp.einsum('bhqd,bhkd->bhqk', q, k) / jnp.sqrt(jnp.float32(D))
        causal = jnp.tril(jnp.ones((T, T), dtype=bool))
        scores = jnp.where(causal[None, None, :, :], scores, -jnp.inf)
        weights = jax.nn.softmax(scores, axis=-1)
        out = jnp.einsum('bhqk,bhkd->bhqd', weights, v)
        out = out.transpose(0, 2, 1, 3).reshape(B, T, C)
        return out @ Wo + bo

    def _L2_xattn_ref(xx, ee, ln1_g, ln1_b, ln2_g, ln2_b, a1_wq, a1_wk, a1_wv, a1_li1_w, a1_li1_b, a1_lnx_g, a1_lnx_b, a1_lny_g, a1_lny_b, a1_ln3_g, a1_ln3_b, a1_li2_w, a1_li2_b, a1_li3_w, a1_li3_b, a2_wq, a2_wk, a2_wv, a2_li1_w, a2_li1_b, a2_lnx_g, a2_lnx_b, a2_lny_g, a2_lny_b, a2_ln3_g, a2_ln3_b, a2_li2_w, a2_li2_b, a2_li3_w, a2_li3_b, training):
        import jax, jax.numpy as jnp
        import numpy as np
        H, D, C1, C2, S, M, B, W = (16, 32, 128, 64, 256, 64, 2, 4)

        def _ln(x, g, b):
            m = jnp.mean(x, -1, keepdims=True)
            v = jnp.var(x, -1, keepdims=True)
            return (x - m) * jax.lax.rsqrt(v + 1e-05) * g + b

        def _mha(x, y, wq, wk, wv, li1_w, li1_b, lnx_g, lnx_b, lny_g, lny_b, ln3_g, ln3_b, li2_w, li2_b, li3_w, li3_b, causal):
            xn = _ln(x, lnx_g, lnx_b)
            yn = _ln(y, lny_g, lny_b)
            q = jnp.einsum('bsc,hcd->bhsd', xn, wq)
            k = jnp.einsum('btc,hcd->bhtd', yn, wk)
            v = jnp.einsum('btc,hcd->bhtd', yn, wv)
            a = jax.nn.softmax(jnp.einsum('bhsd,bhtd->bhst', q, k) * D ** (-0.5), axis=-1)
            if causal:
                s, t = (a.shape[-2], a.shape[-1])
                mask = (jnp.arange(t)[None, :] > jnp.arange(s)[:, None]).astype(a.dtype)
                a = a * mask
            o = jnp.einsum('bhst,bhtd->bhsd', a, v)
            o = o.transpose(0, 2, 1, 3).reshape(x.shape[0], x.shape[1], H * D)
            x_out = x + o @ li1_w + li1_b
            h = jax.nn.gelu(_ln(x_out, ln3_g, ln3_b) @ li2_w + li2_b, approximate=False)
            return x_out + h @ li3_w + li3_b
        x = _ln(xx, ln1_g, ln1_b)
        x = x + _mha(x, x, a1_wq, a1_wk, a1_wv, a1_li1_w, a1_li1_b, a1_lnx_g, a1_lnx_b, a1_lny_g, a1_lny_b, a1_ln3_g, a1_ln3_b, a1_li2_w, a1_li2_b, a1_li3_w, a1_li3_b, causal=True)
        x = _ln(x, ln2_g, ln2_b)
        return x + _mha(x, ee, a2_wq, a2_wk, a2_wv, a2_li1_w, a2_li1_b, a2_lnx_g, a2_lnx_b, a2_lny_g, a2_lny_b, a2_ln3_g, a2_ln3_b, a2_li2_w, a2_li2_b, a2_li3_w, a2_li3_b, causal=False)

    def _L2_ffn_ref(x, weight):
        import jax, jax.numpy as jnp
        import numpy as np
        EPS = 1e-05

        @jax.custom_vjp
        def ste_quantize(w):
            scale = jnp.maximum(jnp.mean(jnp.abs(w)), EPS)
            return jnp.clip(jnp.round(w / scale), -1.0, 1.0)

        def _ste_fwd(w):
            return (ste_quantize(w), None)

        def _ste_bwd(_, g):
            return (g,)
        ste_quantize.defvjp(_ste_fwd, _ste_bwd)
        w_ternary = ste_quantize(weight)
        scale = jnp.maximum(jnp.mean(jnp.abs(weight)), EPS)
        return jnp.einsum('bsi,oi->bso', x, w_ternary * scale)

    def _L3_attn_ref(x, W_q, b_q, W_k, b_k, W_v, b_v, W_o, b_o, rel_k_table, rel_v_table):
        import jax, jax.numpy as jnp
        import numpy as np
        EMBED_DIM = 128
        NUM_HEADS = 16
        HEAD_DIM = EMBED_DIM // NUM_HEADS
        SEQ_LEN = 128
        BATCH = 4
        MAX_REL_POS = 2

        def _rel_index(length_q, length_k):
            q = jnp.arange(length_q)[:, None]
            k = jnp.arange(length_k)[None, :]
            return jnp.clip(k - q, -MAX_REL_POS, MAX_REL_POS) + MAX_REL_POS
        B, S, E = x.shape
        H, D = (NUM_HEADS, HEAD_DIM)
        scale = jnp.sqrt(jnp.asarray(D, x.dtype))
        Q = x @ W_q + b_q
        K = x @ W_k + b_k
        V = x @ W_v + b_v
        Qh = Q.reshape(B, S, H, D).transpose(0, 2, 1, 3)
        Kh = K.reshape(B, S, H, D).transpose(0, 2, 1, 3)
        Vh = V.reshape(B, S, H, D).transpose(0, 2, 1, 3)
        scores = jnp.einsum('bhqd,bhkd->bhqk', Qh, Kh)
        idx = _rel_index(S, S)
        rel_k = rel_k_table[idx]
        scores = (scores + jnp.einsum('bhqd,qkd->bhqk', Qh, rel_k)) / scale
        causal = jnp.tril(jnp.ones((S, S), dtype=bool))
        scores = jnp.where(causal[None, None], scores, jnp.asarray(-1000000000.0, scores.dtype))
        attn = jax.nn.softmax(scores, axis=-1)
        out = jnp.einsum('bhqk,bhkd->bhqd', attn, Vh)
        rel_v = rel_v_table[idx]
        out = out + jnp.einsum('bhqk,qkd->bhqd', attn, rel_v)
        out = out.transpose(0, 2, 1, 3).reshape(B, S, E)
        return out @ W_o + b_o

    def _L3_xattn_ref(query, key, value, Wq, bq, Wk, bk, Wv, bv):
        import jax, jax.numpy as jnp
        import numpy as np
        B, LQ, LK = (8, 256, 256)
        QD, KD, VD = (128, 64, 64)
        q = jnp.einsum('bld,de->ble', query, Wq) + bq
        k = jnp.einsum('bld,de->ble', key, Wk) + bk
        v = jnp.einsum('bld,de->ble', value, Wv) + bv
        scores = jnp.einsum('bqe,bke->bqk', q, k)
        attn = jax.nn.softmax(scores, axis=-1)
        out = jnp.einsum('bqk,bke->bqe', attn, v)
        return out

    def _L3_ffn_ref(x, Wq, Wk, Wv, Wo, bo, Wr, We1, be1, We2, be2, ln1_g, ln1_b, ln2_g, ln2_b):
        import jax, jax.numpy as jnp
        import numpy as np
        B, S, D, H, F, E = (2, 128, 128, 16, 512, 8)
        HD = D // H
        EPS = 1e-06

        def _layernorm(x, g, b):
            m = jnp.mean(x, axis=-1, keepdims=True)
            v = jnp.var(x, axis=-1, keepdims=True)
            return (x - m) / jnp.sqrt(v + EPS) * g + b
        b, s, d = x.shape

        def split_heads(t):
            return t.reshape(b, s, H, HD).transpose(0, 2, 1, 3)
        q = split_heads(x @ Wq)
        k = split_heads(x @ Wk)
        v = split_heads(x @ Wv)
        scores = jnp.einsum('bhqd,bhkd->bhqk', q, k) / jnp.sqrt(jnp.float32(HD))
        attn_w = jax.nn.softmax(scores, axis=-1)
        ctx = jnp.einsum('bhqk,bhkd->bhqd', attn_w, v)
        ctx = ctx.transpose(0, 2, 1, 3).reshape(b, s, d)
        attn_out = ctx @ Wo + bo
        out1 = _layernorm(x + attn_out, ln1_g, ln1_b)
        router_probs = jax.nn.softmax(out1 @ Wr, axis=-1)
        top_g, top_i = jax.lax.top_k(router_probs, 2)
        top_g = jax.nn.softmax(top_g, axis=-1)
        acc = jnp.zeros_like(out1)
        for e in range(E):
            sel = top_i == e
            msk = jnp.any(sel, axis=-1)[..., None].astype(out1.dtype)
            h = jax.nn.gelu(out1 * msk @ We1[e] + be1[e], approximate=False)
            o = h @ We2[e] + be2[e]
            gate = jnp.sum(top_g * sel.astype(top_g.dtype), axis=-1, keepdims=True)
            acc = acc + o * gate
        return _layernorm(out1 + acc, ln2_g, ln2_b)
    x = _layernorm(x + _L0_attn_ref(x, L0_attn_Wq, L0_attn_Wk, L0_attn_Wv, L0_attn_Wo), axis=-1)
    x = _layernorm(x + _L0_xattn_ref(x, ctx_512, ctx_512, L0_xattn_Wq, L0_xattn_bq, L0_xattn_Wk, L0_xattn_bk, L0_xattn_Wv, L0_xattn_bv), axis=-1)
    x = _layernorm(x + _L0_ffn_ref(x, L0_ffn_Wfc_s, L0_ffn_bfc_s, L0_ffn_Wproj_s, L0_ffn_bproj_s, L0_ffn_Wr, L0_ffn_Wfc, L0_ffn_bfc, L0_ffn_Wproj, L0_ffn_bproj), axis=-1)
    x = _layernorm(x + _L1_attn_ref(x, L1_attn_Wq, L1_attn_Wk, L1_attn_Wv, L1_attn_Wo, L1_attn_bo, L1_attn_ln1_g, L1_attn_ln1_b, L1_attn_W1, L1_attn_b1, L1_attn_W2, L1_attn_b2, L1_attn_ln2_g, L1_attn_ln2_b), axis=-1)
    x = _layernorm(x + _L1_xattn_ref(x, ctx_512, L1_xattn_Wq, L1_xattn_Wkv, L1_xattn_Wo), axis=-1)
    x = _layernorm(x + _L1_ffn_ref(x, L1_ffn_gate_w, L1_ffn_gate_b, L1_ffn_w0, L1_ffn_b0, L1_ffn_w1, L1_ffn_b1, L1_ffn_w2, L1_ffn_b2), axis=-1)
    x = _layernorm(x + _L2_attn_ref(x, L2_attn_Wq, L2_attn_bq, L2_attn_Wk, L2_attn_bk, L2_attn_Wv, L2_attn_bv, L2_attn_Wo, L2_attn_bo), axis=-1)
    x = _layernorm(x + _L2_xattn_ref(x, ctx_512, L2_xattn_ln1_g, L2_xattn_ln1_b, L2_xattn_ln2_g, L2_xattn_ln2_b, L2_xattn_a1_wq, L2_xattn_a1_wk, L2_xattn_a1_wv, L2_xattn_a1_li1_w, L2_xattn_a1_li1_b, L2_xattn_a1_lnx_g, L2_xattn_a1_lnx_b, L2_xattn_a1_lny_g, L2_xattn_a1_lny_b, L2_xattn_a1_ln3_g, L2_xattn_a1_ln3_b, L2_xattn_a1_li2_w, L2_xattn_a1_li2_b, L2_xattn_a1_li3_w, L2_xattn_a1_li3_b, L2_xattn_a2_wq, L2_xattn_a2_wk, L2_xattn_a2_wv, L2_xattn_a2_li1_w, L2_xattn_a2_li1_b, L2_xattn_a2_lnx_g, L2_xattn_a2_lnx_b, L2_xattn_a2_lny_g, L2_xattn_a2_lny_b, L2_xattn_a2_ln3_g, L2_xattn_a2_ln3_b, L2_xattn_a2_li2_w, L2_xattn_a2_li2_b, L2_xattn_a2_li3_w, L2_xattn_a2_li3_b, 0), axis=-1)
    x = _layernorm(x + _L2_ffn_ref(x, L2_ffn_weight), axis=-1)
    x = _layernorm(x + _L3_attn_ref(x, L3_attn_W_q, L3_attn_b_q, L3_attn_W_k, L3_attn_b_k, L3_attn_W_v, L3_attn_b_v, L3_attn_W_o, L3_attn_b_o, L3_attn_rel_k_table, L3_attn_rel_v_table), axis=-1)
    x = _layernorm(x + _L3_xattn_ref(x, ctx_512, ctx_512, L3_xattn_Wq, L3_xattn_bq, L3_xattn_Wk, L3_xattn_bk, L3_xattn_Wv, L3_xattn_bv), axis=-1)
    x = _layernorm(x + _L3_ffn_ref(x, L3_ffn_Wq, L3_ffn_Wk, L3_ffn_Wv, L3_ffn_Wo, L3_ffn_bo, L3_ffn_Wr, L3_ffn_We1, L3_ffn_be1, L3_ffn_We2, L3_ffn_be2, L3_ffn_ln1_g, L3_ffn_ln1_b, L3_ffn_ln2_g, L3_ffn_ln2_b), axis=-1)
    return x

_drawn_inputs = setup_inputs


def setup_inputs(seed=0):
    import zlib

    import numpy as np

    out = dict(_drawn_inputs(seed))
    spreads = {'L0_xattn_bq': (0.0, 0.735),
     'L0_xattn_bk': (0.0, 2.0),
     'L0_xattn_bv': (0.0, 0.1),
     'L0_ffn_bfc_s': (0.0, 0.268),
     'L0_ffn_bproj_s': (0.0, 0.1),
     'L0_ffn_bfc': (0.0, 0.532),
     'L0_ffn_bproj': (0.0, 0.1),
     'L1_attn_bo': (0.0, 0.1),
     'L1_attn_ln1_g': (1.0, 0.6),
     'L1_attn_ln1_b': (0.0, 0.8),
     'L1_attn_b1': (0.0, 0.1),
     'L1_attn_b2': (0.0, 0.1),
     'L1_attn_ln2_g': (1.0, 0.6),
     'L1_attn_ln2_b': (0.0, 0.8),
     'L1_ffn_gate_b': (0.0, 0.27),
     'L1_ffn_b0': (0.0, 0.8),
     'L1_ffn_b1': (0.0, 0.8),
     'L1_ffn_b2': (0.0, 0.1),
     'L2_attn_bq': (0.0, 0.608),
     'L2_attn_bk': (0.0, 2.0),
     'L2_attn_bv': (0.0, 0.1),
     'L2_attn_bo': (0.0, 0.1),
     'L2_xattn_ln1_g': (1.0, 0.2),
     'L2_xattn_ln1_b': (0.0, 0.1),
     'L2_xattn_ln2_g': (1.0, 0.2),
     'L2_xattn_ln2_b': (0.0, 0.1),
     'L2_xattn_a1_li1_b': (0.0, 0.1),
     'L2_xattn_a1_lnx_g': (1.0, 0.6),
     'L2_xattn_a1_lnx_b': (0.0, 0.8),
     'L2_xattn_a1_lny_g': (1.0, 0.6),
     'L2_xattn_a1_lny_b': (0.0, 0.8),
     'L2_xattn_a1_ln3_g': (1.0, 0.6),
     'L2_xattn_a1_ln3_b': (0.0, 0.8),
     'L2_xattn_a1_li2_b': (0.0, 0.783),
     'L2_xattn_a1_li3_b': (0.0, 0.1),
     'L2_xattn_a2_li1_b': (0.0, 0.1),
     'L2_xattn_a2_lnx_g': (1.0, 0.6),
     'L2_xattn_a2_lnx_b': (0.0, 0.8),
     'L2_xattn_a2_lny_g': (1.0, 0.6),
     'L2_xattn_a2_lny_b': (0.0, 0.8),
     'L2_xattn_a2_ln3_g': (1.0, 0.6),
     'L2_xattn_a2_ln3_b': (0.0, 0.8),
     'L2_xattn_a2_li2_b': (0.0, 0.8),
     'L2_xattn_a2_li3_b': (0.0, 0.1),
     'L3_attn_b_q': (0.0, 0.8),
     'L3_attn_b_k': (0.0, 2.0),
     'L3_attn_b_v': (0.0, 0.1),
     'L3_attn_b_o': (0.0, 0.1),
     'L3_xattn_bq': (0.0, 0.8),
     'L3_xattn_bk': (0.0, 2.0),
     'L3_xattn_bv': (0.0, 0.1),
     'L3_ffn_bo': (0.0, 0.1),
     'L3_ffn_be1': (0.0, 0.8),
     'L3_ffn_be2': (0.0, 0.273),
     'L3_ffn_ln1_g': (1.0, 0.2),
     'L3_ffn_ln1_b': (0.0, 0.1),
     'L3_ffn_ln2_g': (1.0, 0.2),
     'L3_ffn_ln2_b': (0.0, 0.1)}
    factors = {'L0_attn_Wq': 8.0,
     'L0_attn_Wk': 8.0,
     'L0_xattn_Wq': 4.936,
     'L0_xattn_Wk': 3.78,
     'L1_attn_Wq': 8.0,
     'L1_attn_Wk': 8.0,
     'L1_attn_Wv': 2.858,
     'L1_attn_Wo': 2.913,
     'L1_ffn_w0': 8.0,
     'L1_ffn_w1': 8.0,
     'L1_ffn_w2': 8.0,
     'L2_xattn_a1_wq': 8.0,
     'L2_xattn_a1_wk': 8.0,
     'L2_xattn_a1_wv': 3.339,
     'L2_xattn_a1_li1_w': 3.348,
     'L2_xattn_a1_li2_w': 3.482,
     'L2_xattn_a1_li3_w': 2.904,
     'L2_xattn_a2_wq': 8.0,
     'L2_xattn_a2_wk': 8.0,
     'L2_xattn_a2_wv': 4.307,
     'L2_xattn_a2_li1_w': 4.197,
     'L2_xattn_a2_li2_w': 3.571,
     'L2_xattn_a2_li3_w': 3.263,
     'L3_xattn_Wq': 3.778,
     'L3_xattn_Wk': 3.623,
     'L3_ffn_Wq': 8.0,
     'L3_ffn_Wk': 8.0,
     'L3_ffn_Wv': 2.744,
     'L3_ffn_Wo': 2.696,
     'L3_ffn_We1': 2.928,
     'L3_ffn_We2': 2.724}
    for name, (base, spread) in spreads.items():
        noise = np.random.default_rng([zlib.crc32(name.encode()), seed]).standard_normal(out[name].shape)
        drawn = base * np.exp(spread * noise) if base else spread * noise
        out[name] = jnp.asarray(drawn.astype(out[name].dtype))
    for name, factor in factors.items():
        out[name] = (out[name] * factor).astype(out[name].dtype)
    return out
```

```python
from contextlib import ExitStack

import concourse.bass as bass
from concourse import mybir

F32 = mybir.dt.float32
BF16 = mybir.dt.bfloat16
ALU = mybir.AluOpType
ACT = mybir.ActivationFunctionType
AX_X = mybir.AxisListType.X

P = 128
BATCH = 32
CTX_LEN, CTX_DIM = 77, 64
CHAINS = 2
PER = 2
GROUP = CHAINS * PER
TOK = PER * P
CTOK = PER * CTX_LEN
HEADS = 16
EXPERTS = 8
MASKED = -1e30
DEPTH = 4


def small_entries():
    out = []
    for n in ("Wq", "Wqs", "Wk", "Wks", "Wv", "Wo"):
        out.append(("L0_attn_" + n, 128))
    for lv in ("L0", "L3"):
        out += [(lv + "_xattn_Wq", 128), (lv + "_xattn_Wk", 128), (lv + "_xattn_Wv", 128),
                (lv + "_xattn_bq", 1), (lv + "_xattn_bk", 1), (lv + "_xattn_bv_row", 128)]
    out += [("L0_ffn_Wr", EXPERTS), ("L0_ffn_b1", 4 * (EXPERTS + 1)), ("L0_ffn_b2", EXPERTS + 1)]
    for i in range(DEPTH):
        out += [(f"L1_{i}_{n}", 1) for n in ("bo", "ln1_g", "ln1_b", "ln2_g", "ln2_b", "b2")]
        out.append((f"L1_{i}_b1", 4))
    out += [("L1_xattn_Wq", 128), ("L1_xattn_Wk", 128), ("L1_xattn_Wv", 128), ("L1_xattn_Wo", 128)]
    out += [("L1_ffn_Wr", EXPERTS), ("L1_ffn_br_row", EXPERTS), ("L1_ffn_b0", 2 * EXPERTS),
            ("L1_ffn_b1", 2 * EXPERTS), ("L1_ffn_b2", EXPERTS)]
    for lv in ("L2", "L3"):
        out += [(f"{lv}_attn_W{n}", 128) for n in "qkvo"]
        out += [(f"{lv}_attn_b{n}", 1) for n in "qkvo"] + [(f"{lv}_attn_bv_row", 128)]
    out += [("L2_ln1_g", 1), ("L2_ln1_b", 1), ("L2_ln2_g", 1), ("L2_ln2_b", 1)]
    for a in ("L2_a1_", "L2_a2_"):
        out += [(a + n, 1) for n in ("lnx_g", "lnx_b", "lny_g", "lny_b", "ln3_g", "ln3_b", "li1_b", "li3_b")]
        out.append((a + "li2_b", 4))
    out.append(("L2_ffn_W", 128))
    out += [("L3_rel_k", 3), ("L3_rel_v", 3), ("L3_rel_v_row", 128)]
    out += [("L3_ffn_W" + n, 128) for n in "qkvo"]
    out += [("L3_ffn_bo", 1), ("L3_ffn_Wr", EXPERTS), ("L3_ffn_b1", 4 * EXPERTS), ("L3_ffn_b2", EXPERTS),
            ("L3_ffn_ln1_g", 1), ("L3_ffn_ln1_b", 1), ("L3_ffn_ln2_g", 1), ("L3_ffn_ln2_b", 1)]
    out += [("rope_cos", 128), ("rope_sin", 128), ("head_block", 128), ("head_pick", HEADS),
            ("ones8", 4 * 32), ("ones16", 2 * 32), ("mask8", 4), ("mask16", 2), ("lin_block", 64),
            ("descending", EXPERTS)]
    return out


def big_entries():
    l0 = [(f"L0_ffn_W1_{e}", 512) for e in range(EXPERTS + 1)]
    l0 = [x for e in range(EXPERTS + 1) for x in ((f"L0_ffn_W1_{e}", 512), (f"L0_ffn_W2_{e}", 512))]
    l1a = [x for i in range(DEPTH) for x in
           ((f"L1_{i}_Wq", 64), (f"L1_{i}_Wk", 64), (f"L1_{i}_Wlin", 128), (f"L1_{i}_Wv", 128), (f"L1_{i}_Wo", 128),
            (f"L1_{i}_W1", 512), (f"L1_{i}_W2", 512))]
    l1f = [x for e in range(EXPERTS) for x in
           ((f"L1_ffn_w0_{e}", 256), (f"L1_ffn_w1_{e}", 256), (f"L1_ffn_w2_{e}", 256))]
    l2x = [x for a in ("L2_a1_", "L2_a2_") for x in
           ((a + "wq", 512), (a + "wk", 512), (a + "wv", 512), (a + "li1", 512), (a + "li2", 512), (a + "li3", 512))]
    l3f = [x for e in range(EXPERTS) for x in ((f"L3_ffn_W1_{e}", 512), (f"L3_ffn_W2_{e}", 512))]
    return {"w_l0_ffn": l0, "w_l1_attn": l1a, "w_l1_ffn": l1f, "w_l2_xattn": l2x, "w_l3_ffn": l3f}


REGION = {"w_l0_ffn": "A", "w_l1_ffn": "A", "w_l3_ffn": "A", "w_l1_attn": "B", "w_l2_xattn": "B"}


def columns(entries):
    at, out = 0, {}
    for name, n in entries:
        out[name] = (at, n)
        at += n
    return out, at


def sequence():
    seq = []

    def norm(name, src, after, dst, **k):
        seq.append(dict(kind="norm", name=name, src=src, after=after, dst=dst, eps=1e-5, g=None, add=None) | k)
        return ("normed", name)

    def mha(name, src, after, res, dst, **k):
        seq.append(dict(kind="mha", name=name, src=src, after=after, res=res, dst=dst, D=8, nk=P, mask=None,
                        rope=False, rel=False, kv=None, kv_after=None, bias=False, bo=None, post=False,
                        linear=False) | k)
        return ("residual", name)

    def xattn(name, after):
        seq.append(dict(kind="xattn", name=name, src="x", after=after))
        return ("residual", name)

    def mlp(name, src, after, res, dst, adds, **k):
        seq.append(dict(kind="mlp", name=name, src=src, after=after, res=res, dst=dst, adds=adds) | k)
        return ("residual", name)

    def moe(name, src, after, **k):
        seq.append(dict(kind="moe", name=name, src=src, after=after) | k)
        return ("residual", name)

    e = mha("L0_attn", "x", ("x_loaded", ""), "x", "u", mask="causal", rope=True)
    e = norm("L0_attn_ln", "u", e, "x")
    e = xattn("L0_xattn", e)
    e = norm("L0_xattn_ln", "u", e, "x")
    e = moe("L0_ffn", "x", e, shared=True, act=ACT.Gelu_apprx_tanh, glu=False, on="logits", region="w_l0_ffn")
    e = norm("L0_ffn_ln", "u", e, "x")
    for i in range(DEPTH):
        n = f"L1_{i}"
        y = "x" if i == 0 else "y"
        e = norm(n + "_ln1", y, e, "hn", g=n + "_ln1")
        e = mha(n, "hn", e, y, "y", D=16, mask="causal", linear=True, bo=n + "_bo")
        e = norm(n + "_ln2", "y", e, "hn", g=n + "_ln2")
        last = i == DEPTH - 1
        e = mlp(n + "_mlp", "hn", e, "y", "u" if last else "y", ["x"] if last else [],
                W1=n + "_W1", b1=n + "_b1", W2=n + "_W2", b2=n + "_b2")
    e = norm("L1_attn_ln", "u", e, "x")
    e = mha("L1_xattn", "x", e, "x", "u", nk=CTX_LEN, kv="ctx", kv_after=("ctx_loaded", ""))
    e = norm("L1_xattn_ln", "u", e, "x")
    e = moe("L1_ffn", "x", e, shared=False, act=ACT.Silu, glu=True, on="logits", region="w_l1_ffn")
    e = norm("L1_ffn_ln", "u", e, "x")
    e = mha("L2_attn", "x", e, "x", "u", mask="causal", bias=True, bo="L2_attn_bo")
    e = norm("L2_attn_ln", "u", e, "x")
    e = norm("L2_ln1", "x", e, "y", g="L2_ln1")
    e = norm("L2_a1_lnx", "y", e, "hn", g="L2_a1_lnx", g2="L2_a1_lny", dst2="hn2")
    e = mha("L2_a1", "hn", e, "y", "z", D=32, kv="hn2", kv_after=e, post=True, bo="L2_a1_li1_b")
    e = norm("L2_a1_ln3", "z", e, "hn", g="L2_a1_ln3")
    e = mlp("L2_a1_mlp", "hn", e, "z", "y", ["y"], W1="L2_a1_li2", b1="L2_a1_li2_b", W2="L2_a1_li3", b2="L2_a1_li3_b")
    e = norm("L2_ln2", "y", e, "y", g="L2_ln2")
    e = norm("L2_a2_lnx", "y", e, "hn", g="L2_a2_lnx")
    c = norm("L2_a2_lny", "ctx", ("ctx_loaded", ""), "yc", g="L2_a2_lny", rows=CTX_DIM, cols=CTOK)
    e = mha("L2_a2", "hn", e, "y", "z", D=32, nk=CTX_LEN, kv="yc", kv_after=c, bo="L2_a2_li1_b")
    e = norm("L2_a2_ln3", "z", e, "hn", g="L2_a2_ln3")
    e = mlp("L2_a2_mlp", "hn", e, "z", "u", ["y", "x"], W1="L2_a2_li2", b1="L2_a2_li2_b", W2="L2_a2_li3",
            b2="L2_a2_li3_b")
    e = norm("L2_xattn_ln", "u", e, "x")
    seq.append(dict(kind="linear", name="L2_ffn", src="x", after=e))
    e = norm("L2_ffn_ln", "u", ("residual", "L2_ffn"), "x")
    e = mha("L3_attn", "x", e, "x", "u", mask="far", rel=True, bias=True, bo="L3_attn_bo")
    e = norm("L3_attn_ln", "u", e, "x")
    e = xattn("L3_xattn", e)
    e = norm("L3_xattn_ln", "u", e, "x")
    e = mha("L3_ffn", "x", e, "x", "u", bo="L3_ffn_bo")
    e = norm("L3_ffn_ln1", "u", e, "y", g="L3_ffn_ln1", eps=1e-6)
    e = moe("L3_ffn_moe", "y", e, shared=False, act=ACT.Gelu, glu=False, on="probs", region="w_l3_ffn")
    e = norm("L3_ffn_ln2", "u", e, "u", g="L3_ffn_ln2", eps=1e-6, add="x")
    e = norm("L3_ffn_ln", "u", e, "x")
    return seq, e


SEQ, LAST = sequence()
STOP_AFTER = None


class Events:

    def __init__(self, nc, ctx, known):
        self.known, self.counts, self.seen = known, {}, {}
        labels = sorted({label for label, _ in known})
        self.sems = {label: ctx.enter_context(nc.semaphore(label)) for label in labels}
        self.make = lambda label: ctx.enter_context(nc.semaphore(label))

    def sem(self, label):
        if label not in self.sems:
            self.sems[label] = self.make(label)
        return self.sems[label]

    def made(self, label, key, by=1):
        self.counts[label] = self.counts.get(label, 0) + by
        assert (label, key) not in self.seen, (label, key)
        self.seen[(label, key)] = self.counts[label]
        return self.sem(label), by

    def have(self, label, key):
        assert not self.known or (label, key) in self.known, (label, key)
        return self.sem(label), self.known.get((label, key), 1)


class Banks:

    def __init__(self, rings):
        self.rings, self.n, self.tenant, self.place = rings, {}, {}, {}

    def take(self, ring, tile, freed_by):
        i = self.n.get(ring, 0) % len(self.rings[ring])
        self.n[ring] = self.n.get(ring, 0) + 1
        bank = self.rings[ring][i]
        before = self.tenant.get((ring, i))
        self.tenant[(ring, i)] = freed_by
        self.place[tile] = bank
        return bank, before

    def where(self, tile):
        return self.place[tile]


def decoder(nc, io, known):
    small_at, small_cols = columns(small_entries())
    big_at, region_cols = {}, {"A": 0, "B": 0}
    for array, entries in big_entries().items():
        at, n = columns(entries)
        big_at |= {name: (REGION[array], *where) for name, where in at.items()}
        region_cols[REGION[array]] = max(region_cols[REGION[array]], n)
    seq, end = SEQ, LAST
    if STOP_AFTER is not None:
        seq = SEQ[:[st["name"] for st in SEQ].index(STOP_AFTER) + 1]
        end = ("normed", STOP_AFTER)
    C = range(CHAINS)
    S = range(PER)
    items = [(c, s) for c in C for s in S]

    with ExitStack() as ctx:
        def sb(name, shape, dt=F32):
            return ctx.enter_context(nc.sbuf_tensor(name, shape, dt))

        psum = [ctx.enter_context(nc.psum_tensor(f"bank{i}", [P, 512], F32)) for i in range(8)]
        ring = {"flow": psum[CHAINS:]} | {f"hold{c}": [psum[c]] for c in C}
        banks = Banks(ring)

        small = sb("small", [P, small_cols])
        region = {r: sb("region" + r, [P, n]) for r, n in region_cols.items()}

        def W(name, rows=P):
            if name in small_at:
                o, n = small_at[name]
                return small[0:rows, o:o + n]
            r, o, n = big_at[name]
            return region[r][0:rows, o:o + n]

        ident = sb("ident", [P, P])
        identb = sb("identb", [P, P], BF16)
        center = sb("center", [P, P])
        average = sb("average", [P, P])
        center64 = sb("center64", [CTX_DIM, CTX_DIM])
        average64 = sb("average64", [CTX_DIM, CTX_DIM])
        mask = {k: sb("mask_" + k, [P, P], BF16) for k in ("causal", "far")}
        maskT = {k: sb("maskT_" + k, [P, P], BF16) for k in ("causal", "far")}
        after_mask = sb("after_mask", [P, P])
        pick = sb("pick", [P, 4, P], BF16)
        spread = sb("spread", [32, P], BF16)
        ones32 = sb("ones32", [P, 32])
        ones_row = sb("ones_row", [1, P])
        eps = {1e-5: sb("eps5", [P, 1]), 1e-6: sb("eps6", [P, 1])}
        tern = sb("tern", [P, P])
        tern_neg = sb("tern_neg", [P, P])
        tcol = sb("tcol", [P, 4])
        rel_col = sb("rel_col", [P, 6])
        rel_row = sb("rel_row", [1, P])

        B = {}
        for n in ("x", "u", "y", "z", "hn", "hn2", "sq", "rs", "q", "k", "o", "oL1"):
            B[n] = [sb(f"{n}{c}", [P, TOK]) for c in C]
        B["ctx"] = [sb(f"ctx{c}", [CTX_DIM, CTOK]) for c in C]
        B["yc"] = [sb(f"yc{c}", [CTX_DIM, CTOK]) for c in C]
        qm = [sb(f"qm{c}", [P, PER, 4, P]) for c in C]
        km = [sb(f"km{c}", [P, PER, 4, P]) for c in C]
        vm = [sb(f"vm{c}", [P, PER, 4, P]) for c in C]
        v4 = [sb(f"v4{c}", [P, PER, 512]) for c in C]
        q4 = [qm[c][:].rearrange("p s j t -> p (s j t)").rearrange("p (t n) -> p t n", t=4) for c in C]
        k4 = [km[c][:].rearrange("p s j t -> p (s j t)").rearrange("p (t n) -> p t n", t=4) for c in C]
        vm16 = [sb(f"vm16{c}", [P, PER, 2, 64]) for c in C]
        vlin = [sb(f"vlin{c}", [P, PER, 65]) for c in C]
        work = sb("work", [P, 2, 2048])
        probs = [work[:, i].rearrange("p (r j t) -> p r j t", r=4, j=4) for i in range(2)]
        hid = [work[:].rearrange("p a b -> p (a b)")[:, c * 2 * 4 * TOK:(c + 1) * 2 * 4 * TOK]
               .rearrange("p (i m t) -> p i m t", i=2, m=4) for c in C]
        rowmax = [sb(f"rowmax{i}", [P, HEADS]) for i in range(2)]
        maxb = [sb(f"maxb{i}", [P, 4, 2, HEADS], BF16) for i in range(2)]
        maxT = [sb(f"maxT{i}", [P, P], BF16) for i in range(2)]
        recip = [sb(f"recip{i}", [P, 512]) for i in range(2)]
        diag = [sb(f"diag{c}", [P, PER, 32]) for c in C]
        qe = [sb(f"qe{c}", [P, PER, 64]) for c in C]
        ke = [sb(f"ke{c}", [P, PER, 64]) for c in C]
        kx = [sb(f"kx{c}", [P, PER, 64]) for c in C]
        qT = [sb(f"qT{c}", [64, TOK]) for c in C]
        lctx = [sb(f"lctx{c}", [64, PER, 64]) for c in C]
        lcol = [sb(f"lcol{c}", [P, 4 * PER * 4]) for c in C]
        gate = [sb(f"gate{c}", [P, PER, EXPERTS]) for c in C]
        gtmp = [sb(f"gtmp{c}", [P, 8, PER, EXPERTS]) for c in C]
        gcol = [sb(f"gcol{c}", [P, 8, PER]) for c in C]
        gb = [sb(f"gb{c}", [P, TOK]) for c in C]
        part = [sb(f"part{c}", [P, TOK]) for c in C]
        silu = [sb(f"silu{c}", [P, 2, TOK]) for c in C]
        px = [part[c][:, 0:CTOK].rearrange("p (s k) -> p s k", s=PER) for c in C]
        pxT = [km[c][:, :, 0, :] for c in C]
        vx = [qm[c][:, :, 0, :] for c in C]
        xcol = [sb(f"xcol{c}", [P, 3, PER]) for c in C]

        w_small = ctx.enter_context(nc.semaphore("w_small"))
        cleared = ctx.enter_context(nc.semaphore("cleared"))
        shaped = ctx.enter_context(nc.semaphore("shaped"))
        setup_step = ctx.enter_context(nc.semaphore("setup_step"))
        setup_sum = ctx.enter_context(nc.semaphore("setup_sum"))

        with nc.Block() as block:
            @block.sync
            def _(sp):
                sp.dma_start(small[:], io["w_small"]).then_inc(w_small, 16)

            @block.gpsimd
            def _(pool):
                n = 0
                for t, value in [(ident, 0.0), (identb, 0.0), (pick, 0.0), (spread, 0.0), (after_mask, 1.0)] + \
                        [(m, 0.0) for m in list(mask.values()) + list(maskT.values())]:
                    nc.gpsimd.memset(t[:], value).then_inc(cleared, 1)
                    n += 1
                pool.wait_ge(cleared, n)

                def keep(t, op, fill, base, step, per_row, pattern=None):
                    return nc.gpsimd.affine_select(out=t[:], in_=t[:], compare_op=op, fill=fill, base=base,
                                                   pattern=pattern or [[step, P]], channel_multiplier=per_row)
                keep(ident, ALU.not_equal, 1.0, 0, -1, 1).then_inc(shaped, 1)
                keep(identb, ALU.not_equal, 1.0, 0, -1, 1).then_inc(shaped, 1)
                for name, back in (("causal", 0), ("far", -2)):
                    keep(mask[name], ALU.is_ge, MASKED, back, -1, 1).then_inc(shaped, 1)
                    keep(maskT[name], ALU.is_ge, MASKED, back, 1, -1).then_inc(shaped, 1)
                keep(after_mask, ALU.is_ge, 0.0, -1, -1, 1).then_inc(shaped, 1)
                for half in range(2):
                    for r in range(4):
                        pool.wait_ge(shaped, 7 + 4 * half + r)
                        rows = pick[32 * r:32 * r + 32]
                        nc.gpsimd.affine_select(out=rows, in_=rows, compare_op=ALU.not_equal, fill=1.0,
                                                base=-4 * r - HEADS * half, pattern=[[-1, 4], [0, P]],
                                                channel_multiplier=1).then_inc(shaped, 1)
                for half in range(2):
                    pool.wait_ge(shaped, 15 + half)
                    keep(spread, ALU.not_equal, 1.0, -HEADS * half, 0, 1, [[-1, HEADS], [0, P // HEADS]]).then_inc(shaped, 1)
                pool.wait_ge(shaped, 17)
                for c in C:
                    nc.gpsimd.memset(vm[c][:], 0.0)
                    nc.gpsimd.memset(vm16[c][:], 0.0)
                    nc.gpsimd.memset(vlin[c][:], 1.0)
                    nc.gpsimd.memset(B["oL1"][c][:], 0.0)
                for i in range(2):
                    nc.gpsimd.memset(rowmax[i][:], 0.0)
                    nc.gpsimd.memset(maxb[i][:], 0.0)

            @block.vector
            def _(dve):
                step = [0]

                def link(ins):
                    step[0] += 1
                    ins.then_inc(setup_step, 1)
                    dve.wait_ge(setup_step, step[0])

                nc.vector.memset(average[:], 1.0 / P)
                nc.vector.memset(average64[:], 1.0 / CTX_DIM)
                nc.vector.memset(ones32[:], 1.0)
                nc.vector.memset(ones_row[:], 1.0)
                for value, t in eps.items():
                    link(nc.vector.memset(t[:], value))
                dve.wait_ge(shaped, 1)
                nc.vector.tensor_scalar(center[:], ident[:], -1.0 / P, None, ALU.add)
                link(nc.vector.tensor_scalar(center64[:], ident[0:CTX_DIM, 0:CTX_DIM], -1.0 / CTX_DIM, None, ALU.add))
                dve.wait_ge(w_small, 16)
                w = W("L2_ffn_W")
                link(nc.vector.tensor_reduce(tcol[:, 0:1], w, AX_X, ALU.add, apply_absolute_value=True))
                nc.vector.tensor_scalar(rel_col[:, 0:3], W("L3_rel_k"), W("L3_attn_bk"), None, ALU.add)
                nc.vector.tensor_scalar(rel_col[:, 3:6], W("L3_rel_v"), W("L3_attn_bv"), None, ALU.add)
                nc.vector.tensor_tensor(rel_row[:], W("L3_rel_v_row", 1), W("L3_attn_bv_row", 1), ALU.add)
                dve.wait_ge(setup_sum, 1)
                link(nc.vector.tensor_scalar(tcol[:, 1:2], psum[0][:, 0:1], 1.0 / P, 1e-5, ALU.mult, ALU.max))
                link(nc.vector.tensor_scalar(tcol[:, 2:3], tcol[:, 1:2], 0.5, None, ALU.mult))
                link(nc.vector.tensor_scalar(tcol[:, 3:4], tcol[:, 1:2], -0.5, None, ALU.mult))
                link(nc.vector.tensor_scalar(tern[:], w, tcol[:, 2:3], tcol[:, 1:2], ALU.is_gt, ALU.mult))
                link(nc.vector.tensor_scalar(tern_neg[:], w, tcol[:, 3:4], tcol[:, 1:2], ALU.is_lt, ALU.mult))
                nc.vector.tensor_tensor(tern[:], tern[:], tern_neg[:], ALU.subtract)

            @block.tensor
            def _(pe):
                pe.wait_ge(setup_step, 4)
                nc.tensor.matmul(psum[0][:, 0:1], average[:], tcol[:, 0:1], start=True, stop=True).then_inc(setup_sum, 1)

        ev = Events(nc, ctx, known)
        made, have = ev.made, ev.have

        def input_of(after, c):
            label, name = after
            return have(label + (str(c) if label.endswith("_loaded") else ""), (name, c))

        def cols(ap, s):
            return ap[:, s * P:(s + 1) * P]

        def blocks(st):
            return range(2 if st["D"] == 16 else 4)

        def per_block(st):
            return 2 if st["D"] == 16 else 4

        def weight(st, n):
            return W(f"{st['name']}_W{n}", CTX_DIM if st["kv"] and n in "kv" else P)

        first_use = {"L0_ffn": "w_l0_ffn", "L1_0": "w_l1_attn", "L1_ffn": "w_l1_ffn", "L2_a1": "w_l2_xattn",
                     "L3_ffn_moe": "w_l3_ffn"}

        with nc.Fori(0, BATCH // GROUP) as g:
            with nc.Block() as block:

                @block.tensor
                def _(pe):
                    def bank(tile, freed_by, kind="flow"):
                        b, before = banks.take(kind, tile, freed_by)
                        if before is not None:
                            pe.wait_ge(*have(*before))
                        return b

                    def norm(st):
                        n, rows, w = st["name"], st.get("rows", P), st.get("cols", TOK)
                        cen, avg = (center, average) if rows == P else (center64, average64)
                        for c in C:
                            pe.wait_ge(*input_of(st["after"], c))
                            b = bank(("centred", n, c), ("normed", (n, c)), f"hold{c}")
                            nc.tensor.matmul(b[0:rows, 0:w], cen[:], B[st["src"]][c][0:rows, 0:w],
                                             start=True, stop=True).then_inc(*made("centred", (n, c)))
                        for c in C:
                            b = bank(("variance", n, c), ("log_var", (n, c)))
                            pe.wait_ge(*have("squared", (n, c)))
                            nc.tensor.matmul(b[0:rows, 0:w], avg[:], B["sq"][c][0:rows, 0:w],
                                             start=True, stop=True).then_inc(*made("variance", (n, c)))

                    def rows_of(st, n, c, src, w, rows, nk, bias_row, width):
                        b = bank(("v_raw", n, c), ("v", (n, c)))
                        for s in S:
                            out = b[0:nk, s * width:(s + 1) * width]
                            ins = nc.tensor.matmul(out, src[0:rows, s * nk:(s + 1) * nk], w, start=True,
                                                   stop=bias_row is None)
                            if bias_row is not None:
                                ins = nc.tensor.matmul(out, ones_row[:, 0:nk], bias_row, start=False, stop=True)
                        ins.then_inc(*made("v_raw", (n, c)))

                    def mha(st):
                        n, nk, D = st["name"], st["nk"], st["D"]
                        J = per_block(st)
                        for c in C:
                            src = B[st["src"]][c]
                            pe.wait_ge(*input_of(st["after"], c))
                            kv, rows = src, P
                            if st["kv"]:
                                kv = B[st["kv"]][c]
                                rows = P if st["kv"] == "hn2" else CTX_DIM
                                pe.wait_ge(*input_of(st["kv_after"], c))
                            if n in first_use and c == 0:
                                pe.wait_ge(*have("w_" + first_use[n], ""))
                            if D == 32:
                                for t in range(4):
                                    b = bank(("q_raw", n, c, t), ("q", (n, c, t)))
                                    nc.tensor.matmul(b[:, 0:TOK], W(n + "_wq")[:, t * P:(t + 1) * P], src[:],
                                                     start=True, stop=True).then_inc(*made("q_raw", (n, c, t)))
                                    b = bank(("k_raw", n, c, t), ("k_copy", (n, c, t)))
                                    nc.tensor.matmul(b[:, 0:PER * nk], W(n + "_wk", rows)[:, t * P:(t + 1) * P],
                                                     kv[:], start=True, stop=True).then_inc(*made("k_raw", (n, c, t)))
                                for s in S:
                                    b = bank(("v_raw", n, c, s), ("v", (n, c, s)))
                                    nc.tensor.matmul(b[0:nk, 0:512], kv[0:rows, s * nk:(s + 1) * nk], W(n + "_wv", rows),
                                                     start=True, stop=True).then_inc(*made("v_raw", (n, c, s)))
                                continue
                            M = 64 if D == 16 else P
                            for which in ("q", "qs", "k", "ks") if st["rope"] else ("q", "k"):
                                b = bank((which + "_raw", n, c),
                                         ("near_prod", (n, c)) if st["rel"] and which == "k" else (which, (n, c)))
                                rhs, N = (kv, PER * nk) if which[0] == "k" else (src, TOK)
                                nc.tensor.matmul(b[0:M, 0:N], weight(st, which), rhs[:],
                                                 start=True, stop=True).then_inc(*made(which + "_raw", (n, c)))
                            if st["rel"]:
                                b = bank(("vT_raw", n, c), ("vT", (n, c)))
                                nc.tensor.matmul(b[:, 0:TOK], weight(st, "v"), src[:],
                                                 start=True, stop=True).then_inc(*made("vT_raw", (n, c)))
                            row = None
                            if st["bias"]:
                                row = rel_row[:] if st["rel"] else W(n + "_bv_row", 1)
                            rows_of(st, n, c, kv, weight(st, "v"), rows, nk, row, P)
                            if st["linear"]:
                                b = bank(("lin_raw", n, c), ("lin_shift", (n, c)))
                                for s in S:
                                    ins = nc.tensor.matmul(cols(b, s), cols(src, s), W(n + "_Wlin"), start=True, stop=True)
                                ins.then_inc(*made("lin_raw", (n, c)))
                        if st["linear"]:
                            for c in C:
                                b = bank(("lin_qT", n, c), ("lin_qTs", (n, c)))
                                pe.wait_ge(*have("lin_ready", (n, c)))
                                for s in S:
                                    ins = nc.tensor.transpose(b[0:64, s * P:(s + 1) * P], qe[c][:, s, :], ident[:])
                                ins.then_inc(*made("lin_qT", (n, c)))
                                b = bank(("lin_sum", n, c), ("lin_ctx", (n, c)))
                                pe.wait_ge(*have("v", (n, c)))
                                for s in S:
                                    ins = nc.tensor.matmul(b[0:64, s * 65:(s + 1) * 65], ke[c][0:64, s, :],
                                                           vlin[c][0:64, s, :], start=True, stop=True)
                                ins.then_inc(*made("lin_sum", (n, c)))
                        if st["rel"]:
                            for c in C:
                                b = bank(("diag_raw", n, c), ("diag", (n, c)))
                                pe.wait_ge(*have("near_prod", (n, c)))
                                for s in S:
                                    for i in range(2):
                                        ins = nc.tensor.matmul(b[:, s * 32 + i * 16:s * 32 + (i + 1) * 16],
                                                               v4[c][:, s, (2 + i) * P:(3 + i) * P], W("head_pick"),
                                                               start=True, stop=True)
                                ins.then_inc(*made("diag_raw", (n, c)))

                        def turn(t):
                            c, s = items[t]
                            b = bank(("max_turned", n, c, s), ("max_row", (n, c, s)))
                            pe.wait_ge(*have("max_split", (n, c, s)))
                            nc.tensor.transpose(b[:].bitcast(BF16)[:, 0:P],
                                                maxb[t % 2][:].rearrange("p g i h -> p (g i h)"), identb[:]).then_inc(*made("max_turned", (n, c, s)))

                        def scores(t):
                            c, s = items[t]
                            for r in blocks(st):
                                g32 = slice(32 * r, 32 * r + 32)
                                b = bank(("scores", n, c, s, r), ("row_max", (n, c, s, r)))
                                if s == 0 and r == 0:
                                    if D == 32:
                                        pe.wait_ge(*have("q", (n, c, 3)))
                                        pe.wait_ge(*have("k_copy", (n, c, 3)))
                                    else:
                                        pe.wait_ge(*have("q", (n, c)))
                                        pe.wait_ge(*have("k_masked", (n, c, J - 1)))
                                if D == 32:
                                    for j in range(4):
                                        ins = nc.tensor.matmul(b[:, j * nk:(j + 1) * nk], q4[c][g32, j, s * P:(s + 1) * P],
                                                               k4[c][g32, j, s * nk:(s + 1) * nk], start=True, stop=True)
                                else:
                                    out = b[:, 0:J * nk]
                                    if st["mask"]:
                                        nc.tensor.matmul(out, identb[:], mask[st["mask"]][:].unsqueeze(1)
                                                         .to_broadcast([P, J, P]), start=True, stop=False)
                                    ins = nc.tensor.matmul(out, B["q"][c][g32, s * P:(s + 1) * P],
                                                           km[c][g32, s, 0:J, 0:nk], start=not st["mask"], stop=True)
                                ins.then_inc(*made("scores", (n, c, s, r)))

                        def shifted(t):
                            c, s = items[t]
                            for r in blocks(st):
                                g32 = slice(32 * r, 32 * r + 32)
                                b = bank(("shifted", n, c, s, r), ("probs", (n, c, s, r)))
                                if r == 0:
                                    pe.wait_ge(*have("max_row", (n, c, s)))
                                    if D != 32 and s == 0:
                                        pe.wait_ge(*have("q_masked", (n, c, J - 1)))
                                if D != 32:
                                    out = b[0:nk, 0:J * P]
                                    if st["mask"]:
                                        nc.tensor.matmul(out, identb[:], maskT[st["mask"]][:].unsqueeze(1)
                                                         .to_broadcast([P, J, P]), start=True, stop=False)
                                    nc.tensor.matmul(out, B["k"][c][g32, s * nk:(s + 1) * nk], qm[c][g32, s, 0:J, :],
                                                     start=not st["mask"], stop=False)
                                for j in range(J):
                                    out = b[0:nk, j * P:(j + 1) * P]
                                    if D == 32:
                                        nc.tensor.matmul(out, k4[c][g32, j, s * nk:(s + 1) * nk],
                                                         q4[c][g32, j, s * P:(s + 1) * P], start=True, stop=False)
                                    ins = nc.tensor.matmul(out, pick[g32, j, 0:nk], maxT[t % 2][g32],
                                                           start=False, stop=(D == 32 or j == J - 1))
                                ins.then_inc(*made("shifted", (n, c, s, r)))
                            if st["rel"]:
                                b = bank(("near_raw", n, c, s), ("near_exp", (n, c, s)))
                                for i in range(2):
                                    out = b[:, i * P:(i + 1) * P]
                                    nc.tensor.matmul(out, W("head_block"), v4[c][:, s, (2 + i) * P:(3 + i) * P],
                                                     start=True, stop=False)
                                    ins = nc.tensor.matmul(out, spread[:], maxT[t % 2][0:32], start=False, stop=True)
                                ins.then_inc(*made("near_raw", (n, c, s)))

                        def attend(t):
                            c, s = items[t]
                            pr = probs[t % 2]
                            if D == 32:
                                b = bank(("sums", n, c, s), ("recip", (n, c, s)))
                                for r in range(4):
                                    pe.wait_ge(*have("probs", (n, c, s, r)))
                                    ins = nc.tensor.matmul(b[32 * r:32 * r + 32, 0:512], ones32[0:nk, :],
                                                           pr[0:nk, r], start=True, stop=True)
                                ins.then_inc(*made("sums", (n, c, s)))
                                b = bank(("attended", n, c, s), ("context", (n, c, s)))
                                pe.wait_ge(*have("v", (n, c, s)))
                                for r in range(4):
                                    if st["post"]:
                                        pe.wait_ge(*have("kept", (n, c, s, r)))
                                    for j in range(4):
                                        h = 4 * j + r
                                        ins = nc.tensor.matmul(b[32 * r:32 * r + 32, j * P:(j + 1) * P],
                                                               v4[c][0:nk, s, h * 32:(h + 1) * 32], pr[0:nk, r, j, :],
                                                               start=True, stop=True)
                                ins.then_inc(*made("attended", (n, c, s)))
                                return
                            b = bank(("attended", n, c, s), ("context", (n, c, s)))
                            pe.wait_ge(*have("v", (n, c)))
                            vals, ones = (vm16, W("ones16")) if D == 16 else (vm, W("ones8"))
                            for r in blocks(st):
                                g32 = slice(32 * r, 32 * r + 32)
                                pe.wait_ge(*have("probs", (n, c, s, r)))
                                for j in range(J):
                                    nc.tensor.matmul(b[g32, 0:P], vals[c][0:nk, s, j, g32], pr[0:nk, r, j, :],
                                                     start=(j == 0), stop=(j == J - 1))
                                for j in range(J):
                                    ins = nc.tensor.matmul(b[g32, P:2 * P], ones[0:nk, j * 32:(j + 1) * 32],
                                                           pr[0:nk, r, j, :], start=(j == 0), stop=(j == J - 1))
                            if st["linear"]:
                                if s == 0:
                                    pe.wait_ge(*have("lin_ctx", (n, c)))
                                    pe.wait_ge(*have("lin_qTs", (n, c)))
                                ins = nc.tensor.matmul(b[64:P, 64:P], lctx[c][:, s, :], qT[c][:, s * P + 64:(s + 1) * P],
                                                       start=True, stop=True)
                            ins.then_inc(*made("attended", (n, c, s)))

                        for t in range(GROUP + 2):
                            if 1 <= t <= GROUP:
                                turn(t - 1)
                            if t < GROUP:
                                scores(t)
                            if 1 <= t <= GROUP:
                                shifted(t - 1)
                            if t >= 2:
                                attend(t - 2)
                        for c in C:
                            b = bank(("proj", n, c), ("residual", (n, c)))
                            pe.wait_ge(*have("context", (n, c, PER - 1)))
                            if D == 32:
                                for j in range(4):
                                    ins = nc.tensor.matmul(b[:, 0:TOK], W(n + "_li1")[:, j * P:(j + 1) * P], q4[c][:, j, :],
                                                           start=(j == 0), stop=(j == 3))
                            else:
                                o = B["oL1" if st["linear"] else "o"][c]
                                ins = nc.tensor.matmul(b[:, 0:TOK], weight(st, "o"), o[:], start=True, stop=True)
                            ins.then_inc(*made("proj", (n, c)))

                    def xattn(st):
                        n = st["name"]
                        for c in C:
                            pe.wait_ge(*input_of(st["after"], c))
                            pe.wait_ge(*input_of(("ctx_loaded", ""), c))
                            b = bank(("q_raw", n, c), ("q", (n, c)))
                            nc.tensor.matmul(b[:, 0:TOK], W(n + "_Wq"), B["x"][c][:], start=True,
                                             stop=True).then_inc(*made("q_raw", (n, c)))
                            b = bank(("k_raw", n, c), ("k", (n, c)))
                            nc.tensor.matmul(b[:, 0:CTOK], W(n + "_Wk", CTX_DIM), B["ctx"][c][:], start=True,
                                             stop=True).then_inc(*made("k_raw", (n, c)))
                            rows_of(st, n, c, B["ctx"][c], W(n + "_Wv", CTX_DIM), CTX_DIM, CTX_LEN,
                                    W(n + "_bv_row", 1), P)
                        for c in C:
                            b = bank(("xscores", n, c), ("xexp", (n, c)))
                            pe.wait_ge(*have("q", (n, c)))
                            pe.wait_ge(*have("k", (n, c)))
                            for s in S:
                                ins = nc.tensor.matmul(b[:, s * CTX_LEN:(s + 1) * CTX_LEN], cols(B["q"][c], s),
                                                       B["k"][c][:, s * CTX_LEN:(s + 1) * CTX_LEN], start=True, stop=True)
                            ins.then_inc(*made("xscores", (n, c)))
                        for c in C:
                            b = bank(("xturned", n, c), ("xprobsT", (n, c)))
                            pe.wait_ge(*have("xprobs", (n, c)))
                            for s in S:
                                ins = nc.tensor.transpose(b[0:CTX_LEN, s * P:(s + 1) * P], px[c][:, s, :], ident[:])
                            ins.then_inc(*made("xturned", (n, c)))
                        for c in C:
                            b = bank(("xout", n, c), ("residual", (n, c)))
                            pe.wait_ge(*have("xprobsT", (n, c)))
                            pe.wait_ge(*have("v", (n, c)))
                            for s in S:
                                ins = nc.tensor.matmul(cols(b, s), vx[c][0:CTX_LEN, s, :], pxT[c][0:CTX_LEN, s, :],
                                                       start=True, stop=True)
                            ins.then_inc(*made("xout", (n, c)))

                    def mlp(st):
                        n = st["name"]
                        for c in C:
                            pe.wait_ge(*input_of(st["after"], c))
                            for m in range(4):
                                b = bank(("hid_raw", n, c, m), ("hid", (n, c, m)))
                                nc.tensor.matmul(b[:, 0:TOK], W(st["W1"])[:, m * P:(m + 1) * P], B[st["src"]][c][:],
                                                 start=True, stop=True).then_inc(*made("hid_raw", (n, c, m)))
                        for c in C:
                            b = bank(("proj", n, c), ("acc_taken" if st["adds"] else "residual", (n, c)))
                            for m in range(4):
                                pe.wait_ge(*have("hid", (n, c, m)))
                                ins = nc.tensor.matmul(b[:, 0:TOK], W(st["W2"])[:, m * P:(m + 1) * P], hid[c][:, 0, m, :],
                                                       start=(m == 0), stop=(m == 3))
                            ins.then_inc(*made("proj", (n, c)))

                    def moe(st):
                        n, base = st["name"], "L3_ffn" if st["name"] == "L3_ffn_moe" else st["name"]
                        for c in C:
                            pe.wait_ge(*input_of(st["after"], c))
                            b = bank(("logits", n, c), ("logits_in", (n, c)))
                            for s in S:
                                out = b[:, s * EXPERTS:(s + 1) * EXPERTS]
                                ins = nc.tensor.matmul(out, cols(B[st["src"]][c], s), W(base + "_Wr"), start=True,
                                                       stop=not st["glu"])
                                if st["glu"]:
                                    ins = nc.tensor.matmul(out, ones_row[:], W(base + "_br_row", 1), start=False, stop=True)
                            ins.then_inc(*made("logits", (n, c)))
                        pe.wait_ge(*have("w_" + st["region"], ""))
                        work_items = [(e, c) for e in range(EXPERTS + st["shared"]) for c in C]

                        def up(e, c):
                            src = B[st["src"]][c][:]
                            if st["glu"]:
                                for m in range(2):
                                    for w, lab, by in (("w1", "gate_raw", "silu"), ("w0", "hid_raw", "gated")):
                                        b = bank((lab, n, e, c, m), (by, (n, e, c, m)))
                                        nc.tensor.matmul(b[:, 0:TOK], W(f"{base}_{w}_{e}")[:, m * P:(m + 1) * P], src,
                                                         start=True, stop=True).then_inc(*made(lab, (n, e, c, m)))
                                return
                            for m in range(4):
                                b = bank(("hid_raw", n, e, c, m), ("hid", (n, e, c, m)))
                                nc.tensor.matmul(b[:, 0:TOK], W(f"{base}_W1_{e}")[:, m * P:(m + 1) * P], src,
                                                 start=True, stop=True).then_inc(*made("hid_raw", (n, e, c, m)))

                        def down(e, c):
                            if not (st["shared"] and e == 0):
                                b = bank(("gate_wide", n, e, c), ("gate_copy", (n, e, c)))
                                pe.wait_ge(*have("gate", (n, c)))
                                for s in S:
                                    one = gate[c][:, s, e - st["shared"]:e - st["shared"] + 1].to_broadcast([P, P])
                                    ins = nc.tensor.matmul(cols(b, s), one, ident[:], start=True, stop=True)
                                ins.then_inc(*made("gate_wide", (n, e, c)))
                            M = 2 if st["glu"] else 4
                            b = bank(("expert", n, e, c), ("expert_taken", (n, e, c)))
                            w = W(f"{base}_w2_{e}" if st["glu"] else f"{base}_W2_{e}")
                            for m in range(M):
                                pe.wait_ge(*have("gated" if st["glu"] else "hid", (n, e, c, m)))
                                ins = nc.tensor.matmul(b[:, 0:TOK], w[:, m * P:(m + 1) * P], hid[c][:, e % 2, m, :],
                                                       start=(m == 0), stop=(m == M - 1))
                            ins.then_inc(*made("expert", (n, e, c)))

                        for i in range(len(work_items) + 1):
                            if i < len(work_items):
                                up(*work_items[i])
                            if i:
                                down(*work_items[i - 1])

                    def linear(st):
                        for c in C:
                            pe.wait_ge(*input_of(st["after"], c))
                            b = bank(("proj", st["name"], c), ("residual", (st["name"], c)))
                            nc.tensor.matmul(b[:, 0:TOK], tern[:], B["x"][c][:], start=True,
                                             stop=True).then_inc(*made("proj", (st["name"], c)))

                    todo = dict(norm=norm, mha=mha, xattn=xattn, mlp=mlp, moe=moe, linear=linear)
                    for st in seq:
                        todo[st["kind"]](st)

                @block.scalar
                def _(act):
                    step = [0]

                    def link(ins):
                        step[0] += 1
                        ins.then_inc(*made("scalar_step", step[0]))
                        act.wait_ge(*have("scalar_step", step[0]))

                    def norm(st):
                        n, rows, w = st["name"], st.get("rows", P), st.get("cols", TOK)
                        for c in C:
                            act.wait_ge(*have("centred", (n, c)))
                            nc.scalar.activation(B["sq"][c][0:rows, 0:w], banks.where(("centred", n, c))[0:rows, 0:w],
                                                 ACT.Square).then_inc(*made("squared", (n, c)))
                        for c in C:
                            rs = B["rs"][c][0:rows, 0:w]
                            act.wait_ge(*have("variance", (n, c)))
                            nc.scalar.activation(rs, banks.where(("variance", n, c))[0:rows, 0:w], ACT.Ln,
                                                 bias=eps[st["eps"]][0:rows]).then_inc(*made("log_var", (n, c)))
                            act.wait_ge(*have("log_var", (n, c)))
                            nc.scalar.activation(rs, rs, ACT.Exp, scale=-0.5).then_inc(*made("rstd", (n, c)))

                    def mha(st):
                        n, nk, D = st["name"], st["nk"], st["D"]
                        J = per_block(st)
                        for c in C:
                            if D == 32:
                                for t in range(4):
                                    act.wait_ge(*have("k_raw", (n, c, t)))
                                    nc.scalar.activation(k4[c][:, t, 0:PER * nk], banks.where(("k_raw", n, c, t))[:, 0:PER * nk],
                                                         ACT.Copy).then_inc(*made("k_copy", (n, c, t)))
                                for s in S:
                                    act.wait_ge(*have("v_raw", (n, c, s)))
                                    nc.scalar.activation(v4[c][0:nk, s, :], banks.where(("v_raw", n, c, s))[0:nk, :],
                                                         ACT.Copy).then_inc(*made("v", (n, c, s)))
                                continue
                            M = 64 if D == 16 else P
                            act.wait_ge(*have("v_raw", (n, c)))
                            raw = banks.where(("v_raw", n, c))[0:nk, 0:TOK].rearrange("p (s f) -> p s f", s=PER)
                            d = D
                            for j in range(J):
                                src = raw[:, :, 0:M].rearrange("p s (r j d) -> p s r j d", j=J, d=d)[:, :, :, j, :]
                                dst = (vm16 if D == 16 else vm)[c][0:nk, :, j, :] \
                                    .rearrange("p s (r j d) -> p s r j d", j=J, d=d)[:, :, :, j, :]
                                ins = nc.scalar.activation(dst, src, ACT.Copy)
                            if st["linear"]:
                                ins = nc.scalar.activation(vlin[c][:, :, 0:64], raw[:, :, 64:P], ACT.Copy)
                            ins.then_inc(*made("v", (n, c)))
                            act.wait_ge(*have("q", (n, c)))
                            sel = W("mask16" if D == 16 else "mask8")
                            for j in range(J):
                                nc.scalar.activation(qm[c][0:M, :, j, :], B["q"][c][0:M, :].rearrange("p (s t) -> p s t", s=PER),
                                                     ACT.Copy, scale=sel[0:M, j:j + 1]).then_inc(*made("q_masked", (n, c, j)))
                        if st["linear"]:
                            for c in C:
                                act.wait_ge(*have("lin_shift", (n, c)))
                                nc.scalar.activation(qe[c][:], qe[c][:], ACT.Exp)
                                nc.scalar.activation(ke[c][:], ke[c][:], ACT.Exp).then_inc(*made("lin_exp", (n, c)))
                        scale = float(D) ** -0.5

                        def soften(t):
                            c, s = items[t]
                            for r in blocks(st):
                                act.wait_ge(*have("shifted", (n, c, s, r)))
                                if r == 0 and t >= 2:
                                    act.wait_ge(*have("attended", (n, *items[t - 2])))
                                nc.scalar.activation(probs[t % 2][0:nk, r, 0:J, :],
                                                     banks.where(("shifted", n, c, s, r))[0:nk, 0:J * P]
                                                     .rearrange("p (j t) -> p j t", j=J),
                                                     ACT.Exp, scale=scale).then_inc(*made("probs", (n, c, s, r)))
                            if st["rel"]:
                                act.wait_ge(*have("near_raw", (n, c, s)))
                                nc.scalar.activation(v4[c][:, s, 0:2 * P], banks.where(("near_raw", n, c, s))[:, 0:2 * P],
                                                     ACT.Exp, scale=scale).then_inc(*made("near_exp", (n, c, s)))

                        def divide(t):
                            c, s = items[t]
                            M, w = (64, P) if D == 16 else (P, 512 if D == 32 else P)
                            out = recip[t % 2][0:M, 0:w]
                            if D == 32:
                                act.wait_ge(*have("sums", (n, c, s)))
                                src = banks.where(("sums", n, c, s))[:, 0:512]
                            elif st["rel"]:
                                act.wait_ge(*have("all_sums", (n, c, s)))
                                src = out
                            else:
                                act.wait_ge(*have("attended", (n, c, s)))
                                src = banks.where(("attended", n, c, s))[0:M, P:2 * P]
                            if t >= 2 and not st["rel"]:
                                act.wait_ge(*have("context", (n, *items[t - 2])))
                            link(nc.scalar.activation(out, src, ACT.Ln))
                            nc.scalar.activation(out, out, ACT.Exp, scale=-1.0).then_inc(*made("recip", (n, c, s)))

                        for t in range(GROUP + 2):
                            if 1 <= t <= GROUP:
                                soften(t - 1)
                            if t >= 2:
                                divide(t - 2)

                    def xattn(st):
                        n = st["name"]
                        for c in C:
                            act.wait_ge(*have("v_raw", (n, c)))
                            nc.scalar.activation(vx[c][0:CTX_LEN], banks.where(("v_raw", n, c))[0:CTX_LEN, 0:TOK]
                                                 .rearrange("p (s f) -> p s f", s=PER), ACT.Copy).then_inc(*made("v", (n, c)))
                        for c in C:
                            act.wait_ge(*have("xmax", (n, c)))
                            for s in S:
                                ins = nc.scalar.activation(px[c][:, s, :],
                                                           banks.where(("xscores", n, c))[:, s * CTX_LEN:(s + 1) * CTX_LEN],
                                                           ACT.Exp, bias=xcol[c][:, 0, s:s + 1])
                            ins.then_inc(*made("xexp", (n, c)))
                        for c in C:
                            act.wait_ge(*have("xturned", (n, c)))
                            nc.scalar.activation(pxT[c][0:CTX_LEN], banks.where(("xturned", n, c))[0:CTX_LEN, 0:TOK]
                                                 .rearrange("p (s f) -> p s f", s=PER),
                                                 ACT.Copy).then_inc(*made("xprobsT", (n, c)))

                    def mlp(st):
                        n = st["name"]
                        for c in C:
                            for m in range(4):
                                act.wait_ge(*have("hid_raw", (n, c, m)))
                                nc.scalar.activation(hid[c][:, 0, m, :], banks.where(("hid_raw", n, c, m))[:, 0:TOK], ACT.Gelu,
                                                     bias=W(st["b1"])[:, m:m + 1]).then_inc(*made("hid", (n, c, m)))

                    def moe(st):
                        n, base = st["name"], "L3_ffn" if st["name"] == "L3_ffn_moe" else st["name"]
                        if st["on"] == "probs":
                            for c in C:
                                act.wait_ge(*have("logits_in", (n, c)))
                                nc.scalar.activation(gtmp[c][:, 0], gtmp[c][:, 0], ACT.Exp).then_inc(*made("router_exp", (n, c)))
                        for c in C:
                            act.wait_ge(*have("gate_shift", (n, c)))
                            nc.scalar.activation(gtmp[c][:, 1], gtmp[c][:, 1], ACT.Exp).then_inc(*made("gate_exp", (n, c)))
                        work_items = [(e, c) for e in range(EXPERTS + st["shared"]) for c in C]
                        for i in range(len(work_items) + 1):
                            if i < len(work_items):
                                e, c = work_items[i]
                                if st["glu"]:
                                    for m in range(2):
                                        act.wait_ge(*have("gate_raw", (n, e, c, m)))
                                        if e:
                                            act.wait_ge(*have("gated", (n, e - 1, c, m)))
                                        nc.scalar.activation(silu[c][:, m, :], banks.where(("gate_raw", n, e, c, m))[:, 0:TOK],
                                                             st["act"], bias=W(base + "_b1")[:, 2 * e + m:2 * e + m + 1]
                                                             ).then_inc(*made("silu", (n, e, c, m)))
                                else:
                                    for m in range(4):
                                        act.wait_ge(*have("hid_raw", (n, e, c, m)))
                                        nc.scalar.activation(hid[c][:, e % 2, m, :], banks.where(("hid_raw", n, e, c, m))[:, 0:TOK],
                                                             st["act"], bias=W(base + "_b1")[:, 4 * e + m:4 * e + m + 1]
                                                             ).then_inc(*made("hid", (n, e, c, m)))
                            if i:
                                e, c = work_items[i - 1]
                                if st["shared"] and e == 0:
                                    continue
                                act.wait_ge(*have("gate_wide", (n, e, c)))
                                if e - st["shared"] > 0:
                                    act.wait_ge(*have("expert_taken", (n, e - 1, c)))
                                nc.scalar.activation(gb[c][:], banks.where(("gate_wide", n, e, c))[:, 0:TOK],
                                                     ACT.Copy).then_inc(*made("gate_copy", (n, e, c)))

                    todo = dict(norm=norm, mha=mha, xattn=xattn, mlp=mlp, moe=moe, linear=lambda st: None)
                    for st in seq:
                        todo[st["kind"]](st)

                @block.vector
                def _(dve):
                    step = [0]

                    def link(ins):
                        step[0] += 1
                        ins.then_inc(*made("vector_step", step[0]))
                        dve.wait_ge(*have("vector_step", step[0]))

                    V = nc.vector

                    def norm(st):
                        n, rows, w = st["name"], st.get("rows", P), st.get("cols", TOK)
                        for c in C:
                            cen = banks.where(("centred", n, c))[0:rows, 0:w]
                            rs = B["rs"][c][0:rows, 0:w]
                            dst = B[st["dst"]][c][0:rows, 0:w]
                            dve.wait_ge(*have("rstd", (n, c)))
                            if st["g"] is None:
                                V.tensor_tensor(dst, cen, rs, ALU.mult).then_inc(*made("normed", (n, c)))
                                continue
                            gain, shift = W(st["g"] + "_g", rows), W(st["g"] + "_b", rows)
                            if "dst2" in st:
                                dst2 = B[st["dst2"]][c][0:rows, 0:w]
                                link(V.tensor_tensor(rs, cen, rs, ALU.mult))
                                V.tensor_scalar(dst2, rs, W(st["g2"] + "_g", rows), W(st["g2"] + "_b", rows), ALU.mult, ALU.add)
                                V.tensor_scalar(dst, rs, gain, shift, ALU.mult, ALU.add).then_inc(*made("normed", (n, c)))
                                continue
                            link(V.scalar_tensor_tensor(dst, cen, gain, rs, ALU.mult, ALU.mult))
                            if st["add"]:
                                V.scalar_tensor_tensor(dst, dst, shift, B[st["add"]][c][:], ALU.add,
                                                       ALU.add).then_inc(*made("normed", (n, c)))
                            else:
                                V.tensor_scalar(dst, dst, shift, None, ALU.add).then_inc(*made("normed", (n, c)))

                    def mha(st):
                        n, nk, D = st["name"], st["nk"], st["D"]
                        J = per_block(st)
                        M = 64 if D == 16 else P
                        for c in C:
                            if D == 32:
                                for t in range(4):
                                    dve.wait_ge(*have("q_raw", (n, c, t)))
                                    V.tensor_copy(q4[c][:, t, :], banks.where(("q_raw", n, c, t))[:, 0:TOK]
                                                  ).then_inc(*made("q", (n, c, t)))
                                continue
                            if st["rope"]:
                                for a in "qk":
                                    out = B[a][c][:].rearrange("p (s t) -> p s t", s=PER)
                                    other = part[c][:].rearrange("p (s t) -> p s t", s=PER)
                                    wide = [W("rope_" + f).unsqueeze(1).to_broadcast([P, PER, P]) for f in ("cos", "sin")]
                                    raw = [banks.where((a + f + "_raw", n, c))[:, 0:TOK].rearrange("p (s t) -> p s t", s=PER)
                                           for f in ("", "s")]
                                    dve.wait_ge(*have(a + "_raw", (n, c)))
                                    link(V.tensor_tensor(out, raw[0], wide[0], ALU.mult))
                                    dve.wait_ge(*have(a + "s_raw", (n, c)))
                                    V.tensor_tensor(other, raw[1], wide[1], ALU.mult).then_inc(*made(a + "s", (n, c)))
                                    dve.wait_ge(*have(a + "s", (n, c)))
                                    V.tensor_tensor(out, out, other, ALU.add).then_inc(*made(a, (n, c)))
                                    dve.wait_ge(*have(a, (n, c)))
                            else:
                                for a in "qk":
                                    N = PER * nk if a == "k" else TOK
                                    dve.wait_ge(*have(a + "_raw", (n, c)))
                                    raw = banks.where((a + "_raw", n, c))[0:M, 0:N]
                                    out = B[a][c][0:M, 0:N]
                                    if st["rel"] and a == "k":
                                        V.tensor_scalar(out, raw, rel_col[:, 0:1], None, ALU.add).then_inc(*made(a, (n, c)))
                                    elif st["bias"]:
                                        V.tensor_scalar(out, raw, W(f"{n}_b{a}"), None, ALU.add).then_inc(*made(a, (n, c)))
                                    else:
                                        V.tensor_copy(out, raw).then_inc(*made(a, (n, c)))
                            if st["rel"]:
                                raw = banks.where(("k_raw", n, c))[:, 0:TOK].rearrange("p (s t) -> p s t", s=PER)
                                qv = B["q"][c][:].rearrange("p (s t) -> p s t", s=PER)
                                dve.wait_ge(*have("q", (n, c)))
                                link(V.scalar_tensor_tensor(v4[c][:, :, 2 * P:3 * P], raw, rel_col[:, 2:3], qv, ALU.add, ALU.mult))
                                V.tensor_copy(v4[c][:, :, 3 * P:3 * P + 1], v4[c][:, :, 2 * P:2 * P + 1])
                                V.scalar_tensor_tensor(v4[c][:, :, 3 * P + 1:4 * P], raw[:, :, 0:P - 1], rel_col[:, 1:2],
                                                       qv[:, :, 1:P], ALU.add, ALU.mult).then_inc(*made("near_prod", (n, c)))
                                dve.wait_ge(*have("vT_raw", (n, c)))
                                raw = banks.where(("vT_raw", n, c))[:, 0:TOK]
                                V.tensor_scalar(B["hn"][c][:], raw, rel_col[:, 4:5], None, ALU.add)
                                V.tensor_scalar(B["hn2"][c][:], raw, rel_col[:, 5:6], None, ALU.add).then_inc(*made("vT", (n, c)))
                            if st["linear"]:
                                raw = banks.where(("lin_raw", n, c))[:, 0:TOK].rearrange("p (s f) -> p s f", s=PER)
                                dve.wait_ge(*have("lin_raw", (n, c)))
                                top = lcol[c][:, 0:PER * 4].rearrange("p (s h) -> p s h", s=PER)
                                link(V.tensor_reduce(top, raw[:, :, 0:64].rearrange("p s (h d) -> p s h d", h=4), AX_X, ALU.max))
                                V.tensor_scalar(ke[c][:], raw[:, :, 64:P], 0.0, None, ALU.min)
                                V.tensor_scalar(kx[c][:], raw[:, :, 64:P], 0.0, None, ALU.max)
                                for s in S:
                                    ins = V.tensor_tensor(qe[c][:, s, :].rearrange("p (h d) -> p h d", h=4),
                                                          raw[:, s, 0:64].rearrange("p (h d) -> p h d", h=4),
                                                          top[:, s, :].unsqueeze(2).to_broadcast([P, 4, 16]), ALU.subtract)
                                ins.then_inc(*made("lin_shift", (n, c)))
                        if st["rel"]:
                            for c in C:
                                dve.wait_ge(*have("diag_raw", (n, c)))
                                V.tensor_copy(diag[c][:], banks.where(("diag_raw", n, c))[:, 0:PER * 32]
                                              .rearrange("p (s i) -> p s i", s=PER)).then_inc(*made("diag", (n, c)))
                        if st["linear"]:
                            for c in C:
                                total = lcol[c][:, 4 * PER:8 * PER].rearrange("p (s h) -> p s h", s=PER)
                                inv = lcol[c][:, 8 * PER:12 * PER].rearrange("p (s h) -> p s h", s=PER)
                                dve.wait_ge(*have("lin_exp", (n, c)))
                                link(V.tensor_reduce(total, qe[c][:].rearrange("p s (h d) -> p s h d", h=4), AX_X, ALU.add))
                                link(V.reciprocal(inv, total))
                                for s in S:
                                    qv = qe[c][:, s, :].rearrange("p (h d) -> p h d", h=4)
                                    V.tensor_tensor(qv, qv, inv[:, s, :].unsqueeze(2).to_broadcast([P, 4, 16]), ALU.mult)
                                V.tensor_tensor(ke[c][:], ke[c][:], kx[c][:], ALU.add).then_inc(*made("lin_ready", (n, c)))
                            for c in C:
                                dve.wait_ge(*have("lin_qT", (n, c)))
                                V.tensor_copy(qT[c][:], banks.where(("lin_qT", n, c))[0:64, 0:TOK]).then_inc(*made("lin_qTs", (n, c)))
                                raw = banks.where(("lin_sum", n, c))[0:64, 0:PER * 65].rearrange("p (s f) -> p s f", s=PER)
                                den = lcol[c][0:64, 12 * PER:13 * PER].rearrange("p (s a) -> p s a", a=1)
                                dve.wait_ge(*have("lin_sum", (n, c)))
                                link(V.tensor_scalar(den, raw[:, :, 64:65], 1e-6, None, ALU.add))
                                link(V.reciprocal(den, den))
                                link(V.tensor_tensor(lctx[c][:], raw[:, :, 0:64], den.to_broadcast([64, PER, 64]), ALU.mult))
                                V.tensor_tensor(lctx[c][:], lctx[c][:], W("lin_block", 64).unsqueeze(1)
                                                .to_broadcast([64, PER, 64]), ALU.mult).then_inc(*made("lin_ctx", (n, c)))

                        def max_row(t):
                            c, s = items[t]
                            dve.wait_ge(*have("max_turned", (n, c, s)))
                            if t >= 2:
                                if st["rel"]:
                                    dve.wait_ge(*have("near_raw", (n, *items[t - 2])))
                                else:
                                    dve.wait_ge(*have("shifted", (n, *items[t - 2], blocks(st)[-1])))
                            V.tensor_copy(maxT[t % 2][:], banks.where(("max_turned", n, c, s))[:].bitcast(BF16)[:, 0:P]
                                          ).then_inc(*made("max_row", (n, c, s)))

                        def row_max(t):
                            c, s = items[t]
                            m = rowmax[t % 2]
                            for r in blocks(st):
                                dve.wait_ge(*have("scores", (n, c, s, r)))
                                V.tensor_reduce(m[:, 4 * r:4 * r + J], banks.where(("scores", n, c, s, r))[:, 0:J * nk]
                                                .rearrange("p (j k) -> p j k", j=J), AX_X, ALU.max,
                                                negate=True).then_inc(*made("row_max", (n, c, s, r)))
                            dve.wait_ge(*have("row_max", (n, c, s, blocks(st)[-1])))
                            if st["rel"]:
                                for i in range(2):
                                    link(V.scalar_tensor_tensor(m[:], diag[c][:, s, i * 16:(i + 1) * 16], -1.0, m[:],
                                                                ALU.mult, ALU.min))
                            copies = m[:].unsqueeze(1).to_broadcast([P, 4, HEADS])
                            upper, lower = maxb[t % 2][:, :, 0, :], maxb[t % 2][:, :, 1, :]
                            link(V.tensor_copy(upper, copies))
                            V.tensor_tensor(lower, copies, upper, ALU.subtract).then_inc(*made("max_split", (n, c, s)))

                        def context(t):
                            c, s = items[t]
                            b = banks.where(("attended", n, c, s))
                            rc = recip[t % 2]
                            if st["rel"]:
                                own, before = v4[c][:, s, 0:P], v4[c][:, s, P:2 * P]
                                v_own, v_before = cols(B["hn2"][c], s), cols(B["hn"][c], s)
                                t1, t2 = v4[c][:, s, 2 * P:3 * P], v4[c][:, s, 3 * P:4 * P]
                                dve.wait_ge(*have("near_exp", (n, c, s)))
                                link(V.memset(v4[c][:, s, P:P + 1], 0.0))
                                V.tensor_tensor(t1, own, v_own, ALU.mult)
                                link(V.tensor_tensor(t2[:, 1:P], before[:, 1:P], v_before[:, 0:P - 1], ALU.mult))
                                V.tensor_tensor(t1[:, 1:P], t1[:, 1:P], t2[:, 1:P], ALU.add)
                                link(V.tensor_tensor(rc[:, 0:P], own, before, ALU.add))
                                dve.wait_ge(*have("attended", (n, c, s)))
                                V.tensor_tensor(rc[:, 0:P], rc[:, 0:P], b[:, P:2 * P], ALU.add).then_inc(*made("all_sums", (n, c, s)))
                                link(V.tensor_tensor(t1, t1, b[:, 0:P], ALU.add))
                                dve.wait_ge(*have("recip", (n, c, s)))
                                V.tensor_tensor(cols(B["o"][c], s), t1, rc[:, 0:P], ALU.mult).then_inc(*made("context", (n, c, s)))
                                return
                            dve.wait_ge(*have("recip", (n, c, s)))
                            if D == 32:
                                dve.wait_ge(*have("attended", (n, c, s)))
                                V.tensor_tensor(q4[c][:, :, s * P:(s + 1) * P], b[:].rearrange("p (t n) -> p t n", t=4),
                                                rc[:].rearrange("p (t n) -> p t n", t=4), ALU.mult
                                                ).then_inc(*made("context", (n, c, s)))
                            elif st["linear"]:
                                o = B["oL1"][c]
                                V.tensor_copy(o[64:P, s * P + 64:(s + 1) * P], b[64:P, 64:P])
                                V.tensor_tensor(cols(o, s)[0:64], b[0:64, 0:P], rc[0:64, 0:P], ALU.mult
                                                ).then_inc(*made("context", (n, c, s)))
                            else:
                                V.tensor_tensor(cols(B["o"][c], s), b[:, 0:P], rc[:, 0:P], ALU.mult
                                                ).then_inc(*made("context", (n, c, s)))

                        for t in range(GROUP + 2):
                            if 1 <= t <= GROUP:
                                max_row(t - 1)
                            if t < GROUP:
                                row_max(t)
                            if t >= 2:
                                context(t - 2)
                        for c in C:
                            b = banks.where(("proj", n, c))[:, 0:TOK]
                            dve.wait_ge(*have("proj", (n, c)))
                            if st["bo"]:
                                V.scalar_tensor_tensor(B[st["dst"]][c][:], b, W(st["bo"]), B[st["res"]][c][:], ALU.add,
                                                       ALU.add).then_inc(*made("residual", (n, c)))
                            else:
                                V.tensor_tensor(B[st["dst"]][c][:], b, B[st["res"]][c][:], ALU.add
                                                ).then_inc(*made("residual", (n, c)))

                    def xattn(st):
                        n = st["name"]
                        for c in C:
                            for a, N in (("q", TOK), ("k", CTOK)):
                                dve.wait_ge(*have(a + "_raw", (n, c)))
                                V.tensor_scalar(B[a][c][:, 0:N], banks.where((a + "_raw", n, c))[:, 0:N], W(f"{n}_b{a}"), None,
                                                ALU.add).then_inc(*made(a, (n, c)))
                        for c in C:
                            dve.wait_ge(*have("xscores", (n, c)))
                            V.tensor_reduce(xcol[c][:, 0, :], banks.where(("xscores", n, c))[:, 0:CTOK]
                                            .rearrange("p (s k) -> p s k", s=PER), AX_X, ALU.max, negate=True
                                            ).then_inc(*made("xmax", (n, c)))
                        for c in C:
                            dve.wait_ge(*have("xexp", (n, c)))
                            link(V.tensor_reduce(xcol[c][:, 1, :], px[c], AX_X, ALU.add))
                            link(V.reciprocal(xcol[c][:, 2, :], xcol[c][:, 1, :]))
                            V.tensor_tensor(px[c], px[c], xcol[c][:, 2, :].unsqueeze(2).to_broadcast([P, PER, CTX_LEN]), ALU.mult
                                            ).then_inc(*made("xprobs", (n, c)))
                        for c in C:
                            dve.wait_ge(*have("xout", (n, c)))
                            V.tensor_tensor(B["u"][c][:], banks.where(("xout", n, c))[:, 0:TOK], B["x"][c][:], ALU.add
                                            ).then_inc(*made("residual", (n, c)))

                    def mlp(st):
                        n = st["name"]
                        for c in C:
                            b = banks.where(("proj", n, c))[:, 0:TOK]
                            dst = B[st["dst"]][c][:]
                            dve.wait_ge(*have("proj", (n, c)))
                            if not st["adds"]:
                                V.scalar_tensor_tensor(dst, b, W(st["b2"]), B[st["res"]][c][:], ALU.add, ALU.add
                                                       ).then_inc(*made("residual", (n, c)))
                                continue
                            V.scalar_tensor_tensor(part[c][:], b, W(st["b2"]), B[st["res"]][c][:], ALU.add, ALU.add
                                                   ).then_inc(*made("acc_taken", (n, c)))
                            dve.wait_ge(*have("acc_taken", (n, c)))
                            if len(st["adds"]) == 2:
                                link(V.tensor_tensor(part[c][:], part[c][:], B[st["adds"][1]][c][:], ALU.add))
                            V.tensor_tensor(dst, part[c][:], B[st["adds"][0]][c][:], ALU.add).then_inc(*made("residual", (n, c)))

                    def moe(st):
                        n, base = st["name"], "L3_ffn" if st["name"] == "L3_ffn_moe" else st["name"]
                        wide = [P, PER, EXPERTS]
                        desc = W("descending").unsqueeze(1).to_broadcast(wide)

                        def bc(col):
                            return col.unsqueeze(2).to_broadcast(wide)
                        for c in C:
                            T = [gtmp[c][:, i] for i in range(8)]
                            k = [gcol[c][:, i] for i in range(8)]
                            raw = banks.where(("logits", n, c))[:, 0:PER * EXPERTS].rearrange("p (s e) -> p s e", s=PER)
                            dve.wait_ge(*have("logits", (n, c)))
                            if st["on"] == "probs":
                                link(V.tensor_reduce(k[6], raw, AX_X, ALU.max))
                                V.tensor_tensor(T[0], raw, bc(k[6]), ALU.subtract).then_inc(*made("logits_in", (n, c)))
                            else:
                                V.tensor_copy(T[0], raw).then_inc(*made("logits_in", (n, c)))
                                dve.wait_ge(*have("logits_in", (n, c)))
                        for c in C:
                            T = [gtmp[c][:, i] for i in range(8)]
                            k = [gcol[c][:, i] for i in range(8)]
                            if st["on"] == "probs":
                                dve.wait_ge(*have("router_exp", (n, c)))
                                link(V.tensor_reduce(k[6], T[0], AX_X, ALU.add))
                                link(V.reciprocal(k[7], k[6]))
                                link(V.tensor_tensor(T[0], T[0], bc(k[7]), ALU.mult))
                            v = T[0]
                            for i in range(2):
                                link(V.tensor_reduce(k[3 * i], v, AX_X, ALU.max))
                                if i == 0:
                                    V.tensor_tensor(T[1], v, bc(k[0]), ALU.subtract).then_inc(*made("gate_shift", (n, c)))
                                link(V.tensor_tensor(T[2], v, bc(k[3 * i]), ALU.is_ge))
                                link(V.tensor_tensor(T[2], T[2], desc, ALU.mult))
                                link(V.tensor_reduce(k[3 * i + 1], T[2], AX_X, ALU.max))
                                link(V.tensor_tensor(T[3 + i], T[2], bc(k[3 * i + 1]), ALU.is_equal))
                                if i == 0:
                                    link(V.scalar_tensor_tensor(T[5], T[3], MASKED, T[0], ALU.mult, ALU.add))
                                    v = T[5]
                            link(V.tensor_tensor(T[6], T[3], T[4], ALU.add))
                            dve.wait_ge(*have("gate_exp", (n, c)))
                            link(V.tensor_tensor(T[6], T[6], T[1], ALU.mult))
                            link(V.tensor_reduce(k[2], T[6], AX_X, ALU.add))
                            link(V.reciprocal(k[5], k[2]))
                            V.tensor_tensor(gate[c][:], T[6], bc(k[5]), ALU.mult).then_inc(*made("gate", (n, c)))
                        E = EXPERTS + st["shared"]
                        work_items = [(e, c) for e in range(E) for c in C]

                        def gated(e, c):
                            for m in range(2):
                                b = banks.where(("hid_raw", n, e, c, m))[:, 0:TOK]
                                dve.wait_ge(*have("silu", (n, e, c, m)))
                                dve.wait_ge(*have("hid_raw", (n, e, c, m)))
                                V.scalar_tensor_tensor(hid[c][:, e % 2, m, :], b, W(base + "_b0")[:, 2 * e + m:2 * e + m + 1],
                                                       silu[c][:, m, :], ALU.add, ALU.mult).then_inc(*made("gated", (n, e, c, m)))

                        def combine(e, c):
                            b = banks.where(("expert", n, e, c))[:, 0:TOK]
                            bias = W(base + "_b2")[:, e:e + 1]
                            u, src = B["u"][c][:], B[st["src"]][c][:]
                            dve.wait_ge(*have("expert", (n, e, c)))
                            if st["shared"] and e == 0:
                                V.scalar_tensor_tensor(u, b, bias, src, ALU.add, ALU.add).then_inc(*made("expert_taken", (n, e, c)))
                                return
                            dve.wait_ge(*have("gate_copy", (n, e, c)))
                            V.scalar_tensor_tensor(part[c][:], b, bias, gb[c][:], ALU.add, ALU.mult
                                                   ).then_inc(*made("expert_taken", (n, e, c)))
                            dve.wait_ge(*have("expert_taken", (n, e, c)))
                            if e == E - 1:
                                V.tensor_tensor(u, u, part[c][:], ALU.add).then_inc(*made("residual", (n, c)))
                            else:
                                link(V.tensor_tensor(u, src if e == 0 else u, part[c][:], ALU.add))

                        for i in range(len(work_items) + 1):
                            if i < len(work_items) and st["glu"]:
                                gated(*work_items[i])
                            if i:
                                combine(*work_items[i - 1])

                    def linear(st):
                        for c in C:
                            dve.wait_ge(*have("proj", (st["name"], c)))
                            V.tensor_tensor(B["u"][c][:], banks.where(("proj", st["name"], c))[:, 0:TOK], B["x"][c][:], ALU.add
                                            ).then_inc(*made("residual", (st["name"], c)))

                    todo = dict(norm=norm, mha=mha, xattn=xattn, mlp=mlp, moe=moe, linear=linear)
                    for st in seq:
                        todo[st["kind"]](st)

                @block.gpsimd
                def _(pool):
                    def mha(st):
                        n, nk, D = st["name"], st["nk"], st["D"]
                        J = per_block(st)
                        M = 64 if D == 16 else P
                        if D != 32:
                            sel = W("mask16" if D == 16 else "mask8")
                            for c in C:
                                pool.wait_ge(*have("k", (n, c)))
                                kv = B["k"][c][0:M, 0:PER * nk].rearrange("p (s t) -> p s t", s=PER)
                                for j in range(J):
                                    nc.gpsimd.tensor_scalar(km[c][0:M, :, j, 0:nk], kv, sel[0:M, j:j + 1], None, ALU.mult
                                                            ).then_inc(*made("k_masked", (n, c, j)))
                        if st["post"]:
                            for t, (c, s) in enumerate(items):
                                pool.wait_ge(*have("sums", (n, c, s)))
                                for r in range(4):
                                    nc.gpsimd.tensor_tensor(probs[t % 2][:, r], probs[t % 2][:, r],
                                                            after_mask[:].unsqueeze(1).to_broadcast([P, 4, P]), ALU.mult
                                                            ).then_inc(*made("kept", (n, c, s, r)))

                    for st in seq:
                        if st["kind"] == "mha":
                            mha(st)

                @block.sync
                def _(sp):
                    for c in C:
                        sp.dma_start(B["x"][c][:], io["x"][:, bass.ds(g * (GROUP * P) + c * TOK, TOK)]
                                     ).then_inc(*made(f"x_loaded{c}", ("", c), 16))
                        sp.dma_start(B["ctx"][c][:], io["ctx"][:, bass.ds(g * (GROUP * CTX_LEN) + c * CTOK, CTOK)]
                                     ).then_inc(*made(f"ctx_loaded{c}", ("", c), 16))
                    for array, free in (("w_l0_ffn", None), ("w_l1_attn", None), ("w_l1_ffn", "L0_ffn"),
                                        ("w_l2_xattn", "L1_3_mlp"), ("w_l3_ffn", "L1_ffn")):
                        if free is not None and free not in [st["name"] for st in seq]:
                            continue
                        if free is not None:
                            for c in C:
                                sp.wait_ge(*have("residual", (free, c)))
                        sp.dma_start(region[REGION[array]][:, 0:io[array].shape[1]], io[array]
                                     ).then_inc(*made("w_" + array, "", 16))
                    for c in C:
                        sp.wait_ge(*have(end[0], (end[1], c)))
                        sp.dma_start(io["out"][:, bass.ds(g * (GROUP * P) + c * TOK, TOK)], B["x"][c][:]
                                     ).then_inc(*made("stored", c, 16))
                    sp.wait_ge(*have("stored", CHAINS - 1))

            nums = sorted(s.num for s in ev.sems.values())
            if known:
                assert nums == list(range(nums[0], nums[0] + len(nums)))
                nc.all_engine_barrier(sems_to_clear=range(nums[0], nums[-1] + 1))
        return ev


def pack(entries, parts):
    import numpy as np
    at, n = columns(entries)
    out = np.zeros((P, n), np.float32)
    for name, (o, w) in at.items():
        a = parts[name]
        assert a.shape[1] == w, (name, a.shape, w)
        out[:a.shape[0], o:o + w] = a
    return out


def lay_out(i):
    import numpy as np
    p = {}

    def col(v):
        return v.reshape(-1, P).T

    def col64(v):
        return v.reshape(CTX_DIM, 1)

    def deep(w):
        return w.reshape(-1, P, w.shape[-1]).transpose(1, 0, 2).reshape(P, -1)

    swap = np.arange(P) ^ 1
    for n in "qkvo":
        p["L0_attn_W" + n] = i["L0_attn_W" + n]
        p["L2_attn_W" + n] = i["L2_attn_W" + n]
        p["L3_attn_W" + n] = i["L3_attn_W_" + n]
        p["L3_ffn_W" + n] = i["L3_ffn_W" + n]
        p["L2_attn_b" + n] = col(i["L2_attn_b" + n])
        p["L3_attn_b" + n] = col(i["L3_attn_b_" + n])
    p["L0_attn_Wqs"], p["L0_attn_Wks"] = i["L0_attn_Wq"][:, swap], i["L0_attn_Wk"][:, swap]
    p["L2_attn_bv_row"], p["L3_attn_bv_row"] = i["L2_attn_bv"][None], i["L3_attn_b_v"][None]
    for lv in ("L0", "L3"):
        a = lv + "_xattn_"
        for n in "qkv":
            p[a + "W" + n] = i[a + "W" + n]
        p[a + "bq"], p[a + "bk"], p[a + "bv_row"] = col(i[a + "bq"]), col(i[a + "bk"]), i[a + "bv"][None]
    p["L0_ffn_Wr"] = i["L0_ffn_Wr"]
    p["L0_ffn_b1"] = np.concatenate([col(i["L0_ffn_bfc_s"])] + [col(b) for b in i["L0_ffn_bfc"]], 1)
    p["L0_ffn_b2"] = np.concatenate([col(i["L0_ffn_bproj_s"])] + [col(b) for b in i["L0_ffn_bproj"]], 1)
    for e in range(EXPERTS + 1):
        p[f"L0_ffn_W1_{e}"] = i["L0_ffn_Wfc"][e - 1] if e else i["L0_ffn_Wfc_s"]
        p[f"L0_ffn_W2_{e}"] = deep(i["L0_ffn_Wproj"][e - 1] if e else i["L0_ffn_Wproj_s"])
    for d in range(DEPTH):
        n = f"L1_{d}_"
        for k in ("bo", "ln1_g", "ln1_b", "ln2_g", "ln2_b", "b1", "b2"):
            p[n + k] = col(i["L1_attn_" + k][d])
        wq, wk = i["L1_attn_Wq"][d], i["L1_attn_Wk"][d]
        p[n + "Wq"], p[n + "Wk"] = wq[:, :64], wk[:, :64]
        p[n + "Wlin"] = np.concatenate([wq[:, 64:], wk[:, 64:]], 1)
        p[n + "Wv"], p[n + "Wo"] = i["L1_attn_Wv"][d], i["L1_attn_Wo"][d]
        p[n + "W1"], p[n + "W2"] = i["L1_attn_W1"][d], deep(i["L1_attn_W2"][d])
    p["L1_xattn_Wq"], p["L1_xattn_Wo"] = i["L1_xattn_Wq"].T, i["L1_xattn_Wo"].T
    p["L1_xattn_Wk"], p["L1_xattn_Wv"] = i["L1_xattn_Wkv"][:P].T, i["L1_xattn_Wkv"][P:].T
    p["L1_ffn_Wr"], p["L1_ffn_br_row"] = i["L1_ffn_gate_w"].T, i["L1_ffn_gate_b"][None]
    for k in ("b0", "b1", "b2"):
        p["L1_ffn_" + k] = np.concatenate([col(b) for b in i["L1_ffn_" + k]], 1)
    for e in range(EXPERTS):
        p[f"L1_ffn_w0_{e}"], p[f"L1_ffn_w1_{e}"] = i["L1_ffn_w0"][e].T, i["L1_ffn_w1"][e].T
        p[f"L1_ffn_w2_{e}"] = deep(i["L1_ffn_w2"][e].T)
    for k in ("ln1_g", "ln1_b", "ln2_g", "ln2_b"):
        p["L2_" + k] = col(i["L2_xattn_" + k])
        p["L3_ffn_" + k] = col(i["L3_ffn_" + k])
    for a, src in (("L2_a1_", "L2_xattn_a1_"), ("L2_a2_", "L2_xattn_a2_")):
        for k in ("lnx_g", "lnx_b", "lny_g", "lny_b", "ln3_g", "ln3_b", "li1_b", "li2_b", "li3_b"):
            v = i[src + k]
            p[a + k] = col64(v) if v.shape[0] == CTX_DIM else col(v)
        for k in ("wq", "wk", "wv"):
            w = i[src + k]
            p[a + k] = w.transpose(1, 0, 2).reshape(w.shape[1], -1)
        p[a + "li1"], p[a + "li2"], p[a + "li3"] = deep(i[src + "li1_w"]), i[src + "li2_w"], deep(i[src + "li3_w"])
    p["L2_ffn_W"] = i["L2_ffn_weight"].T
    p["L3_rel_k"] = np.tile(i["L3_attn_rel_k_table"][:3].T, (HEADS, 1))
    p["L3_rel_v"] = np.tile(i["L3_attn_rel_v_table"][:3].T, (HEADS, 1))
    p["L3_rel_v_row"] = np.tile(i["L3_attn_rel_v_table"][0], HEADS)[None]
    p["L3_ffn_bo"], p["L3_ffn_Wr"] = col(i["L3_ffn_bo"]), i["L3_ffn_Wr"]
    p["L3_ffn_b1"] = np.concatenate([col(b) for b in i["L3_ffn_be1"]], 1)
    p["L3_ffn_b2"] = np.concatenate([col(b) for b in i["L3_ffn_be2"]], 1)
    for e in range(EXPERTS):
        p[f"L3_ffn_W1_{e}"], p[f"L3_ffn_W2_{e}"] = i["L3_ffn_We1"][e], deep(i["L3_ffn_We2"][e])
    return p


def shape_constants():
    import numpy as np
    D = P // HEADS
    f = np.arange(P)
    inv = (1.0 / np.float32(10000.0) ** (np.arange(0, D, 2, dtype=np.float32) / np.float32(D))).astype(np.float32)
    theta = inv[(f % D) // 2][:, None] * np.arange(P, dtype=np.float32)[None]
    sign = np.where(f % 2 == 0, -1.0, 1.0)[:, None]
    k = {"rope_cos": np.cos(theta), "rope_sin": np.sin(theta) * sign}
    k["head_block"] = (f[:, None] // D == f[None] // D)
    k["head_pick"] = (f[:, None] // D == np.arange(HEADS)[None])
    c = np.arange(32)
    k["ones8"] = np.tile(np.concatenate([c // 8 == j for j in range(4)])[None], (P, 1))
    k["ones16"] = np.tile(np.concatenate([c // 16 == j for j in range(2)])[None], (P, 1))
    k["mask8"] = (f[:, None] // 8) % 4 == np.arange(4)[None]
    k["mask16"] = (f[:, None] // 16) % 2 == np.arange(2)[None]
    g = np.arange(64)
    k["lin_block"] = (g[:, None] // 16 == g[None] // 16)
    k["descending"] = np.tile(np.arange(EXPERTS, 0, -1)[None], (P, 1))
    return k


def kernel(**inputs):
    import numpy as np
    import concourse.bacc as bacc
    from concourse.bass_utils import run_bass_kernel_spmd

    i = {k: np.asarray(v) for k, v in inputs.items()}
    parts = lay_out(i) | shape_constants()
    arrays = {
        "x": np.ascontiguousarray(i["x"].transpose(2, 0, 1).reshape(P, BATCH * P)),
        "ctx": np.ascontiguousarray(i["ctx_512"].transpose(2, 0, 1).reshape(CTX_DIM, BATCH * CTX_LEN)),
        "w_small": pack(small_entries(), parts),
    }
    for name, entries in big_entries().items():
        arrays[name] = pack(entries, parts)

    def program(known):
        nc = bacc.Bacc("TRN2", target_bir_lowering=False, num_devices=1)
        io = {n: nc.dram_tensor("in_" + n, a.shape, F32, kind="ExternalInput").ap() for n, a in arrays.items()}
        io["out"] = nc.dram_tensor("out", (P, BATCH * P), F32, kind="ExternalOutput").ap()
        return nc, decoder(nc, io, known)

    _, counted = program({})
    nc, final = program(counted.seen)
    assert final.seen == counted.seen
    got = run_bass_kernel_spmd(nc, [{"in_" + n: a for n, a in arrays.items()}], core_ids=[0]).results[0]["out"]
    return np.ascontiguousarray(got.reshape(P, BATCH, P).transpose(1, 2, 0))
```

```python
from contextlib import ExitStack

import concourse.bass as bass
from concourse import mybir

F32 = mybir.dt.float32
BF16 = mybir.dt.bfloat16
ALU = mybir.AluOpType
ACT = mybir.ActivationFunctionType
AX_X = mybir.AxisListType.X

P = 128
BATCH = 32
CTX_LEN, CTX_DIM = 77, 64
CHAINS = 2
PER = 4
GROUP = CHAINS * PER
TOK = PER * P
CTOK = PER * CTX_LEN
HEADS = 16
EXPERTS = 8
MASKED = -1e30
VECTOR_TURNS = (0, 1, 2)
DEPTH = 4
SLOTS = 4


def small_entries():
    out = []
    for n in ("Wq", "Wqs", "Wk", "Wks", "Wv", "Wo"):
        out.append(("L0_attn_" + n, 128))
    for lv in ("L0", "L3"):
        out += [(lv + "_xattn_Wq", 128), (lv + "_xattn_Wk", 128), (lv + "_xattn_Wv", 128),
                (lv + "_xattn_bq", 1), (lv + "_xattn_bk", 1), (lv + "_xattn_bv_row", 128)]
    out += [("L0_ffn_Wr", EXPERTS), ("L0_ffn_b1", 4 * (EXPERTS + 1)), ("L0_ffn_b2", EXPERTS + 1)]
    for i in range(DEPTH):
        out += [(f"L1_{i}_{n}", 1) for n in ("bo", "ln1_g", "ln1_b", "ln2_g", "ln2_b", "b2")]
        out.append((f"L1_{i}_b1", 4))
    out += [("L1_xattn_Wq", 128), ("L1_xattn_Wk", 128), ("L1_xattn_Wv", 128), ("L1_xattn_Wo", 128)]
    out += [("L1_ffn_Wr", EXPERTS), ("L1_ffn_br_row", EXPERTS), ("L1_ffn_b0", 2 * EXPERTS),
            ("L1_ffn_b1", 2 * EXPERTS), ("L1_ffn_b2", EXPERTS)]
    for lv in ("L2", "L3"):
        out += [(f"{lv}_attn_W{n}", 128) for n in "qkvo"]
        out += [(f"{lv}_attn_b{n}", 1) for n in "qkvo"] + [(f"{lv}_attn_bv_row", 128)]
    out += [("L2_ln1_g", 1), ("L2_ln1_b", 1), ("L2_ln2_g", 1), ("L2_ln2_b", 1)]
    for a in ("L2_a1_", "L2_a2_"):
        out += [(a + n, 1) for n in ("lnx_g", "lnx_b", "lny_g", "lny_b", "ln3_g", "ln3_b", "li1_b", "li3_b")]
        out.append((a + "li2_b", 4))
    out.append(("L2_ffn_W", 128))
    out += [("L3_rel_k", 3), ("L3_rel_v", 3), ("L3_rel_v_row", 128)]
    out += [("L3_ffn_W" + n, 128) for n in "qkvo"]
    out += [("L3_ffn_bo", 1), ("L3_ffn_Wr", EXPERTS), ("L3_ffn_b1", 4 * EXPERTS), ("L3_ffn_b2", EXPERTS),
            ("L3_ffn_ln1_g", 1), ("L3_ffn_ln1_b", 1), ("L3_ffn_ln2_g", 1), ("L3_ffn_ln2_b", 1)]
    out += [("rope_cos_q", 128), ("rope_sin_q", 128), ("rope_cos_k", 128), ("rope_sin_k", 128), ("head_pick", HEADS),
            ("mask8", 4), ("mask16", 2), ("lin_block", 64),
            ("descending", EXPERTS)]
    return out


def pieces():
    out = []

    def piece(name, user, entries, label, key, tail=()):
        out.append(dict(name=name, user=user, entries=entries, freed=(label, key, tail)))

    for e in range(EXPERTS + 1):
        piece(f"L0_ffn_{e}", "L0_ffn", [(f"L0_ffn_W1_{e}", 512), (f"L0_ffn_W2_{e}", 512)], "expert", ("L0_ffn", e))
    for i in range(DEPTH):
        piece(f"L1_{i}", f"L1_{i}",
              [(f"L1_{i}_Wq", 64), (f"L1_{i}_Wk", 64), (f"L1_{i}_Wlin", 128), (f"L1_{i}_Wv", 128),
               (f"L1_{i}_Wo", 128), (f"L1_{i}_W1", 512), (f"L1_{i}_W2", 512)], "proj", (f"L1_{i}_mlp",))
    for e in range(EXPERTS):
        piece(f"L1_ffn_{e}", "L1_ffn", [(f"L1_ffn_w{k}_{e}", 256) for k in range(3)], "expert", ("L1_ffn", e))
    for a in ("L2_a1", "L2_a2"):
        piece(a + "_qkv", a, [(f"{a}_w{k}", 512) for k in "qkv"], "v_raw", (a,), (PER - 1,))
        piece(a + "_out", a, [(f"{a}_li{k}", 512) for k in (1, 2, 3)], "proj", (a + "_mlp",))
    for e in range(EXPERTS):
        piece(f"L3_ffn_moe_{e}", "L3_ffn_moe", [(f"L3_ffn_W1_{e}", 512), (f"L3_ffn_W2_{e}", 512)], "expert",
              ("L3_ffn_moe", e))
    return out


def columns(entries):
    at, out = 0, {}
    for name, n in entries:
        out[name] = (at, n)
        at += n
    return out, at


def sequence():
    seq = []

    def norm(name, src, after, dst, **k):
        seq.append(dict(kind="norm", name=name, src=src, after=after, dst=dst, eps=1e-5, g=None, add=None, behind=None) | k)
        return ("normed", name)

    def mha(name, src, after, res, dst, **k):
        seq.append(dict(kind="mha", name=name, src=src, after=after, res=res, dst=dst, D=8, nk=P, mask=None,
                        rope=False, rel=False, kv=None, kv_after=None, bias=False, bo=None, post=False,
                        linear=False, wipes=False, wiped=None) | k)
        return ("residual", name)

    def xattn(name, after):
        seq.append(dict(kind="xattn", name=name, src="x", after=after))
        return ("residual", name)

    def mlp(name, src, after, res, dst, adds, **k):
        seq.append(dict(kind="mlp", name=name, src=src, after=after, res=res, dst=dst, adds=adds) | k)
        return ("residual", name)

    def moe(name, src, after, **k):
        seq.append(dict(kind="moe", name=name, src=src, after=after) | k)
        return ("residual", name)

    e = mha("L0_attn", "x", ("x_loaded", ""), "x", "u", mask="causal", rope=True)
    e = norm("L0_attn_ln", "u", e, "x")
    e = xattn("L0_xattn", e)
    e = norm("L0_xattn_ln", "u", e, "x")
    e = moe("L0_ffn", "x", e, shared=True, act=ACT.Gelu_apprx_tanh, glu=False, on="logits")
    e = norm("L0_ffn_ln", "u", e, "x")
    for i in range(DEPTH):
        n = f"L1_{i}"
        y = "x" if i == 0 else "y"
        e = norm(n + "_ln1", y, e, "hn", g=n + "_ln1")
        e = mha(n, "hn", e, y, "y", D=16, mask="causal", linear=True, bo=n + "_bo")
        e = norm(n + "_ln2", "y", e, "hn", g=n + "_ln2")
        last = i == DEPTH - 1
        e = mlp(n + "_mlp", "hn", e, "y", "u" if last else "y", ["x"] if last else [],
                W1=n + "_W1", b1=n + "_b1", W2=n + "_W2", b2=n + "_b2")
    e = norm("L1_attn_ln", "u", e, "x")
    e = mha("L1_xattn", "x", e, "x", "u", nk=CTX_LEN, kv="ctx", kv_after=("ctx_loaded", ""))
    e = norm("L1_xattn_ln", "u", e, "x")
    e = moe("L1_ffn", "x", e, shared=False, act=ACT.Silu, glu=True, on="logits")
    e = norm("L1_ffn_ln", "u", e, "x")
    e = mha("L2_attn", "x", e, "x", "u", mask="causal", bias=True, bo="L2_attn_bo")
    e = norm("L2_attn_ln", "u", e, "x")
    e = norm("L2_ln1", "x", e, "y", g="L2_ln1")
    e = norm("L2_a1_lnx", "y", e, "hn", g="L2_a1_lnx", g2="L2_a1_lny", dst2="hn2")
    e = mha("L2_a1", "hn", e, "y", "z", D=32, kv="hn2", kv_after=e, post=True, bo="L2_a1_li1_b")
    e = norm("L2_a1_ln3", "z", e, "hn", g="L2_a1_ln3")
    e = mlp("L2_a1_mlp", "hn", e, "z", "y", ["y"], W1="L2_a1_li2", b1="L2_a1_li2_b", W2="L2_a1_li3", b2="L2_a1_li3_b")
    e = norm("L2_ln2", "y", e, "y", g="L2_ln2")
    e = norm("L2_a2_lnx", "y", e, "hn", g="L2_a2_lnx")
    c = norm("L2_a2_lny", "ctx", ("ctx_loaded", ""), "yc", g="L2_a2_lny", rows=CTX_DIM, cols=CTOK,
             behind="L2_a2_lnx")
    e = mha("L2_a2", "hn", e, "y", "z", D=32, nk=CTX_LEN, kv="yc", kv_after=c, bo="L2_a2_li1_b", wipes=True)
    e = norm("L2_a2_ln3", "z", e, "hn", g="L2_a2_ln3")
    e = mlp("L2_a2_mlp", "hn", e, "z", "u", ["y", "x"], W1="L2_a2_li2", b1="L2_a2_li2_b", W2="L2_a2_li3",
            b2="L2_a2_li3_b")
    e = norm("L2_xattn_ln", "u", e, "x")
    seq.append(dict(kind="linear", name="L2_ffn", src="x", after=e))
    e = norm("L2_ffn_ln", "u", ("residual", "L2_ffn"), "x")
    e = mha("L3_attn", "x", e, "x", "u", mask="far", rel=True, bias=True, bo="L3_attn_bo",
            wiped="L2_a2")
    e = norm("L3_attn_ln", "u", e, "x")
    e = xattn("L3_xattn", e)
    e = norm("L3_xattn_ln", "u", e, "x")
    e = mha("L3_ffn", "x", e, "x", "u", bo="L3_ffn_bo")
    e = norm("L3_ffn_ln1", "u", e, "y", g="L3_ffn_ln1", eps=1e-6)
    e = moe("L3_ffn_moe", "y", e, shared=False, act=ACT.Gelu, glu=False, on="probs")
    e = norm("L3_ffn_ln2", "u", e, "u", g="L3_ffn_ln2", eps=1e-6, add="x")
    e = norm("L3_ffn_ln", "u", e, "x")
    return seq, e


SEQ, LAST = sequence()
STOP_AFTER = None


class Events:

    def __init__(self, nc, ctx, known):
        self.known, self.counts, self.seen = known, {}, {}
        labels = sorted({label for label, _ in known})
        self.sems = {label: ctx.enter_context(nc.semaphore(label)) for label in labels}
        self.make = lambda label: ctx.enter_context(nc.semaphore(label))

    def sem(self, label):
        if label not in self.sems:
            self.sems[label] = self.make(label)
        return self.sems[label]

    def made(self, label, key, by=1):
        self.counts[label] = self.counts.get(label, 0) + by
        assert (label, key) not in self.seen, (label, key)
        self.seen[(label, key)] = self.counts[label]
        return self.sem(label), by

    def have(self, label, key):
        assert not self.known or (label, key) in self.known, (label, key)
        return self.sem(label), self.known.get((label, key), 1)


class Banks:

    def __init__(self, rings):
        self.rings, self.n, self.tenant, self.place = rings, {}, {}, {}

    def take(self, ring, tile, freed_by):
        i = self.n.get(ring, 0) % len(self.rings[ring])
        self.n[ring] = self.n.get(ring, 0) + 1
        bank = self.rings[ring][i]
        before = self.tenant.get((ring, i))
        self.tenant[(ring, i)] = freed_by
        self.place[tile] = bank
        return bank, before

    def where(self, tile):
        return self.place[tile]


def decoder(nc, io, known):
    small_at, small_cols = columns(small_entries())
    stream = pieces()
    big_at, slot_cols = {}, 0
    for i, p in enumerate(stream):
        at, n = columns(p["entries"])
        p["slot"] = i % SLOTS
        big_at |= {name: (p["slot"], *where) for name, where in at.items()}
        slot_cols = max(slot_cols, n)
    slot_of = {p["name"]: p["slot"] for p in stream}
    seq, end = SEQ, LAST
    if STOP_AFTER is not None:
        seq = SEQ[:[st["name"] for st in SEQ].index(STOP_AFTER) + 1]
        end = ("normed", STOP_AFTER)
    C = range(CHAINS)
    S = range(PER)
    items = [(c, s) for c in C for s in S]

    with ExitStack() as ctx:
        def sb(name, shape, dt=F32):
            return ctx.enter_context(nc.sbuf_tensor(name, shape, dt))

        psum = [ctx.enter_context(nc.psum_tensor(f"bank{i}", [P, 512], F32)) for i in range(8)]
        banks = Banks({"flow": psum})

        small = sb("small", [P, small_cols])
        slots = [sb(f"slot{i}", [P, slot_cols]) for i in range(SLOTS)]

        def W(name, rows=P):
            if name in small_at:
                o, n = small_at[name]
                return small[0:rows, o:o + n]
            slot, o, n = big_at[name]
            return slots[slot][0:rows, o:o + n]

        ident = sb("ident", [P, P])
        identb = sb("identb", [P, P], BF16)
        center = sb("center", [P, P])
        average = sb("average", [P, P])
        center64 = sb("center64", [CTX_DIM, CTX_DIM])
        average64 = sb("average64", [CTX_DIM, CTX_DIM])
        mask = {k: sb("mask_" + k, [P, P], BF16) for k in ("causal", "far")}
        after_mask = sb("after_mask", [P, P])
        ones_row = sb("ones_row", [1, P])
        eps = {1e-5: sb("eps5", [P, 1]), 1e-6: sb("eps6", [P, 1])}
        tern = sb("tern", [P, P])
        tern_neg = sb("tern_neg", [P, P])
        tcol = sb("tcol", [P, 4])
        rel_col = sb("rel_col", [P, 6])
        rel_row = sb("rel_row", [1, P])

        B = {}
        for n in ("x", "u", "y", "z", "hn", "hn2", "sq", "part", "q", "k", "oL1"):
            B[n] = [sb(f"{n}{c}", [P, TOK]) for c in C]
        B["ctx"] = [sb(f"ctx{c}", [CTX_DIM, CTOK]) for c in C]
        B["yc"] = [B["z"][c][0:CTX_DIM, 0:CTOK] for c in C]
        B["rs"] = part = B["part"]
        gb = B["sq"]
        B["o"] = B["q"]
        silu = [(B["hn"][c], B["hn2"][c]) for c in C]
        qT = [B["hn2"][c][0:64, :] for c in C]
        qd = [sb(f"qd{c}", [P, 4 * TOK]) for c in C]
        km = [sb(f"km{c}", [P, PER, 4, P]) for c in C]
        vm = [sb(f"vm{c}", [P, PER, 4, P]) for c in C]
        near = [qd[c][:].rearrange("p (s n) -> p s n", s=PER) for c in C]
        v32 = [vm[c][:].rearrange("p s j t -> p s (j t)") for c in C]
        q4 = [qd[c][:].rearrange("p (t n) -> p t n", t=4) for c in C]
        k4 = [km[c][:].rearrange("p s j t -> p (s j t)").rearrange("p (t n) -> p t n", t=4) for c in C]
        vm16 = [sb(f"vm16{c}", [P, PER, 2, 64]) for c in C]
        vlin = [sb(f"vlin{c}", [P, PER, 65]) for c in C]
        work = sb("work", [P, 2, max(2048, 4 * TOK)])
        probs = [work[:, i, 0:2048].rearrange("p (r j t) -> p r j t", r=4, j=4) for i in range(2)]
        probsT = [sb(f"probsT{i}", [P, 4, 4, P]) for i in range(2)]
        hid = [work[:, c, 0:4 * TOK].rearrange("p (m t) -> p m t", m=4) for c in C]
        rowmax = [sb(f"rowmax{i}", [P, HEADS]) for i in range(2)]
        expsum = [sb(f"expsum{i}", [P, HEADS]) for i in range(2)]
        inverse = [sb(f"inverse{i}", [P, HEADS]) for i in range(2)]
        nearexp = [sb(f"nearexp{i}", [P, 2, HEADS]) for i in range(2)]
        spread = [sb(f"spread{i}", [P, 4, P]) for i in range(2)]
        spreadT = [sb(f"spreadT{i}", [P, 4, P]) for i in range(2)]
        diag = [sb(f"diag{c}", [P, PER, 32]) for c in C]
        qe, ke, kx = ([qd[c][:, i * PER * 64:(i + 1) * PER * 64].rearrange("p (s f) -> p s f", s=PER) for c in C]
                      for i in range(3))
        lctx = [sb(f"lctx{c}", [64, PER, 64]) for c in C]
        lcol = [sb(f"lcol{c}", [P, 4 * PER * 4]) for c in C]
        gate = [sb(f"gate{c}", [P, PER, EXPERTS]) for c in C]
        gtmp = [sb(f"gtmp{c}", [P, 8, PER, EXPERTS]) for c in C]
        gcol = [sb(f"gcol{c}", [P, 8, PER]) for c in C]
        px = [part[c][:, 0:CTOK].rearrange("p (s k) -> p s k", s=PER) for c in C]
        pxT = [km[c][:, :, 0, :] for c in C]
        vx = [qd[c][:, 0:TOK].rearrange("p (s f) -> p s f", s=PER) for c in C]
        xcol = [sb(f"xcol{c}", [P, 3, PER]) for c in C]

        w_small = ctx.enter_context(nc.semaphore("w_small"))
        cleared = ctx.enter_context(nc.semaphore("cleared"))
        shaped = ctx.enter_context(nc.semaphore("shaped"))
        setup_step = ctx.enter_context(nc.semaphore("setup_step"))
        setup_sum = ctx.enter_context(nc.semaphore("setup_sum"))

        with nc.Block() as block:
            @block.sync
            def _(sp):
                sp.dma_start(small[:], io["w_small"]).then_inc(w_small, 16)

            @block.gpsimd
            def _(pool):
                n = 0
                for t, value in [(ident, 0.0), (identb, 0.0), (after_mask, 1.0)] + [(m, 0.0) for m in mask.values()]:
                    nc.gpsimd.memset(t[:], value).then_inc(cleared, 1)
                    n += 1
                pool.wait_ge(cleared, n)

                def keep(t, op, fill, base, step, per_row):
                    return nc.gpsimd.affine_select(out=t[:], in_=t[:], compare_op=op, fill=fill, base=base,
                                                   pattern=[[step, P]], channel_multiplier=per_row)
                keep(ident, ALU.not_equal, 1.0, 0, -1, 1).then_inc(shaped, 1)
                keep(identb, ALU.not_equal, 1.0, 0, -1, 1).then_inc(shaped, 1)
                for name, back in (("causal", 0), ("far", -2)):
                    keep(mask[name], ALU.is_ge, MASKED, back, -1, 1).then_inc(shaped, 1)
                keep(after_mask, ALU.is_ge, 0.0, -1, -1, 1).then_inc(shaped, 1)
                for c in C:
                    nc.gpsimd.memset(vm[c][:], 0.0)
                    nc.gpsimd.memset(vm16[c][:], 0.0)
                    nc.gpsimd.memset(vlin[c][:], 1.0)
                    nc.gpsimd.memset(B["oL1"][c][:], 0.0)
                for i in range(2):
                    nc.gpsimd.memset(rowmax[i][:], 0.0)

            @block.vector
            def _(dve):
                step = [0]

                def link(ins):
                    step[0] += 1
                    ins.then_inc(setup_step, 1)
                    dve.wait_ge(setup_step, step[0])

                nc.vector.memset(average[:], 1.0 / P)
                nc.vector.memset(average64[:], 1.0 / CTX_DIM)
                nc.vector.memset(ones_row[:], 1.0)
                for value, t in eps.items():
                    link(nc.vector.memset(t[:], value))
                dve.wait_ge(shaped, 1)
                nc.vector.tensor_scalar(center[:], ident[:], -1.0 / P, None, ALU.add)
                link(nc.vector.tensor_scalar(center64[:], ident[0:CTX_DIM, 0:CTX_DIM], -1.0 / CTX_DIM, None, ALU.add))
                dve.wait_ge(w_small, 16)
                w = W("L2_ffn_W")
                link(nc.vector.tensor_reduce(tcol[:, 0:1], w, AX_X, ALU.add, apply_absolute_value=True))
                nc.vector.tensor_scalar(rel_col[:, 0:3], W("L3_rel_k"), W("L3_attn_bk"), None, ALU.add)
                nc.vector.tensor_scalar(rel_col[:, 3:6], W("L3_rel_v"), W("L3_attn_bv"), None, ALU.add)
                nc.vector.tensor_tensor(rel_row[:], W("L3_rel_v_row", 1), W("L3_attn_bv_row", 1), ALU.add)
                dve.wait_ge(setup_sum, 1)
                link(nc.vector.tensor_scalar(tcol[:, 1:2], psum[0][:, 0:1], 1.0 / P, 1e-5, ALU.mult, ALU.max))
                link(nc.vector.tensor_scalar(tcol[:, 2:3], tcol[:, 1:2], 0.5, None, ALU.mult))
                link(nc.vector.tensor_scalar(tcol[:, 3:4], tcol[:, 1:2], -0.5, None, ALU.mult))
                link(nc.vector.tensor_scalar(tern[:], w, tcol[:, 2:3], tcol[:, 1:2], ALU.is_gt, ALU.mult))
                link(nc.vector.tensor_scalar(tern_neg[:], w, tcol[:, 3:4], tcol[:, 1:2], ALU.is_lt, ALU.mult))
                nc.vector.tensor_tensor(tern[:], tern[:], tern_neg[:], ALU.subtract)

            @block.tensor
            def _(pe):
                pe.wait_ge(setup_step, 4)
                nc.tensor.matmul(psum[0][:, 0:1], average[:], tcol[:, 0:1], start=True, stop=True).then_inc(setup_sum, 1)

        ev = Events(nc, ctx, known)
        made, have = ev.made, ev.have

        def input_of(after, c):
            label, name = after
            return have(label + (str(c) if label.endswith("_loaded") else ""), (name, c))

        def cols(ap, s):
            return ap[:, s * P:(s + 1) * P]

        def turned_by(st, r):
            return "turned_v" if st["post"] or r in VECTOR_TURNS else "turned_s"

        def blocks(st):
            return range(2 if st["D"] == 16 else 4)

        def masked_keys(st, c, j):
            rows, nk = 64 if st["D"] == 16 else P, st["nk"]
            keys = B["k"][c][0:rows, 0:PER * nk].rearrange("p (s t) -> p s t", s=PER)
            return km[c][0:rows, :, j, 0:nk], keys, W("mask16" if st["D"] == 16 else "mask8", rows)[:, j:j + 1]

        def output_step(c):
            return min((c + 1) * PER + 2, GROUP + 1)

        def per_feature(st):
            return 4 if st["D"] == 32 else 3 if st["rel"] else 1

        def per_block(st):
            return 2 if st["D"] == 16 else 4

        def weight(st, n):
            return W(f"{st['name']}_W{n}", CTX_DIM if st["kv"] and n in "kv" else P)

        with nc.Fori(0, BATCH // GROUP) as g:
            with nc.Block() as block:

                @block.tensor
                def _(pe):
                    def arrived(piece):
                        pe.wait_ge(*have(f"weights{slot_of[piece]}", piece))

                    def bank(tile, freed_by, kind="flow"):
                        b, before = banks.take(kind, tile, freed_by)
                        if before is not None:
                            pe.wait_ge(*have(*before))
                        return b

                    def norm(st):
                        n, rows, w = st["name"], st.get("rows", P), st.get("cols", TOK)
                        cen, avg = (center, average) if rows == P else (center64, average64)
                        for c in C:
                            pe.wait_ge(*input_of(st["after"], c))
                            b = bank(("centred", n, c), ("normed", (n, c)))
                            nc.tensor.matmul(b[0:rows, 0:w], cen[:], B[st["src"]][c][0:rows, 0:w],
                                             start=True, stop=True).then_inc(*made("centred", (n, c)))
                        for c in C:
                            b = bank(("variance", n, c), ("log_var", (n, c)))
                            pe.wait_ge(*have("squared", (n, c)))
                            nc.tensor.matmul(b[0:rows, 0:w], avg[:], B["sq"][c][0:rows, 0:w],
                                             start=True, stop=True).then_inc(*made("variance", (n, c)))

                    def rows_of(st, n, c, src, w, rows, nk, bias_row, width):
                        b = bank(("v_raw", n, c), ("v", (n, c)))
                        for s in S:
                            out = b[0:nk, s * width:(s + 1) * width]
                            ins = nc.tensor.matmul(out, src[0:rows, s * nk:(s + 1) * nk], w, start=True,
                                                   stop=bias_row is None)
                            if bias_row is not None:
                                ins = nc.tensor.matmul(out, ones_row[:, 0:nk], bias_row, start=False, stop=True)
                        ins.then_inc(*made("v_raw", (n, c)))

                    def mha(st):
                        n, nk, D = st["name"], st["nk"], st["D"]
                        J = per_block(st)
                        for c in C:
                            src = B[st["src"]][c]
                            pe.wait_ge(*input_of(st["after"], c))
                            kv, rows = src, P
                            if st["kv"]:
                                kv = B[st["kv"]][c]
                                rows = P if st["kv"] == "hn2" else CTX_DIM
                                pe.wait_ge(*input_of(st["kv_after"], c))
                            if c == 0 and (D == 32 or st["linear"]):
                                arrived(n + "_qkv" if D == 32 else n)
                            if D == 32:
                                for t in range(4):
                                    b = bank(("q_raw", n, c, t), ("q", (n, c, t)))
                                    nc.tensor.matmul(b[:, 0:TOK], W(n + "_wq")[:, t * P:(t + 1) * P], src[:],
                                                     start=True, stop=True).then_inc(*made("q_raw", (n, c, t)))
                                    b = bank(("k_raw", n, c, t), ("k_copy", (n, c, t)))
                                    nc.tensor.matmul(b[:, 0:PER * nk], W(n + "_wk", rows)[:, t * P:(t + 1) * P],
                                                     kv[:], start=True, stop=True).then_inc(*made("k_raw", (n, c, t)))
                                for s in S:
                                    b = bank(("v_raw", n, c, s), ("v", (n, c, s)))
                                    nc.tensor.matmul(b[0:nk, 0:512], kv[0:rows, s * nk:(s + 1) * nk], W(n + "_wv", rows),
                                                     start=True, stop=True).then_inc(*made("v_raw", (n, c, s)))
                                continue
                            M = 64 if D == 16 else P
                            for which in ("q", "qs", "k", "ks") if st["rope"] else ("q", "k"):
                                b = bank((which + "_raw", n, c),
                                         ("near_prod", (n, c)) if st["rel"] and which == "k" else (which, (n, c)))
                                rhs, N = (kv, PER * nk) if which[0] == "k" else (src, TOK)
                                nc.tensor.matmul(b[0:M, 0:N], weight(st, which), rhs[:],
                                                 start=True, stop=True).then_inc(*made(which + "_raw", (n, c)))
                            if st["rel"]:
                                b = bank(("vT_raw", n, c), ("vT", (n, c)))
                                nc.tensor.matmul(b[:, 0:TOK], weight(st, "v"), src[:],
                                                 start=True, stop=True).then_inc(*made("vT_raw", (n, c)))
                            row = None
                            if st["bias"]:
                                row = rel_row[:] if st["rel"] else W(n + "_bv_row", 1)
                            rows_of(st, n, c, kv, weight(st, "v"), rows, nk, row, P)
                            if st["linear"]:
                                b = bank(("lin_raw", n, c), ("lin_shift", (n, c)))
                                for s in S:
                                    ins = nc.tensor.matmul(cols(b, s), cols(src, s), W(n + "_Wlin"), start=True, stop=True)
                                ins.then_inc(*made("lin_raw", (n, c)))
                        def global_heads():
                            for c in C:
                                b = bank(("lin_qT", n, c), ("lin_qTs", (n, c)))
                                pe.wait_ge(*have("lin_ready", (n, c)))
                                for s in S:
                                    ins = nc.tensor.transpose(b[0:64, s * P:(s + 1) * P], qe[c][:, s, :], ident[:])
                                ins.then_inc(*made("lin_qT", (n, c)))
                                b = bank(("lin_sum", n, c), ("lin_ctx", (n, c)))
                                pe.wait_ge(*have("v", (n, c)))
                                for s in S:
                                    ins = nc.tensor.matmul(b[0:64, s * 65:(s + 1) * 65], ke[c][0:64, s, :],
                                                           vlin[c][0:64, s, :], start=True, stop=True)
                                ins.then_inc(*made("lin_sum", (n, c)))

                        if st["rel"]:
                            for c in C:
                                b = bank(("diag_raw", n, c), ("diag", (n, c)))
                                pe.wait_ge(*have("near_prod", (n, c)))
                                for s in S:
                                    for i in range(2):
                                        ins = nc.tensor.matmul(b[:, s * 32 + i * 16:s * 32 + (i + 1) * 16],
                                                               near[c][:, s, (2 + i) * P:(3 + i) * P], W("head_pick"),
                                                               start=True, stop=True)
                                ins.then_inc(*made("diag_raw", (n, c)))

                        def scores(t):
                            c, s = items[t]
                            for r in blocks(st):
                                g32 = slice(32 * r, 32 * r + 32)
                                b = bank(("scores", n, c, s, r), ("probs", (n, c, s, r)))
                                if s == 0 and r == 0:
                                    if D == 32:
                                        pe.wait_ge(*have("q", (n, c, 3)))
                                        pe.wait_ge(*have("k_copy", (n, c, 3)))
                                    else:
                                        pe.wait_ge(*have("q", (n, c)))
                                        pe.wait_ge(*have("k_masked_s", (n, c, J - 2)))
                                        pe.wait_ge(*have("k_masked_v", (n, c, J - 1)))
                                if D == 32:
                                    for j in range(4):
                                        ins = nc.tensor.matmul(b[:, j * nk:(j + 1) * nk], q4[c][g32, j, s * P:(s + 1) * P],
                                                               k4[c][g32, j, s * nk:(s + 1) * nk], start=True, stop=True)
                                else:
                                    out = b[:, 0:J * nk]
                                    if st["mask"]:
                                        nc.tensor.matmul(out, identb[:], mask[st["mask"]][:].unsqueeze(1)
                                                         .to_broadcast([P, J, P]), start=True, stop=False)
                                    ins = nc.tensor.matmul(out, B["q"][c][g32, s * P:(s + 1) * P],
                                                           km[c][g32, s, 0:J, 0:nk], start=not st["mask"], stop=True)
                                ins.then_inc(*made("scores", (n, c, s, r)))

                        def turn(t):
                            c, s = items[t]
                            for r in blocks(st):
                                b = bank(("turned", n, c, s, r), (turned_by(st, r), (n, c, s, r)))
                                pe.wait_ge(*have("probs", (n, c, s, r)))
                                for j in range(J):
                                    ins = nc.tensor.transpose(b[0:nk, j * P:(j + 1) * P], probs[t % 2][:, r, j, 0:nk],
                                                              ident[:])
                                ins.then_inc(*made("turned", (n, c, s, r)))

                        def turn_spread(t):
                            c, s = items[t]
                            b = bank(("wide_turned", n, c, s), ("wide_taken", (n, c, s)))
                            pe.wait_ge(*have("wide", (n, c, s)))
                            M = 64 if D == 16 else P
                            for i in range(per_feature(st)):
                                ins = nc.tensor.transpose(b[0:M, i * P:(i + 1) * P], spread[t % 2][:, i, 0:M], ident[:])
                            ins.then_inc(*made("wide_turned", (n, c, s)))

                        def attend(t):
                            c, s = items[t]
                            pr = probsT[t % 2]
                            if D == 32:
                                b = bank(("attended", n, c, s), ("context", (n, c, s)))
                                pe.wait_ge(*have("v", (n, c, s)))
                                for r in range(4):
                                    pe.wait_ge(*have(turned_by(st, r), (n, c, s, r)))
                                    for j in range(4):
                                        h = 4 * j + r
                                        ins = nc.tensor.matmul(b[32 * r:32 * r + 32, j * P:(j + 1) * P],
                                                               v32[c][0:nk, s, h * 32:(h + 1) * 32], pr[0:nk, r, j, :],
                                                               start=True, stop=True)
                                ins.then_inc(*made("attended", (n, c, s)))
                                return
                            b = bank(("attended", n, c, s), ("context", (n, c, s)))
                            pe.wait_ge(*have("v", (n, c)))
                            vals = vm16 if D == 16 else vm
                            for r in blocks(st):
                                g32 = slice(32 * r, 32 * r + 32)
                                pe.wait_ge(*have(turned_by(st, r), (n, c, s, r)))
                                for j in range(J):
                                    ins = nc.tensor.matmul(b[g32, 0:P], vals[c][0:nk, s, j, g32], pr[0:nk, r, j, :],
                                                           start=(j == 0), stop=(j == J - 1))
                            if st["linear"]:
                                if s == 0:
                                    pe.wait_ge(*have("lin_ctx", (n, c)))
                                    pe.wait_ge(*have("lin_qTs", (n, c)))
                                ins = nc.tensor.matmul(b[64:P, 64:P], lctx[c][:, s, :], qT[c][:, s * P + 64:(s + 1) * P],
                                                       start=True, stop=True)
                            ins.then_inc(*made("attended", (n, c, s)))

                        def output(c):
                            if D == 32 and c == 0:
                                arrived(n + "_out")
                            b = bank(("proj", n, c), ("residual", (n, c)))
                            pe.wait_ge(*have("context", (n, c, PER - 1)))
                            if D == 32:
                                for j in range(4):
                                    ins = nc.tensor.matmul(b[:, 0:TOK], W(n + "_li1")[:, j * P:(j + 1) * P], q4[c][:, j, :],
                                                           start=(j == 0), stop=(j == 3))
                            else:
                                o = B["oL1" if st["linear"] else "o"][c]
                                ins = nc.tensor.matmul(b[:, 0:TOK], weight(st, "o"), o[:], start=True, stop=True)
                            ins.then_inc(*made("proj", (n, c)))

                        for t in range(GROUP + 2):
                            if t >= 2:
                                turn_spread(t - 2)
                            if t < GROUP:
                                scores(t)
                            if st["linear"] and t == 2:
                                global_heads()
                            if t >= 2:
                                attend(t - 2)
                            if 1 <= t <= GROUP:
                                turn(t - 1)
                            for c in C:
                                if t == output_step(c):
                                    output(c)

                    def xattn(st):
                        n = st["name"]
                        for c in C:
                            pe.wait_ge(*input_of(st["after"], c))
                            pe.wait_ge(*input_of(("ctx_loaded", ""), c))
                            b = bank(("q_raw", n, c), ("q", (n, c)))
                            nc.tensor.matmul(b[:, 0:TOK], W(n + "_Wq"), B["x"][c][:], start=True,
                                             stop=True).then_inc(*made("q_raw", (n, c)))
                            b = bank(("k_raw", n, c), ("k", (n, c)))
                            nc.tensor.matmul(b[:, 0:CTOK], W(n + "_Wk", CTX_DIM), B["ctx"][c][:], start=True,
                                             stop=True).then_inc(*made("k_raw", (n, c)))
                            rows_of(st, n, c, B["ctx"][c], W(n + "_Wv", CTX_DIM), CTX_DIM, CTX_LEN,
                                    W(n + "_bv_row", 1), P)
                        for c in C:
                            b = bank(("xscores", n, c), ("xexp", (n, c)))
                            pe.wait_ge(*have("q", (n, c)))
                            pe.wait_ge(*have("k", (n, c)))
                            for s in S:
                                ins = nc.tensor.matmul(b[:, s * CTX_LEN:(s + 1) * CTX_LEN], cols(B["q"][c], s),
                                                       B["k"][c][:, s * CTX_LEN:(s + 1) * CTX_LEN], start=True, stop=True)
                            ins.then_inc(*made("xscores", (n, c)))
                        for c in C:
                            b = bank(("xturned", n, c), ("xprobsT", (n, c)))
                            pe.wait_ge(*have("xprobs", (n, c)))
                            for s in S:
                                ins = nc.tensor.transpose(b[0:CTX_LEN, s * P:(s + 1) * P], px[c][:, s, :], ident[:])
                            ins.then_inc(*made("xturned", (n, c)))
                        for c in C:
                            b = bank(("xout", n, c), ("residual", (n, c)))
                            pe.wait_ge(*have("xprobsT", (n, c)))
                            pe.wait_ge(*have("v", (n, c)))
                            for s in S:
                                ins = nc.tensor.matmul(cols(b, s), vx[c][0:CTX_LEN, s, :], pxT[c][0:CTX_LEN, s, :],
                                                       start=True, stop=True)
                            ins.then_inc(*made("xout", (n, c)))

                    def mlp(st):
                        n = st["name"]
                        for c in C:
                            pe.wait_ge(*input_of(st["after"], c))
                            for m in range(4):
                                b = bank(("hid_raw", n, c, m), ("hid", (n, c, m)))
                                nc.tensor.matmul(b[:, 0:TOK], W(st["W1"])[:, m * P:(m + 1) * P], B[st["src"]][c][:],
                                                 start=True, stop=True).then_inc(*made("hid_raw", (n, c, m)))
                        for c in C:
                            b = bank(("proj", n, c), ("acc_taken" if st["adds"] else "residual", (n, c)))
                            for m in range(4):
                                pe.wait_ge(*have("hid", (n, c, m)))
                                ins = nc.tensor.matmul(b[:, 0:TOK], W(st["W2"])[:, m * P:(m + 1) * P], hid[c][:, m, :],
                                                       start=(m == 0), stop=(m == 3))
                            ins.then_inc(*made("proj", (n, c)))

                    def moe(st):
                        n, base = st["name"], "L3_ffn" if st["name"] == "L3_ffn_moe" else st["name"]
                        for c in C:
                            pe.wait_ge(*input_of(st["after"], c))
                            b = bank(("logits", n, c), ("logits_in", (n, c)))
                            for s in S:
                                out = b[:, s * EXPERTS:(s + 1) * EXPERTS]
                                ins = nc.tensor.matmul(out, cols(B[st["src"]][c], s), W(base + "_Wr"), start=True,
                                                       stop=not st["glu"])
                                if st["glu"]:
                                    ins = nc.tensor.matmul(out, ones_row[:], W(base + "_br_row", 1), start=False, stop=True)
                            ins.then_inc(*made("logits", (n, c)))
                        work_items = [(e, c) for e in range(EXPERTS + st["shared"]) for c in C]

                        def up(e, c):
                            src = B[st["src"]][c][:]
                            if c == 0:
                                arrived(f"{n}_{e}")
                            if st["glu"]:
                                for m in range(2):
                                    for w, lab, by in (("w1", "gate_raw", "silu"), ("w0", "hid_raw", "gated")):
                                        b = bank((lab, n, e, c, m), (by, (n, e, c, m)))
                                        nc.tensor.matmul(b[:, 0:TOK], W(f"{base}_{w}_{e}")[:, m * P:(m + 1) * P], src,
                                                         start=True, stop=True).then_inc(*made(lab, (n, e, c, m)))
                                return
                            for m in range(4):
                                b = bank(("hid_raw", n, e, c, m), ("hid", (n, e, c, m)))
                                nc.tensor.matmul(b[:, 0:TOK], W(f"{base}_W1_{e}")[:, m * P:(m + 1) * P], src,
                                                 start=True, stop=True).then_inc(*made("hid_raw", (n, e, c, m)))

                        def down(e, c):
                            if not (st["shared"] and e == 0):
                                b = bank(("gate_wide", n, e, c), ("gate_copy", (n, e, c)))
                                pe.wait_ge(*have("gate", (n, c)))
                                for s in S:
                                    one = gate[c][:, s, e - st["shared"]:e - st["shared"] + 1].to_broadcast([P, P])
                                    ins = nc.tensor.matmul(cols(b, s), one, ident[:], start=True, stop=True)
                                ins.then_inc(*made("gate_wide", (n, e, c)))
                            M = 2 if st["glu"] else 4
                            b = bank(("expert", n, e, c), ("expert_taken", (n, e, c)))
                            w = W(f"{base}_w2_{e}" if st["glu"] else f"{base}_W2_{e}")
                            for m in range(M):
                                pe.wait_ge(*have("gated" if st["glu"] else "hid", (n, e, c, m)))
                                ins = nc.tensor.matmul(b[:, 0:TOK], w[:, m * P:(m + 1) * P], hid[c][:, m, :],
                                                       start=(m == 0), stop=(m == M - 1))
                            ins.then_inc(*made("expert", (n, e, c)))

                        for i in range(len(work_items) + 1):
                            if i < len(work_items):
                                up(*work_items[i])
                            if i:
                                down(*work_items[i - 1])

                    def linear(st):
                        for c in C:
                            pe.wait_ge(*input_of(st["after"], c))
                            b = bank(("proj", st["name"], c), ("residual", (st["name"], c)))
                            nc.tensor.matmul(b[:, 0:TOK], tern[:], B["x"][c][:], start=True,
                                             stop=True).then_inc(*made("proj", (st["name"], c)))

                    todo = dict(norm=norm, mha=mha, xattn=xattn, mlp=mlp, moe=moe, linear=linear)
                    for st in seq:
                        todo[st["kind"]](st)

                @block.scalar
                def _(act):
                    step = [0]

                    def link(ins):
                        step[0] += 1
                        ins.then_inc(*made("scalar_step", step[0]))
                        act.wait_ge(*have("scalar_step", step[0]))

                    def tables(name):
                        nc.scalar.preload_act_table_set(name)

                    common = "natural_log_exp_and_others"
                    special = {ACT.Gelu: "gelu_and_others", ACT.Gelu_apprx_tanh: "gelu_apprx_tanh_and_others",
                               ACT.Silu: "silu_and_others"}

                    def norm(st):
                        n, rows, w = st["name"], st.get("rows", P), st.get("cols", TOK)
                        for c in C:
                            act.wait_ge(*have("centred", (n, c)))
                            nc.scalar.activation(B["sq"][c][0:rows, 0:w], banks.where(("centred", n, c))[0:rows, 0:w],
                                                 ACT.Square).then_inc(*made("squared", (n, c)))
                        for c in C:
                            rs = B["rs"][c][0:rows, 0:w]
                            if st["behind"]:
                                act.wait_ge(*have("normed", (st["behind"], c)))
                            act.wait_ge(*have("variance", (n, c)))
                            nc.scalar.activation(rs, banks.where(("variance", n, c))[0:rows, 0:w], ACT.Ln,
                                                 bias=eps[st["eps"]][0:rows]).then_inc(*made("log_var", (n, c)))
                            act.wait_ge(*have("log_var", (n, c)))
                            nc.scalar.activation(rs, rs, ACT.Exp, scale=-0.5).then_inc(*made("rstd", (n, c)))

                    def mha(st):
                        n, nk, D = st["name"], st["nk"], st["D"]
                        J = per_block(st)
                        for c in C:
                            if D == 32:
                                for t in range(4):
                                    act.wait_ge(*have("k_raw", (n, c, t)))
                                    nc.scalar.activation(k4[c][:, t, 0:PER * nk], banks.where(("k_raw", n, c, t))[:, 0:PER * nk],
                                                         ACT.Copy).then_inc(*made("k_copy", (n, c, t)))
                                for s in S:
                                    act.wait_ge(*have("v_raw", (n, c, s)))
                                    nc.scalar.activation(v32[c][0:nk, s, :], banks.where(("v_raw", n, c, s))[0:nk, :],
                                                         ACT.Copy).then_inc(*made("v", (n, c, s)))
                                continue
                            M = 64 if D == 16 else P
                            if st["wiped"]:
                                act.wait_ge(*have("values_zeroed", (st["wiped"], c)))
                            act.wait_ge(*have("v_raw", (n, c)))
                            raw = banks.where(("v_raw", n, c))[0:nk, 0:TOK].rearrange("p (s f) -> p s f", s=PER)
                            d = D
                            for j in range(J):
                                src = raw[:, :, 0:M].rearrange("p s (r j d) -> p s r j d", j=J, d=d)[:, :, :, j, :]
                                dst = (vm16 if D == 16 else vm)[c][0:nk, :, j, :] \
                                    .rearrange("p s (r j d) -> p s r j d", j=J, d=d)[:, :, :, j, :]
                                ins = nc.scalar.activation(dst, src, ACT.Copy)
                            if st["linear"]:
                                ins = nc.scalar.activation(vlin[c][:, :, 0:64], raw[:, :, 64:P], ACT.Copy)
                            ins.then_inc(*made("v", (n, c)))
                            act.wait_ge(*have("k", (n, c)))
                            for j in range(0, J, 2):
                                out, keys, sel = masked_keys(st, c, j)
                                nc.scalar.activation(out, keys, ACT.Copy, scale=sel).then_inc(*made("k_masked_s", (n, c, j)))
                        if st["linear"]:
                            for c in C:
                                act.wait_ge(*have("lin_shift", (n, c)))
                                nc.scalar.activation(qe[c][:], qe[c][:], ACT.Exp)
                                nc.scalar.activation(ke[c][:], ke[c][:], ACT.Exp).then_inc(*made("lin_exp", (n, c)))

                        def soften(t):
                            c, s = items[t]
                            if st["rel"]:
                                near_part = nearexp[t % 2][:]
                                act.wait_ge(*have("near_shift", (n, c, s)))
                                nc.scalar.activation(near_part, near_part, ACT.Exp).then_inc(*made("near_exp", (n, c, s)))
                            for r in blocks(st):
                                act.wait_ge(*have("row_max", (n, c, s, r)))
                                if r == 0 and t >= 2:
                                    act.wait_ge(*have("wide_turned", (n, *items[t - 2])))
                                for j in range(J):
                                    ins = nc.scalar.activation(probs[t % 2][:, r, j, 0:nk],
                                                               banks.where(("scores", n, c, s, r))[:, j * nk:(j + 1) * nk],
                                                               ACT.Exp, bias=rowmax[t % 2][:, 4 * r + j:4 * r + j + 1],
                                                               accum_out=expsum[t % 2][:, 4 * r + j:4 * r + j + 1])
                                ins.then_inc(*made("probs", (n, c, s, r)))

                        def untangle(t):
                            c, s = items[t]
                            for r in blocks(st):
                                if turned_by(st, r) != "turned_s":
                                    continue
                                act.wait_ge(*have("turned", (n, c, s, r)))
                                if t >= 2:
                                    act.wait_ge(*have("attended", (n, *items[t - 2])))
                                nc.scalar.activation(probsT[t % 2][0:nk, r, 0:J, :],
                                                     banks.where(("turned", n, c, s, r))[0:nk, 0:J * P]
                                                     .rearrange("p (j t) -> p j t", j=J),
                                                     ACT.Copy).then_inc(*made("turned_s", (n, c, s, r)))

                        def take_spread(t):
                            c, s = items[t]
                            M, w = 64 if D == 16 else P, per_feature(st)
                            act.wait_ge(*have("wide_turned", (n, c, s)))
                            if t >= 2:
                                act.wait_ge(*have("context", (n, *items[t - 2])))
                            nc.scalar.activation(spreadT[t % 2][0:M, 0:w, :], banks.where(("wide_turned", n, c, s))[0:M, 0:w * P]
                                                 .rearrange("p (i t) -> p i t", i=w), ACT.Copy
                                                 ).then_inc(*made("wide_taken", (n, c, s)))

                        for t in range(GROUP + 2):
                            if t >= 2:
                                take_spread(t - 2)
                            if t < GROUP:
                                soften(t)
                            if 1 <= t <= GROUP:
                                untangle(t - 1)

                    def xattn(st):
                        n = st["name"]
                        for c in C:
                            act.wait_ge(*have("v_raw", (n, c)))
                            nc.scalar.activation(vx[c][0:CTX_LEN], banks.where(("v_raw", n, c))[0:CTX_LEN, 0:TOK]
                                                 .rearrange("p (s f) -> p s f", s=PER), ACT.Copy).then_inc(*made("v", (n, c)))
                        for c in C:
                            act.wait_ge(*have("xmax", (n, c)))
                            for s in S:
                                ins = nc.scalar.activation(px[c][:, s, :],
                                                           banks.where(("xscores", n, c))[:, s * CTX_LEN:(s + 1) * CTX_LEN],
                                                           ACT.Exp, bias=xcol[c][:, 0, s:s + 1])
                            ins.then_inc(*made("xexp", (n, c)))
                        for c in C:
                            act.wait_ge(*have("xturned", (n, c)))
                            nc.scalar.activation(pxT[c][0:CTX_LEN], banks.where(("xturned", n, c))[0:CTX_LEN, 0:TOK]
                                                 .rearrange("p (s f) -> p s f", s=PER),
                                                 ACT.Copy).then_inc(*made("xprobsT", (n, c)))

                    def mlp(st):
                        n = st["name"]
                        tables(special[ACT.Gelu])
                        for c in C:
                            for m in range(4):
                                act.wait_ge(*have("hid_raw", (n, c, m)))
                                nc.scalar.activation(hid[c][:, m, :], banks.where(("hid_raw", n, c, m))[:, 0:TOK], ACT.Gelu,
                                                     bias=W(st["b1"])[:, m:m + 1]).then_inc(*made("hid", (n, c, m)))
                        tables(common)

                    def moe(st):
                        n, base = st["name"], "L3_ffn" if st["name"] == "L3_ffn_moe" else st["name"]
                        if st["on"] == "probs":
                            for c in C:
                                act.wait_ge(*have("logits_in", (n, c)))
                                nc.scalar.activation(gtmp[c][:, 0], gtmp[c][:, 0], ACT.Exp).then_inc(*made("router_exp", (n, c)))
                        tables(special[st["act"]])
                        work_items = [(e, c) for e in range(EXPERTS + st["shared"]) for c in C]
                        for i in range(len(work_items) + 1):
                            if i == 1:
                                for c in C:
                                    act.wait_ge(*have("gate_gap", (n, c)))
                                    nc.scalar.activation(gcol[c][:, 6], gcol[c][:, 6], ACT.Tanh, scale=0.5
                                                         ).then_inc(*made("gate_tanh", (n, c)))
                            if i < len(work_items):
                                e, c = work_items[i]
                                if st["glu"]:
                                    for m in range(2):
                                        act.wait_ge(*have("gate_raw", (n, e, c, m)))
                                        if e:
                                            act.wait_ge(*have("gated", (n, e - 1, c, m)))
                                        nc.scalar.activation(silu[c][m][:], banks.where(("gate_raw", n, e, c, m))[:, 0:TOK],
                                                             st["act"], bias=W(base + "_b1")[:, 2 * e + m:2 * e + m + 1]
                                                             ).then_inc(*made("silu", (n, e, c, m)))
                                else:
                                    for m in range(4):
                                        act.wait_ge(*have("hid_raw", (n, e, c, m)))
                                        nc.scalar.activation(hid[c][:, m, :], banks.where(("hid_raw", n, e, c, m))[:, 0:TOK],
                                                             st["act"], bias=W(base + "_b1")[:, 4 * e + m:4 * e + m + 1]
                                                             ).then_inc(*made("hid", (n, e, c, m)))
                            if i:
                                e, c = work_items[i - 1]
                                if st["shared"] and e == 0:
                                    continue
                                act.wait_ge(*have("gate_wide", (n, e, c)))
                                if e - st["shared"] > 0:
                                    act.wait_ge(*have("expert_taken", (n, e - 1, c)))
                                nc.scalar.activation(gb[c][:], banks.where(("gate_wide", n, e, c))[:, 0:TOK],
                                                     ACT.Copy).then_inc(*made("gate_copy", (n, e, c)))
                        tables(common)

                    todo = dict(norm=norm, mha=mha, xattn=xattn, mlp=mlp, moe=moe, linear=lambda st: None)
                    tables(common)
                    for st in seq:
                        todo[st["kind"]](st)

                @block.vector
                def _(dve):
                    step = [0]

                    def link(ins):
                        step[0] += 1
                        ins.then_inc(*made("vector_step", step[0]))
                        dve.wait_ge(*have("vector_step", step[0]))

                    V = nc.vector

                    def norm(st):
                        n, rows, w = st["name"], st.get("rows", P), st.get("cols", TOK)
                        for c in C:
                            cen = banks.where(("centred", n, c))[0:rows, 0:w]
                            rs = B["rs"][c][0:rows, 0:w]
                            dst = B[st["dst"]][c][0:rows, 0:w]
                            dve.wait_ge(*have("rstd", (n, c)))
                            if st["g"] is None:
                                V.tensor_tensor(dst, cen, rs, ALU.mult).then_inc(*made("normed", (n, c)))
                                continue
                            gain, shift = W(st["g"] + "_g", rows), W(st["g"] + "_b", rows)
                            if "dst2" in st:
                                dst2 = B[st["dst2"]][c][0:rows, 0:w]
                                link(V.tensor_tensor(rs, cen, rs, ALU.mult))
                                V.tensor_scalar(dst2, rs, W(st["g2"] + "_g", rows), W(st["g2"] + "_b", rows), ALU.mult, ALU.add)
                                V.tensor_scalar(dst, rs, gain, shift, ALU.mult, ALU.add).then_inc(*made("normed", (n, c)))
                                continue
                            link(V.scalar_tensor_tensor(dst, cen, gain, rs, ALU.mult, ALU.mult))
                            if st["add"]:
                                V.scalar_tensor_tensor(dst, dst, shift, B[st["add"]][c][:], ALU.add,
                                                       ALU.add).then_inc(*made("normed", (n, c)))
                            else:
                                V.tensor_scalar(dst, dst, shift, None, ALU.add).then_inc(*made("normed", (n, c)))

                    def mha(st):
                        n, nk, D = st["name"], st["nk"], st["D"]
                        J = per_block(st)
                        M = 64 if D == 16 else P
                        scale = float(D) ** -0.5
                        for c in C:
                            if D == 32:
                                for t in range(4):
                                    dve.wait_ge(*have("q_raw", (n, c, t)))
                                    V.tensor_scalar(q4[c][:, t, :], banks.where(("q_raw", n, c, t))[:, 0:TOK], scale, None,
                                                    ALU.mult).then_inc(*made("q", (n, c, t)))
                                continue
                            if st["rope"]:
                                for a in "qk":
                                    out = B[a][c][:].rearrange("p (s t) -> p s t", s=PER)
                                    other = part[c][:].rearrange("p (s t) -> p s t", s=PER)
                                    wide = [W(f"rope_{f}_{a}").unsqueeze(1).to_broadcast([P, PER, P]) for f in ("cos", "sin")]
                                    raw = [banks.where((a + f + "_raw", n, c))[:, 0:TOK].rearrange("p (s t) -> p s t", s=PER)
                                           for f in ("", "s")]
                                    dve.wait_ge(*have(a + "_raw", (n, c)))
                                    link(V.tensor_tensor(out, raw[0], wide[0], ALU.mult))
                                    dve.wait_ge(*have(a + "s_raw", (n, c)))
                                    V.tensor_tensor(other, raw[1], wide[1], ALU.mult).then_inc(*made(a + "s", (n, c)))
                                    dve.wait_ge(*have(a + "s", (n, c)))
                                    V.tensor_tensor(out, out, other, ALU.add).then_inc(*made(a, (n, c)))
                                    dve.wait_ge(*have(a, (n, c)))
                            else:
                                for a in "qk":
                                    N = PER * nk if a == "k" else TOK
                                    dve.wait_ge(*have(a + "_raw", (n, c)))
                                    raw = banks.where((a + "_raw", n, c))[0:M, 0:N]
                                    out = B[a][c][0:M, 0:N]
                                    if a == "q" and st["bias"]:
                                        V.tensor_scalar(out, raw, W(f"{n}_bq"), scale, ALU.add, ALU.mult).then_inc(*made(a, (n, c)))
                                    elif a == "q":
                                        V.tensor_scalar(out, raw, scale, None, ALU.mult).then_inc(*made(a, (n, c)))
                                    elif st["rel"]:
                                        V.tensor_scalar(out, raw, rel_col[:, 0:1], None, ALU.add).then_inc(*made(a, (n, c)))
                                    elif st["bias"]:
                                        V.tensor_scalar(out, raw, W(f"{n}_b{a}"), None, ALU.add).then_inc(*made(a, (n, c)))
                                    else:
                                        V.tensor_copy(out, raw).then_inc(*made(a, (n, c)))
                            dve.wait_ge(*have("k", (n, c)))
                            for j in range(1, J, 2):
                                out, keys, sel = masked_keys(st, c, j)
                                V.tensor_scalar(out, keys, sel, None, ALU.mult).then_inc(*made("k_masked_v", (n, c, j)))
                            if st["rel"]:
                                raw = banks.where(("k_raw", n, c))[:, 0:TOK].rearrange("p (s t) -> p s t", s=PER)
                                qv = B["q"][c][:].rearrange("p (s t) -> p s t", s=PER)
                                dve.wait_ge(*have("q", (n, c)))
                                link(V.scalar_tensor_tensor(near[c][:, :, 2 * P:3 * P], raw, rel_col[:, 2:3], qv, ALU.add, ALU.mult))
                                V.tensor_copy(near[c][:, :, 3 * P:3 * P + 1], near[c][:, :, 2 * P:2 * P + 1])
                                V.scalar_tensor_tensor(near[c][:, :, 3 * P + 1:4 * P], raw[:, :, 0:P - 1], rel_col[:, 1:2],
                                                       qv[:, :, 1:P], ALU.add, ALU.mult).then_inc(*made("near_prod", (n, c)))
                                dve.wait_ge(*have("vT_raw", (n, c)))
                                raw = banks.where(("vT_raw", n, c))[:, 0:TOK]
                                V.tensor_scalar(B["hn"][c][:], raw, rel_col[:, 4:5], None, ALU.add)
                                V.tensor_scalar(B["hn2"][c][:], raw, rel_col[:, 5:6], None, ALU.add).then_inc(*made("vT", (n, c)))
                            if st["linear"]:
                                raw = banks.where(("lin_raw", n, c))[:, 0:TOK].rearrange("p (s f) -> p s f", s=PER)
                                dve.wait_ge(*have("lin_raw", (n, c)))
                                top = lcol[c][:, 0:PER * 4].rearrange("p (s h) -> p s h", s=PER)
                                link(V.tensor_reduce(top, raw[:, :, 0:64].rearrange("p s (h d) -> p s h d", h=4), AX_X, ALU.max))
                                V.tensor_scalar(ke[c][:], raw[:, :, 64:P], 0.0, None, ALU.min)
                                V.tensor_scalar(kx[c][:], raw[:, :, 64:P], 0.0, None, ALU.max)
                                for s in S:
                                    ins = V.tensor_tensor(qe[c][:, s, :].rearrange("p (h d) -> p h d", h=4),
                                                          raw[:, s, 0:64].rearrange("p (h d) -> p h d", h=4),
                                                          top[:, s, :].unsqueeze(2).to_broadcast([P, 4, 16]), ALU.subtract)
                                ins.then_inc(*made("lin_shift", (n, c)))
                        if st["rel"]:
                            for c in C:
                                dve.wait_ge(*have("diag_raw", (n, c)))
                                V.tensor_copy(diag[c][:], banks.where(("diag_raw", n, c))[:, 0:PER * 32]
                                              .rearrange("p (s i) -> p s i", s=PER)).then_inc(*made("diag", (n, c)))
                        def global_softmax():
                            for c in C:
                                total = lcol[c][:, 4 * PER:8 * PER].rearrange("p (s h) -> p s h", s=PER)
                                inv = lcol[c][:, 8 * PER:12 * PER].rearrange("p (s h) -> p s h", s=PER)
                                dve.wait_ge(*have("lin_exp", (n, c)))
                                link(V.tensor_reduce(total, qe[c][:].rearrange("p s (h d) -> p s h d", h=4), AX_X, ALU.add))
                                link(V.reciprocal(inv, total))
                                for s in S:
                                    qv = qe[c][:, s, :].rearrange("p (h d) -> p h d", h=4)
                                    V.tensor_tensor(qv, qv, inv[:, s, :].unsqueeze(2).to_broadcast([P, 4, 16]), ALU.mult)
                                V.tensor_tensor(ke[c][:], ke[c][:], kx[c][:], ALU.add).then_inc(*made("lin_ready", (n, c)))

                        def global_heads():
                            for c in C:
                                dve.wait_ge(*have("lin_qT", (n, c)))
                                V.tensor_copy(qT[c][:], banks.where(("lin_qT", n, c))[0:64, 0:TOK]).then_inc(*made("lin_qTs", (n, c)))
                                raw = banks.where(("lin_sum", n, c))[0:64, 0:PER * 65].rearrange("p (s f) -> p s f", s=PER)
                                den = lcol[c][0:64, 12 * PER:13 * PER].rearrange("p (s a) -> p s a", a=1)
                                dve.wait_ge(*have("lin_sum", (n, c)))
                                link(V.tensor_scalar(den, raw[:, :, 64:65], 1e-6, None, ALU.add))
                                link(V.reciprocal(den, den))
                                link(V.tensor_tensor(lctx[c][:], raw[:, :, 0:64], den.to_broadcast([64, PER, 64]), ALU.mult))
                                V.tensor_tensor(lctx[c][:], lctx[c][:], W("lin_block", 64).unsqueeze(1)
                                                .to_broadcast([64, PER, 64]), ALU.mult).then_inc(*made("lin_ctx", (n, c)))

                        def row_max(t):
                            c, s = items[t]
                            m = rowmax[t % 2]
                            if t >= 2:
                                dve.wait_ge(*have("probs", (n, *items[t - 2], blocks(st)[-1])))
                            for r in blocks(st):
                                dve.wait_ge(*have("scores", (n, c, s, r)))
                                V.tensor_reduce(m[:, 4 * r:4 * r + J], banks.where(("scores", n, c, s, r))[:, 0:J * nk]
                                                .rearrange("p (j k) -> p j k", j=J), AX_X, ALU.max,
                                                negate=True).then_inc(*made("row_max", (n, c, s, r)))
                            if st["rel"]:
                                dve.wait_ge(*have("row_max", (n, c, s, blocks(st)[-1])))
                                for i in range(2):
                                    link(V.scalar_tensor_tensor(m[:], diag[c][:, s, i * 16:(i + 1) * 16], -1.0, m[:],
                                                                ALU.mult, ALU.min))
                                for i in range(2):
                                    ins = V.tensor_tensor(nearexp[t % 2][:, i, :], diag[c][:, s, i * 16:(i + 1) * 16], m[:],
                                                          ALU.add)
                                ins.then_inc(*made("near_shift", (n, c, s)))

                        def invert(t):
                            c, s = items[t]
                            total, inv, out = expsum[t % 2], inverse[t % 2], spread[t % 2]
                            dve.wait_ge(*have("probs", (n, c, s, blocks(st)[-1])))
                            if st["rel"]:
                                dve.wait_ge(*have("near_exp", (n, c, s)))
                                link(V.memset(nearexp[t % 2][0:1, 1, :], 0.0))
                                for i in range(2):
                                    link(V.tensor_tensor(total[:], total[:], nearexp[t % 2][:, i, :], ALU.add))
                            by_block = inv[:].rearrange("p (r j) -> p r j", r=4)
                            if D == 16:
                                link(V.reciprocal(by_block[:, 0:2, 0:2],
                                                  total[:].rearrange("p (r j) -> p r j", r=4)[:, 0:2, 0:2]))
                            else:
                                link(V.reciprocal(inv[:], total[:]))
                            if t >= 2:
                                dve.wait_ge(*have("wide_turned", (n, *items[t - 2])))
                            if D == 32:
                                ins = V.tensor_copy(out[:].rearrange("p j (r d) -> p j r d", r=4),
                                                    inv[:].rearrange("p (r j) -> p j r", r=4).unsqueeze(3)
                                                    .to_broadcast([P, 4, 4, 32]))
                            elif D == 16:
                                ins = V.tensor_copy(out[:, 0, 0:64].rearrange("p (r j d) -> p r j d", r=2, j=2),
                                                    by_block[:, 0:2, 0:2].unsqueeze(3).to_broadcast([P, 2, 2, 16]))
                            else:
                                for i, a in enumerate([inv[:]] + [nearexp[t % 2][:, i, :] for i in range(per_feature(st) - 1)]):
                                    ins = V.tensor_copy(out[:, i, :].rearrange("p (h d) -> p h d", h=HEADS),
                                                        a.unsqueeze(2).to_broadcast([P, HEADS, P // HEADS]))
                            ins.then_inc(*made("wide", (n, c, s)))

                        def untangle(t):
                            c, s = items[t]
                            for r in blocks(st):
                                if turned_by(st, r) != "turned_v":
                                    continue
                                dve.wait_ge(*have("turned", (n, c, s, r)))
                                if t >= 2:
                                    dve.wait_ge(*have("attended", (n, *items[t - 2])))
                                out = probsT[t % 2][0:nk, r, 0:J, :]
                                raw = banks.where(("turned", n, c, s, r))[0:nk, 0:J * P].rearrange("p (j t) -> p j t", j=J)
                                if st["post"]:
                                    ins = V.tensor_tensor(out, raw, after_mask[:].unsqueeze(1).to_broadcast([P, J, P]), ALU.mult)
                                else:
                                    ins = V.tensor_copy(out, raw)
                                ins.then_inc(*made("turned_v", (n, c, s, r)))

                        def context(t):
                            c, s = items[t]
                            b = banks.where(("attended", n, c, s))
                            by = spreadT[t % 2]
                            dve.wait_ge(*have("attended", (n, c, s)))
                            dve.wait_ge(*have("wide_taken", (n, c, s)))
                            if st["rel"]:
                                v_own, v_before = cols(B["hn2"][c], s), cols(B["hn"][c], s)
                                t1, t2 = near[c][:, s, 0:P], near[c][:, s, P:2 * P]
                                V.tensor_tensor(t1, by[:, 1, :], v_own, ALU.mult)
                                link(V.tensor_tensor(t2[:, 1:P], by[:, 2, 1:P], v_before[:, 0:P - 1], ALU.mult))
                                link(V.tensor_tensor(t1[:, 1:P], t1[:, 1:P], t2[:, 1:P], ALU.add))
                                link(V.tensor_tensor(t1, t1, b[:, 0:P], ALU.add))
                                ins = V.tensor_tensor(cols(B["o"][c], s), t1, by[:, 0, :], ALU.mult)
                            elif D == 32:
                                ins = V.tensor_tensor(q4[c][:, :, s * P:(s + 1) * P], b[:].rearrange("p (t n) -> p t n", t=4),
                                                      by[:], ALU.mult)
                            elif st["linear"]:
                                o = B["oL1"][c]
                                V.tensor_copy(o[64:P, s * P + 64:(s + 1) * P], b[64:P, 64:P])
                                ins = V.tensor_tensor(cols(o, s)[0:64], b[0:64, 0:P], by[0:64, 0, :], ALU.mult)
                            else:
                                ins = V.tensor_tensor(cols(B["o"][c], s), b[:, 0:P], by[:, 0, :], ALU.mult)
                            ins.then_inc(*made("context", (n, c, s)))

                        def add_residual(c):
                            b = banks.where(("proj", n, c))[:, 0:TOK]
                            dve.wait_ge(*have("proj", (n, c)))
                            if st["bo"]:
                                V.scalar_tensor_tensor(B[st["dst"]][c][:], b, W(st["bo"]), B[st["res"]][c][:], ALU.add,
                                                       ALU.add).then_inc(*made("residual", (n, c)))
                            else:
                                V.tensor_tensor(B[st["dst"]][c][:], b, B[st["res"]][c][:], ALU.add
                                                ).then_inc(*made("residual", (n, c)))

                        for t in range(GROUP + 2):
                            if t < GROUP:
                                row_max(t)
                            if st["linear"] and t in (0, 2):
                                global_heads() if t else global_softmax()
                            if 1 <= t <= GROUP:
                                invert(t - 1)
                            if t >= 2:
                                context(t - 2)
                            if 1 <= t <= GROUP:
                                untangle(t - 1)
                            for c in C:
                                if t == output_step(c):
                                    add_residual(c)

                    def xattn(st):
                        n = st["name"]
                        for c in C:
                            for a, N in (("q", TOK), ("k", CTOK)):
                                dve.wait_ge(*have(a + "_raw", (n, c)))
                                V.tensor_scalar(B[a][c][:, 0:N], banks.where((a + "_raw", n, c))[:, 0:N], W(f"{n}_b{a}"), None,
                                                ALU.add).then_inc(*made(a, (n, c)))
                        for c in C:
                            dve.wait_ge(*have("xscores", (n, c)))
                            V.tensor_reduce(xcol[c][:, 0, :], banks.where(("xscores", n, c))[:, 0:CTOK]
                                            .rearrange("p (s k) -> p s k", s=PER), AX_X, ALU.max, negate=True
                                            ).then_inc(*made("xmax", (n, c)))
                        for c in C:
                            dve.wait_ge(*have("xexp", (n, c)))
                            link(V.tensor_reduce(xcol[c][:, 1, :], px[c], AX_X, ALU.add))
                            link(V.reciprocal(xcol[c][:, 2, :], xcol[c][:, 1, :]))
                            V.tensor_tensor(px[c], px[c], xcol[c][:, 2, :].unsqueeze(2).to_broadcast([P, PER, CTX_LEN]), ALU.mult
                                            ).then_inc(*made("xprobs", (n, c)))
                        for c in C:
                            dve.wait_ge(*have("xout", (n, c)))
                            V.tensor_tensor(B["u"][c][:], banks.where(("xout", n, c))[:, 0:TOK], B["x"][c][:], ALU.add
                                            ).then_inc(*made("residual", (n, c)))

                    def mlp(st):
                        n = st["name"]
                        for c in C:
                            b = banks.where(("proj", n, c))[:, 0:TOK]
                            dst = B[st["dst"]][c][:]
                            dve.wait_ge(*have("proj", (n, c)))
                            if not st["adds"]:
                                V.scalar_tensor_tensor(dst, b, W(st["b2"]), B[st["res"]][c][:], ALU.add, ALU.add
                                                       ).then_inc(*made("residual", (n, c)))
                                continue
                            V.scalar_tensor_tensor(part[c][:], b, W(st["b2"]), B[st["res"]][c][:], ALU.add, ALU.add
                                                   ).then_inc(*made("acc_taken", (n, c)))
                            dve.wait_ge(*have("acc_taken", (n, c)))
                            if len(st["adds"]) == 2:
                                link(V.tensor_tensor(part[c][:], part[c][:], B[st["adds"][1]][c][:], ALU.add))
                            V.tensor_tensor(dst, part[c][:], B[st["adds"][0]][c][:], ALU.add).then_inc(*made("residual", (n, c)))

                    def moe(st):
                        n, base = st["name"], "L3_ffn" if st["name"] == "L3_ffn_moe" else st["name"]
                        wide = [P, PER, EXPERTS]
                        desc = W("descending").unsqueeze(1).to_broadcast(wide)

                        def bc(col):
                            return col.unsqueeze(2).to_broadcast(wide)
                        for c in C:
                            T = [gtmp[c][:, i] for i in range(8)]
                            k = [gcol[c][:, i] for i in range(8)]
                            raw = banks.where(("logits", n, c))[:, 0:PER * EXPERTS].rearrange("p (s e) -> p s e", s=PER)
                            dve.wait_ge(*have("logits", (n, c)))
                            if st["on"] == "probs":
                                link(V.tensor_reduce(k[6], raw, AX_X, ALU.max))
                                V.tensor_tensor(T[0], raw, bc(k[6]), ALU.subtract).then_inc(*made("logits_in", (n, c)))
                            else:
                                V.tensor_copy(T[0], raw).then_inc(*made("logits_in", (n, c)))
                                dve.wait_ge(*have("logits_in", (n, c)))
                        for c in C:
                            T = [gtmp[c][:, i] for i in range(8)]
                            k = [gcol[c][:, i] for i in range(8)]
                            if st["on"] == "probs":
                                dve.wait_ge(*have("router_exp", (n, c)))
                                link(V.tensor_reduce(k[6], T[0], AX_X, ALU.add))
                                link(V.reciprocal(k[7], k[6]))
                                link(V.tensor_tensor(T[0], T[0], bc(k[7]), ALU.mult))
                            v = T[0]
                            for i in range(2):
                                link(V.tensor_reduce(k[2 * i], v, AX_X, ALU.max))
                                link(V.tensor_tensor(T[2], v, bc(k[2 * i]), ALU.is_ge))
                                link(V.tensor_tensor(T[2], T[2], desc, ALU.mult))
                                link(V.tensor_reduce(k[2 * i + 1], T[2], AX_X, ALU.max))
                                link(V.tensor_tensor(T[3 + i], T[2], bc(k[2 * i + 1]), ALU.is_equal))
                                if i == 0:
                                    link(V.scalar_tensor_tensor(T[5], T[3], MASKED, T[0], ALU.mult, ALU.add))
                                    v = T[5]
                            V.tensor_tensor(k[6], k[0], k[2], ALU.subtract).then_inc(*made("gate_gap", (n, c)))
                        for c in C:
                            T = [gtmp[c][:, i] for i in range(8)]
                            k = [gcol[c][:, i] for i in range(8)]
                            dve.wait_ge(*have("gate_tanh", (n, c)))
                            V.tensor_scalar(k[4], k[6], 0.5, 0.5, ALU.mult, ALU.add)
                            link(V.tensor_scalar(k[5], k[6], -0.5, 0.5, ALU.mult, ALU.add))
                            V.tensor_tensor(T[6], T[3], bc(k[4]), ALU.mult)
                            link(V.tensor_tensor(T[7], T[4], bc(k[5]), ALU.mult))
                            V.tensor_tensor(gate[c][:], T[6], T[7], ALU.add).then_inc(*made("gate", (n, c)))
                        E = EXPERTS + st["shared"]
                        work_items = [(e, c) for e in range(E) for c in C]

                        def gated(e, c):
                            for m in range(2):
                                b = banks.where(("hid_raw", n, e, c, m))[:, 0:TOK]
                                dve.wait_ge(*have("silu", (n, e, c, m)))
                                dve.wait_ge(*have("hid_raw", (n, e, c, m)))
                                V.scalar_tensor_tensor(hid[c][:, m, :], b, W(base + "_b0")[:, 2 * e + m:2 * e + m + 1],
                                                       silu[c][m][:], ALU.add, ALU.mult).then_inc(*made("gated", (n, e, c, m)))

                        def combine(e, c):
                            b = banks.where(("expert", n, e, c))[:, 0:TOK]
                            bias = W(base + "_b2")[:, e:e + 1]
                            u, src = B["u"][c][:], B[st["src"]][c][:]
                            dve.wait_ge(*have("expert", (n, e, c)))
                            if st["shared"] and e == 0:
                                V.scalar_tensor_tensor(u, b, bias, src, ALU.add, ALU.add).then_inc(*made("expert_taken", (n, e, c)))
                                return
                            dve.wait_ge(*have("gate_copy", (n, e, c)))
                            V.scalar_tensor_tensor(part[c][:], b, bias, gb[c][:], ALU.add, ALU.mult
                                                   ).then_inc(*made("expert_taken", (n, e, c)))
                            dve.wait_ge(*have("expert_taken", (n, e, c)))
                            if e == E - 1:
                                V.tensor_tensor(u, u, part[c][:], ALU.add).then_inc(*made("residual", (n, c)))
                            else:
                                link(V.tensor_tensor(u, src if e == 0 else u, part[c][:], ALU.add))

                        for i in range(len(work_items) + 1):
                            if i < len(work_items) and st["glu"]:
                                gated(*work_items[i])
                            if i:
                                combine(*work_items[i - 1])

                    def linear(st):
                        for c in C:
                            dve.wait_ge(*have("proj", (st["name"], c)))
                            V.tensor_tensor(B["u"][c][:], banks.where(("proj", st["name"], c))[:, 0:TOK], B["x"][c][:], ALU.add
                                            ).then_inc(*made("residual", (st["name"], c)))

                    todo = dict(norm=norm, mha=mha, xattn=xattn, mlp=mlp, moe=moe, linear=linear)
                    for st in seq:
                        todo[st["kind"]](st)

                @block.gpsimd
                def _(pool):
                    def mha(st):
                        n = st["name"]
                        if st["wipes"]:
                            for c in C:
                                pool.wait_ge(*have("attended", (n, c, PER - 1)))
                                nc.gpsimd.memset(vm[c][:], 0.0).then_inc(*made("values_zeroed", (n, c)))

                    for st in seq:
                        if st["kind"] == "mha":
                            mha(st)

                @block.sync
                def _(sp):
                    for c in C:
                        sp.dma_start(B["x"][c][:], io["x"][:, bass.ds(g * (GROUP * P) + c * TOK, TOK)]
                                     ).then_inc(*made(f"x_loaded{c}", ("", c), 16))
                        sp.dma_start(B["ctx"][c][:], io["ctx"][:, bass.ds(g * (GROUP * CTX_LEN) + c * CTOK, CTOK)]
                                     ).then_inc(*made(f"ctx_loaded{c}", ("", c), 16))
                    names = [st["name"] for st in seq]
                    at = 0
                    for i, p in enumerate(stream):
                        n = columns(p["entries"])[1]
                        if p["user"] in names:
                            if i >= SLOTS:
                                label, key, tail = stream[i - SLOTS]["freed"]
                                for c in C:
                                    sp.wait_ge(*have(label, (*key, c, *tail)))
                            sp.dma_start(slots[p["slot"]][:, 0:n], io["w_stream"][:, at:at + n]
                                         ).then_inc(*made(f"weights{p['slot']}", p["name"], 16))
                        at += n
                    for c in C:
                        sp.wait_ge(*have(end[0], (end[1], c)))
                        sp.dma_start(io["out"][:, bass.ds(g * (GROUP * P) + c * TOK, TOK)], B["x"][c][:]
                                     ).then_inc(*made("stored", c, 16))
                    sp.wait_ge(*have("stored", CHAINS - 1))

            nums = sorted(s.num for s in ev.sems.values())
            if known:
                assert nums == list(range(nums[0], nums[0] + len(nums)))
                nc.all_engine_barrier(sems_to_clear=range(nums[0], nums[-1] + 1))
        return ev


def pack(entries, parts):
    import numpy as np
    at, n = columns(entries)
    out = np.zeros((P, n), np.float32)
    for name, (o, w) in at.items():
        a = parts[name]
        assert a.shape[1] == w, (name, a.shape, w)
        out[:a.shape[0], o:o + w] = a
    return out


def lay_out(i):
    import numpy as np
    p = {}

    def col(v):
        return v.reshape(-1, P).T

    def col64(v):
        return v.reshape(CTX_DIM, 1)

    def deep(w):
        return w.reshape(-1, P, w.shape[-1]).transpose(1, 0, 2).reshape(P, -1)

    swap = np.arange(P) ^ 1
    for n in "qkvo":
        p["L0_attn_W" + n] = i["L0_attn_W" + n]
        p["L2_attn_W" + n] = i["L2_attn_W" + n]
        p["L3_attn_W" + n] = i["L3_attn_W_" + n]
        p["L3_ffn_W" + n] = i["L3_ffn_W" + n]
        p["L2_attn_b" + n] = col(i["L2_attn_b" + n])
        p["L3_attn_b" + n] = col(i["L3_attn_b_" + n])
    p["L0_attn_Wqs"], p["L0_attn_Wks"] = i["L0_attn_Wq"][:, swap], i["L0_attn_Wk"][:, swap]
    p["L2_attn_bv_row"], p["L3_attn_bv_row"] = i["L2_attn_bv"][None], i["L3_attn_b_v"][None]
    for lv in ("L0", "L3"):
        a = lv + "_xattn_"
        for n in "qkv":
            p[a + "W" + n] = i[a + "W" + n]
        p[a + "bq"], p[a + "bk"], p[a + "bv_row"] = col(i[a + "bq"]), col(i[a + "bk"]), i[a + "bv"][None]
    p["L0_ffn_Wr"] = i["L0_ffn_Wr"]
    p["L0_ffn_b1"] = np.concatenate([col(i["L0_ffn_bfc_s"])] + [col(b) for b in i["L0_ffn_bfc"]], 1)
    p["L0_ffn_b2"] = np.concatenate([col(i["L0_ffn_bproj_s"])] + [col(b) for b in i["L0_ffn_bproj"]], 1)
    for e in range(EXPERTS + 1):
        p[f"L0_ffn_W1_{e}"] = i["L0_ffn_Wfc"][e - 1] if e else i["L0_ffn_Wfc_s"]
        p[f"L0_ffn_W2_{e}"] = deep(i["L0_ffn_Wproj"][e - 1] if e else i["L0_ffn_Wproj_s"])
    for d in range(DEPTH):
        n = f"L1_{d}_"
        for k in ("bo", "ln1_g", "ln1_b", "ln2_g", "ln2_b", "b1", "b2"):
            p[n + k] = col(i["L1_attn_" + k][d])
        wq, wk = i["L1_attn_Wq"][d], i["L1_attn_Wk"][d]
        p[n + "Wq"], p[n + "Wk"] = wq[:, :64], wk[:, :64]
        p[n + "Wlin"] = np.concatenate([wq[:, 64:], wk[:, 64:]], 1)
        p[n + "Wv"], p[n + "Wo"] = i["L1_attn_Wv"][d], i["L1_attn_Wo"][d]
        p[n + "W1"], p[n + "W2"] = i["L1_attn_W1"][d], deep(i["L1_attn_W2"][d])
    p["L1_xattn_Wq"], p["L1_xattn_Wo"] = i["L1_xattn_Wq"].T, i["L1_xattn_Wo"].T
    p["L1_xattn_Wk"], p["L1_xattn_Wv"] = i["L1_xattn_Wkv"][:P].T, i["L1_xattn_Wkv"][P:].T
    p["L1_ffn_Wr"], p["L1_ffn_br_row"] = i["L1_ffn_gate_w"].T, i["L1_ffn_gate_b"][None]
    for k in ("b0", "b1", "b2"):
        p["L1_ffn_" + k] = np.concatenate([col(b) for b in i["L1_ffn_" + k]], 1)
    for e in range(EXPERTS):
        p[f"L1_ffn_w0_{e}"], p[f"L1_ffn_w1_{e}"] = i["L1_ffn_w0"][e].T, i["L1_ffn_w1"][e].T
        p[f"L1_ffn_w2_{e}"] = deep(i["L1_ffn_w2"][e].T)
    for k in ("ln1_g", "ln1_b", "ln2_g", "ln2_b"):
        p["L2_" + k] = col(i["L2_xattn_" + k])
        p["L3_ffn_" + k] = col(i["L3_ffn_" + k])
    for a, src in (("L2_a1_", "L2_xattn_a1_"), ("L2_a2_", "L2_xattn_a2_")):
        for k in ("lnx_g", "lnx_b", "lny_g", "lny_b", "ln3_g", "ln3_b", "li1_b", "li2_b", "li3_b"):
            v = i[src + k]
            p[a + k] = col64(v) if v.shape[0] == CTX_DIM else col(v)
        for k in ("wq", "wk", "wv"):
            w = i[src + k]
            p[a + k] = w.transpose(1, 0, 2).reshape(w.shape[1], -1)
        p[a + "li1"], p[a + "li2"], p[a + "li3"] = deep(i[src + "li1_w"]), i[src + "li2_w"], deep(i[src + "li3_w"])
    p["L2_ffn_W"] = i["L2_ffn_weight"].T
    p["L3_rel_k"] = np.tile(i["L3_attn_rel_k_table"][:3].T, (HEADS, 1))
    p["L3_rel_v"] = np.tile(i["L3_attn_rel_v_table"][:3].T, (HEADS, 1))
    p["L3_rel_v_row"] = np.tile(i["L3_attn_rel_v_table"][0], HEADS)[None]
    p["L3_ffn_bo"], p["L3_ffn_Wr"] = col(i["L3_ffn_bo"]), i["L3_ffn_Wr"]
    p["L3_ffn_b1"] = np.concatenate([col(b) for b in i["L3_ffn_be1"]], 1)
    p["L3_ffn_b2"] = np.concatenate([col(b) for b in i["L3_ffn_be2"]], 1)
    for e in range(EXPERTS):
        p[f"L3_ffn_W1_{e}"], p[f"L3_ffn_W2_{e}"] = i["L3_ffn_We1"][e], deep(i["L3_ffn_We2"][e])
    return p


def shape_constants():
    import numpy as np
    D = P // HEADS
    f = np.arange(P)
    inv = (1.0 / np.float32(10000.0) ** (np.arange(0, D, 2, dtype=np.float32) / np.float32(D))).astype(np.float32)
    theta = inv[(f % D) // 2][:, None] * np.arange(P, dtype=np.float32)[None]
    sign = np.where(f % 2 == 0, -1.0, 1.0)[:, None]
    scale = float(D) ** -0.5
    k = {"rope_cos_k": np.cos(theta), "rope_sin_k": np.sin(theta) * sign}
    k |= {"rope_cos_q": k["rope_cos_k"] * scale, "rope_sin_q": k["rope_sin_k"] * scale}
    k["head_pick"] = (f[:, None] // D == np.arange(HEADS)[None])
    k["mask8"] = (f[:, None] // 8) % 4 == np.arange(4)[None]
    k["mask16"] = (f[:, None] // 16) % 2 == np.arange(2)[None]
    g = np.arange(64)
    k["lin_block"] = (g[:, None] // 16 == g[None] // 16)
    k["descending"] = np.tile(np.arange(EXPERTS, 0, -1)[None], (P, 1))
    return k


def kernel(**inputs):
    import numpy as np
    import concourse.bacc as bacc
    from concourse.bass_utils import run_bass_kernel_spmd

    i = {k: np.asarray(v) for k, v in inputs.items()}
    parts = lay_out(i) | shape_constants()
    arrays = {
        "x": np.ascontiguousarray(i["x"].transpose(2, 0, 1).reshape(P, BATCH * P)),
        "ctx": np.ascontiguousarray(i["ctx_512"].transpose(2, 0, 1).reshape(CTX_DIM, BATCH * CTX_LEN)),
        "w_small": pack(small_entries(), parts),
    }
    arrays["w_stream"] = pack([x for p in pieces() for x in p["entries"]], parts)

    def program(known):
        nc = bacc.Bacc("TRN2", target_bir_lowering=False, num_devices=1)
        io = {n: nc.dram_tensor("in_" + n, a.shape, F32, kind="ExternalInput").ap() for n, a in arrays.items()}
        io["out"] = nc.dram_tensor("out", (P, BATCH * P), F32, kind="ExternalOutput").ap()
        return nc, decoder(nc, io, known)

    _, counted = program({})
    nc, final = program(counted.seen)
    assert final.seen == counted.seen
    got = run_bass_kernel_spmd(nc, [{"in_" + n: a for n, a in arrays.items()}], core_ids=[0]).results[0]["out"]
    return np.ascontiguousarray(got.reshape(P, BATCH, P).transpose(1, 2, 0))
```
